# Optimizing a Trainium2 kernel written in Bass

```python
import numpy as np
import jax
import jax.numpy as jnp

def _softmax(x, axis=-1):
    return jax.nn.softmax(x, axis=axis)

def _gelu(x):
    return jax.nn.gelu(x, approximate=True)

def _silu(x):
    return jax.nn.silu(x)

def _sigmoid(x):
    return jax.nn.sigmoid(x)

def _layernorm(x, axis=-1, eps=1e-05):
    m = jnp.mean(x, axis=axis, keepdims=True)
    v = jnp.var(x, axis=axis, keepdims=True)
    return (x - m) / jnp.sqrt(v + eps)

def _scatter_add(tgt, idx, src, axis=0):
    return tgt.at[idx].add(src)

def _segment_sum(src, seg, n):
    return jax.ops.segment_sum(src, seg, n)
kernel_name = 'mk_seq_preln_d1_jaxref_r8_572a75'

def setup_inputs(seed: int=0):
    np.random.seed(seed)
    _w = jnp.asarray

    def _L0_attn_setup():
        import jax, jax.numpy as jnp
        import numpy as np
        D_MODEL = 128
        H = 8
        S = 128
        HD = 128
        LV = 12
        B = 2
        T = 256

        def _level_structure(t, num_levels):
            idx = np.arange(t)
            d = idx[:, None] - idx[None, :]
            lvl = np.where(d <= 0, 0, np.floor(np.log2(np.maximum(d, 1))).astype(np.int64) + 1)
            lvl = np.minimum(lvl, num_levels - 1)
            mask = d >= 0
            return (jnp.asarray(lvl), jnp.asarray(mask))
        key = jax.random.key(seed)
        ks = jax.random.split(key, 8)
        sd = 1.0 / np.sqrt(D_MODEL)
        return {'x': jax.random.normal(ks[0], (B, T, D_MODEL), jnp.float32), 'Wq': jax.random.normal(ks[1], (H * S, D_MODEL), jnp.float32) * sd, 'Wk': jax.random.normal(ks[2], (H * S, D_MODEL), jnp.float32) * sd, 'Wv': jax.random.normal(ks[3], (H * HD, D_MODEL), jnp.float32) * sd, 'Wg': jax.random.normal(ks[4], (H, D_MODEL), jnp.float32) * sd, 'bg': jnp.zeros((H,), jnp.float32), 'Wdl': jax.random.normal(ks[5], (H * LV, D_MODEL), jnp.float32) * sd, 'Lparam': jnp.ones((H, LV), jnp.float32), 'Wo': jax.random.normal(ks[6], (D_MODEL, H * HD), jnp.float32) / np.sqrt(H * HD), 'ln_g': jnp.ones((D_MODEL,), jnp.float32), 'ln_b': jnp.zeros((D_MODEL,), jnp.float32)}
    _L0_attn_in = _L0_attn_setup()

    def _L0_ffn_setup():
        import jax, jax.numpy as jnp
        import numpy as np
        IN_DIM = 128
        OUT_DIM = 128
        NUM_EXPERTS = 8
        TOP_K = 2
        key = jax.random.key(seed)
        ks = jax.random.split(key, 5)
        s = 1.0 / np.sqrt(IN_DIM)
        x = jax.random.normal(ks[0], (4, 256, IN_DIM), dtype=jnp.float32)
        Wg = jax.random.uniform(ks[1], (IN_DIM, NUM_EXPERTS), jnp.float32, -s, s)
        bg = jnp.zeros((NUM_EXPERTS,), jnp.float32)
        We = jax.random.uniform(ks[2], (NUM_EXPERTS, OUT_DIM, IN_DIM), jnp.float32, -s, s)
        be = jax.random.uniform(ks[3], (NUM_EXPERTS, OUT_DIM), jnp.float32, -s, s)
        return {'x': x, 'Wg': Wg, 'bg': bg, 'We': We, 'be': be}
    _L0_ffn_in = _L0_ffn_setup()
    _d = {'L0_attn_x': _L0_attn_in['x'], 'L0_attn_Wq': _L0_attn_in['Wq'], 'L0_attn_Wk': _L0_attn_in['Wk'], 'L0_attn_Wv': _L0_attn_in['Wv'], 'L0_attn_Wg': _L0_attn_in['Wg'], 'L0_attn_bg': _L0_attn_in['bg'], 'L0_attn_Wdl': _L0_attn_in['Wdl'], 'L0_attn_Lparam': _L0_attn_in['Lparam'], 'L0_attn_Wo': _L0_attn_in['Wo'], 'L0_attn_ln_g': _L0_attn_in['ln_g'], 'L0_attn_ln_b': _L0_attn_in['ln_b'], 'L0_ffn_Wg': _L0_ffn_in['Wg'], 'L0_ffn_bg': _L0_ffn_in['bg'], 'L0_ffn_We': _L0_ffn_in['We'], 'L0_ffn_be': _L0_ffn_in['be']}
    _x0 = _d['L0_attn_x']
    _d['L0_attn_x'] = jax.random.normal(jax.random.fold_in(jax.random.key(seed), 1), (8, 1024, 128), dtype=_x0.dtype)
    del _x0
    return _d

def reference(L0_attn_x, L0_attn_Wq, L0_attn_Wk, L0_attn_Wv, L0_attn_Wg, L0_attn_bg, L0_attn_Wdl, L0_attn_Lparam, L0_attn_Wo, L0_attn_ln_g, L0_attn_ln_b, L0_ffn_Wg, L0_ffn_bg, L0_ffn_We, L0_ffn_be):

    def _L0_attn_ref(x, Wq, Wk, Wv, Wg, bg, Wdl, Lparam, Wo, ln_g, ln_b):
        import jax, jax.numpy as jnp
        import numpy as np
        D_MODEL = 128
        H = 8
        S = 128
        HD = 128
        LV = 12
        B = 2
        T = 256

        def _level_structure(t, num_levels):
            idx = np.arange(t)
            d = idx[:, None] - idx[None, :]
            lvl = np.where(d <= 0, 0, np.floor(np.log2(np.maximum(d, 1))).astype(np.int64) + 1)
            lvl = np.minimum(lvl, num_levels - 1)
            mask = d >= 0
            return (jnp.asarray(lvl), jnp.asarray(mask))
        b, t, _ = x.shape
        q = (x @ Wq.T).reshape(b, t, H, S)
        k = (x @ Wk.T).reshape(b, t, H, S)
        v = (x @ Wv.T).reshape(b, t, H, HD)
        g = -jax.nn.softplus(x @ Wg.T + bg)
        dl = (x @ Wdl.T).reshape(b, t, H, LV)
        lam = jax.nn.softplus(dl + Lparam[None, None])
        G = jnp.cumsum(g, axis=1)
        lvl, mask = _level_structure(t, LV)
        scale = 1.0 / np.sqrt(S)
        scores = jnp.einsum('bthd,bshd->bhts', q, k) * scale
        Gh = G.transpose(0, 2, 1)
        logdecay = Gh[:, :, :, None] - Gh[:, :, None, :]
        logdecay = jnp.where(mask[None, None], logdecay, -jnp.inf)
        decay = jnp.exp(logdecay)
        lvl_oh = jax.nn.one_hot(lvl, LV, dtype=x.dtype)
        lamw = jnp.einsum('bthl,tsl->bhts', lam, lvl_oh)
        A = scores * decay * lamw
        y = jnp.einsum('bhts,bshd->bthd', A, v).reshape(b, t, H * HD)
        out = y @ Wo.T + x
        mu = out.mean(-1, keepdims=True)
        var = out.var(-1, keepdims=True)
        return (out - mu) * jax.lax.rsqrt(var + 1e-05) * ln_g + ln_b

    def _L0_ffn_ref(x, Wg, bg, We, be):
        import jax, jax.numpy as jnp
        import numpy as np
        IN_DIM = 128
        OUT_DIM = 128
        NUM_EXPERTS = 8
        TOP_K = 2
        gate = jax.nn.softmax(x @ Wg + bg, axis=-1)
        topk_vals, topk_idx = jax.lax.top_k(gate, TOP_K)
        onehot = jax.nn.one_hot(topk_idx, NUM_EXPERTS, dtype=gate.dtype)
        gate_sparse = jnp.einsum('bsk,bske->bse', topk_vals, onehot)
        gate_sparse = gate_sparse / jnp.sum(gate_sparse, axis=-1, keepdims=True)
        y = jnp.einsum('bsi,eoi->bseo', x, We) + be[None, None, :, :].transpose(0, 1, 2, 3)
        out = jnp.einsum('bseo,bse->bso', y, gate_sparse)
        return out
    x = L0_attn_x
    x = x + _L0_attn_ref(_layernorm(x, axis=-1), L0_attn_Wq, L0_attn_Wk, L0_attn_Wv, L0_attn_Wg, L0_attn_bg, L0_attn_Wdl, L0_attn_Lparam, L0_attn_Wo, L0_attn_ln_g, L0_attn_ln_b)
    x = x + _L0_ffn_ref(_layernorm(x, axis=-1), L0_ffn_Wg, L0_ffn_bg, L0_ffn_We, L0_ffn_be)
    return x

_drawn_inputs = setup_inputs


def setup_inputs(seed=0):
    import zlib

    import numpy as np

    out = dict(_drawn_inputs(seed))
    spreads = {'L0_attn_bg': (0.0, 0.345),
     'L0_attn_Lparam': (1.0, 0.2),
     'L0_attn_ln_g': (1.0, 0.2),
     'L0_attn_ln_b': (0.0, 0.1),
     'L0_ffn_bg': (0.0, 0.1)}
    factors = {'L0_ffn_be': 2.931}
    for name, (base, spread) in spreads.items():
        noise = np.random.default_rng([zlib.crc32(name.encode()), seed]).standard_normal(out[name].shape)
        drawn = base * np.exp(spread * noise) if base else spread * noise
        out[name] = jnp.asarray(drawn.astype(out[name].dtype))
    for name, factor in factors.items():
        out[name] = (out[name] * factor).astype(out[name].dtype)
    return out
```

```python
from contextlib import ExitStack

import numpy as np

import concourse.bass as bass
from concourse import mybir

P = 128
B, T, D = 8, 1024, 128
H = 8
LV = 12
E = 8
NC = T // P
NH = B * H
NLV = 11
LOW = 8
HIGH = NLV - LOW
TA = P // (2 * LOW)
NTA = P // TA
TB = 16
NTB = P // TB
KB = 2 * HIGH * TB
HF = P // 2
NLOG = LV * H + H
SCALE = 1.0 / np.sqrt(np.float32(P))
EPS = 1e-5

F32 = mybir.dt.float32
F32R = mybir.dt.float32r
ALU = mybir.AluOpType
ACT = mybir.ActivationFunctionType
AX = mybir.AxisListType.X

W_AT = [sum(NC - k for k in range(j)) for j in range(NC)]
NT = sum(NC - j for j in range(NC))
BIAS_AT = [sum(NC - k for k in range(d)) for d in range(NC)]
GROUPS = []
for _j in range(NC):
    for _lo in (0, T // 2):
        _a = max(_j * P, _lo)
        if _a < _lo + T // 2:
            GROUPS.append((_j, _a, _lo + T // 2))
NG = len(GROUPS)
UNITS = [[(0, 0, 8)], [(1, 1, 7)], [(2, 2, 6)], [(3, 3, 5), (5, 5, 3)], [(4, 4, 4)]]
NU = len(UNITS)
CONST = {}
_at = 0
for _name, _n in (("ma0", NTA * P), ("ma1", NTA * P), ("mb1", NTB * P), ("mb2", NTB * P), ("mb4", NTB * P),
                  ("m9", P), ("m10", P), ("neg", P), ("ident", P), ("tri", P), ("suf", P), ("dma", TA), ("dmb", TB),
                  ("first", E)):
    CONST[_name] = (_at, _at + _n)
    _at += _n
NCONST = _at
NMASK = CONST["neg"][0]


def constants():
    def level(d):
        return np.where(d <= 0, 0, np.floor(np.log2(np.maximum(d, 1))).astype(np.int64) + 1)

    out = np.zeros((P, NCONST), np.float32)
    row = np.arange(P)
    s = np.arange(P)[None, None, :]

    def put(name, a):
        lo, hi = CONST[name]
        a = a.reshape(a.shape[0], -1)
        out[:a.shape[0], lo:hi] = a

    l_a, q_a = (row // TA % LOW)[:, None, None], (row % TA)[:, None, None]
    t_a = np.arange(NTA)[None, :, None] * TA + q_a
    put("ma0", (s <= t_a) & (level(t_a - s) == l_a))
    put("ma1", (s > t_a) & (level(P + t_a - s) == l_a))
    rb = np.arange(KB)
    l_b, q_b = (rb // TB % HIGH + LOW)[:, None, None], (rb % TB)[:, None, None]
    t_b = np.arange(NTB)[None, :, None] * TB + q_b
    for d in (1, 2, 4):
        put(f"mb{d}", level(d * P + t_b - s) == l_b)
    put("m9", np.broadcast_to(l_b[:, 0] == 9, (KB, P)))
    put("m10", np.broadcast_to(l_b[:, 0] == 10, (KB, P)))
    put("neg", row[None, :] > row[:, None])
    put("ident", row[None, :] == row[:, None])
    put("tri", row[:, None] <= row[None, :])
    put("suf", row[:, None] > row[None, :])
    put("dma", (row % TA)[:, None] == np.arange(TA)[None, :])
    put("dmb", (rb % TB)[:, None] == np.arange(TB)[None, :])
    out[:, CONST["first"][0]:CONST["first"][1]] = E - np.arange(E)
    return out


def program(nc, x, Wq, Wk, Wv, Wg, bg, Wdl, Lparam, Wo, ln_g, ln_b, fWg, fbg, fWe, fbe, table, out):
    mn_dram = nc.dram_tensor("mn_scratch", [H, P, 4, P], F32, kind="Internal").ap()
    xt_dram = nc.dram_tensor("xt_scratch", [B, 2, P, T], F32, kind="Internal").ap()
    ea_dram = nc.dram_tensor("ea_scratch", [NH, P, P], F32, kind="Internal").ap()
    eb_dram = nc.dram_tensor("eb_scratch", [NH, KB, NC * NTB], F32, kind="Internal").ap()
    bias_dram = nc.dram_tensor("bias_scratch", [NH, P, NT], F32, kind="Internal").ap()
    yt_dram = nc.dram_tensor("yt_scratch", [B, P, T], F32, kind="Internal").ap()

    with ExitStack() as outer:
        cst = outer.enter_context(nc.sbuf_tensor("cst", [P, NCONST - NMASK], F32))
        mask = outer.enter_context(nc.sbuf_tensor("mask", [P, NMASK], F32R))
        negm = outer.enter_context(nc.sbuf_tensor("negm", [P, P], F32R))
        identr = outer.enter_context(nc.sbuf_tensor("identr", [P, P], F32R))
        rows = outer.enter_context(nc.sbuf_tensor("rows", [P, NLOG + 2 * P + E], F32))
        wet_hi = outer.enter_context(nc.sbuf_tensor("wet_hi", [P, E * P], F32R))
        wet_lo = outer.enter_context(nc.sbuf_tensor("wet_lo", [P, E * P], F32R))
        fwg_hi = outer.enter_context(nc.sbuf_tensor("fwg_hi", [P, E], F32R))
        fwg_lo = outer.enter_context(nc.sbuf_tensor("fwg_lo", [P, E], F32R))
        be_sb = outer.enter_context(nc.sbuf_tensor("be_sb", [E, P], F32))
        wcat_hi = outer.enter_context(nc.sbuf_tensor("wcat_hi", [P, NLOG], F32R))
        wcat_lo = outer.enter_context(nc.sbuf_tensor("wcat_lo", [P, NLOG], F32R))

        def c(name, rows_=P):
            return cst[0:rows_, CONST[name][0] - NMASK:CONST[name][1] - NMASK]

        def m(name, rows_=P):
            return mask[0:rows_, CONST[name][0]:CONST[name][1]]

        weights_stage(nc, Wq, Wk, Wv, Wg, bg, Wdl, Lparam, Wo, ln_g, ln_b, fWg, fbg, fWe, fbe, table,
                      mn_dram, cst, mask, negm, identr, rows, wet_hi, wet_lo, fwg_hi, fwg_lo, be_sb,
                      wcat_hi, wcat_lo, c)
        token_stage(nc, x, xt_dram, ea_dram, eb_dram, bias_dram, rows, wcat_hi, wcat_lo, c)
        attention_stage(nc, mn_dram, xt_dram, ea_dram, eb_dram, bias_dram, yt_dram, m, c, negm, identr)
        expert_stage(nc, x, yt_dram, out, rows, wet_hi, wet_lo, fwg_hi, fwg_lo, be_sb, c)


def weights_stage(nc, Wq, Wk, Wv, Wg, bg, Wdl, Lparam, Wo, ln_g, ln_b, fWg, fbg, fWe, fbe, table,
                  mn_dram, cst, mask, negm, identr, rows, wet_hi, wet_lo, fwg_hi, fwg_lo, be_sb,
                  wcat_hi, wcat_lo, c):
    with ExitStack() as ctx:
        def sb(name, shape, dt=F32):
            return ctx.enter_context(nc.sbuf_tensor(name, shape, dt))

        def sem(name):
            return ctx.enter_context(nc.semaphore(name))

        masks = sb("masks", [P, NMASK])
        wq = sb("wq", [P, H, P])
        wk = sb("wk", [P, H, P])
        wv = sb("wv", [P, H, P])
        wo = sb("wo", [P, H * P])
        wot = sb("wot", [P, H * P])
        we = sb("we", [P, E, P])
        wcr = sb("wcr", [NLOG, P])
        wcr_t = sb("wcr_t", [P, NLOG])
        wet = sb("wet", [P, E * P])
        fwg = sb("fwg", [P, E])
        row1 = sb("row1", [1, NLOG + 2 * P + E])
        ones = sb("ones", [1, P])
        mn = sb("mn", [P, H, 4, P], F32R)
        m32 = sb("m32", [P, H * P])
        n32 = sb("n32", [P, H * P])
        pm = ctx.enter_context(nc.psum_tensor("pm", [P, H * P], F32))
        pn = ctx.enter_context(nc.psum_tensor("pn", [P, H * P], F32))
        pt = ctx.enter_context(nc.psum_tensor("pt", [P, H * P], F32))
        pr = ctx.enter_context(nc.psum_tensor("pr", [P, 512], F32))
        pc = ctx.enter_context(nc.psum_tensor("pc", [P, 512], F32))

        s_table, s_qk, s_vo, s_small, s_we = (sem(n) for n in ("s_table", "s_qk", "s_vo", "s_small", "s_we"))
        s_cst, s_ones, s_masks = sem("s_cst"), sem("s_ones"), sem("s_masks")
        s_m, s_wot, s_wotc, s_n, s_cat, s_rows = (sem(n) for n in ("s_m", "s_wot", "s_wotc", "s_n", "s_cat", "s_rows"))
        s_wet, s_ptfree = sem("s_wet"), sem("s_ptfree")
        s_m32, s_n32, s_cat32, s_wet32 = (sem(n) for n in ("s_m32", "s_n32", "s_cat32", "s_wet32"))
        s_hi, s_lo, s_stored = sem("s_hi"), sem("s_lo"), sem("s_stored")
        n_small = 0

        with nc.Block() as block:
            @block.sync
            def _(sp):
                sp.dma_start(cst[:, :], table[:, NMASK:]).then_inc(s_cst, 16)
                sp.dma_start(wq[:, :, :], Wq.rearrange("(h e) c -> e h c", h=H)).then_inc(s_qk, 16)
                sp.dma_start(wk[:, :, :], Wk.rearrange("(h e) c -> e h c", h=H)).then_inc(s_qk, 16)
                sp.dma_start(wo[:, :], Wo).then_inc(s_vo, 16)
                sp.dma_start(wv[:, :, :], Wv.rearrange("(h e) c -> e h c", h=H)).then_inc(s_vo, 16)
                sp.dma_start(we[:, :, :], fWe.rearrange("e o c -> o e c")).then_inc(s_we, 16)
                sp.dma_start(masks[:, :], table[:, 0:NMASK]).then_inc(s_table, 16)
                sp.wait_ge(s_hi, 2)
                sp.wait_ge(s_lo, 2)
                sp.dma_start(mn_dram.rearrange("h c k n -> c h (k n)"),
                             mn[:, :, :, :].bitcast(F32).rearrange("c h k n -> c h (k n)")).then_inc(s_stored, 16)
                sp.wait_ge(s_stored, 16)

            @block.gpsimd
            def _(pool):
                pool.memset(ones[:, :], 1.0).then_inc(s_ones, 1)

            wdl_v = Wdl.rearrange("(h l) c -> l h c", h=H)
            small = [(wcr[l * H:(l + 1) * H, :], wdl_v[l]) for l in range(LV)]
            small += [(wcr[LV * H:NLOG, :], Wg),
                      (row1[0:1, 0:LV * H], Lparam.rearrange("(a h) l -> a (h l)", a=1)),
                      (row1[0:1, LV * H:NLOG], bg.rearrange("(a h) -> a h", a=1)),
                      (row1[0:1, NLOG:NLOG + P], ln_g.rearrange("(a h) -> a h", a=1)),
                      (row1[0:1, NLOG + P:NLOG + 2 * P], ln_b.rearrange("(a h) -> a h", a=1)),
                      (row1[0:1, NLOG + 2 * P:NLOG + 2 * P + E], fbg.rearrange("(a h) -> a h", a=1)),
                      (fwg[:, :], fWg), (be_sb[:, :], fbe)]
            n_small = 16 * len(small)

            @block.scalar
            def _(act):
                for dst, src in small:
                    act.dma_start(dst, src).then_inc(s_small, 16)
                act.wait_ge(s_m, 1)
                act.activation(m32[:, :], pm[:, :], ACT.Copy, scale=float(SCALE)).then_inc(s_m32, 1)
                act.wait_ge(s_n, 1)
                act.activation(n32[:, :], pn[:, :], ACT.Copy).then_inc(s_n32, 1)

            @block.tensor
            def _(pe):
                pe.wait_ge(s_qk, 32)
                for h in range(H):
                    last = pe.matmul(pm[:, h * P:(h + 1) * P], wq[:, h, :], wk[:, h, :], start=True, stop=True)
                last.then_inc(s_m, 1)
                pe.wait_ge(s_cst, 16)
                pe.wait_ge(s_vo, 32)
                for h in range(H):
                    last = pe.transpose(pt[:, h * P:(h + 1) * P], wo[:, h * P:(h + 1) * P], c("ident"))
                last.then_inc(s_wot, 1)
                pe.wait_ge(s_small, n_small)
                pe.transpose(pc[:, 0:NLOG], wcr[:, :], c("ident")[0:NLOG, 0:NLOG]).then_inc(s_cat, 1)
                pe.wait_ge(s_ones, 1)
                pe.matmul(pr[:, 0:NLOG + 2 * P + E], ones[:, :], row1[:, :], start=True, stop=True).then_inc(s_rows, 1)
                pe.wait_ge(s_wotc, 1)
                for h in range(H):
                    last = pe.matmul(pn[:, h * P:(h + 1) * P], wv[:, h, :], wot[:, h * P:(h + 1) * P],
                                     start=True, stop=True)
                last.then_inc(s_n, 1)
                pe.wait_ge(s_we, 16)
                for e in range(E):
                    last = pe.transpose(pt[:, e * P:(e + 1) * P], we[:, e, :], c("ident"))
                last.then_inc(s_wet, 1)

            @block.vector
            def _(dve):
                dve.wait_ge(s_cst, 16)
                dve.tensor_scalar(negm[:, :], c("neg"), -1e30, None, ALU.mult).then_inc(s_masks, 1)
                dve.tensor_copy(identr[:, :], c("ident")).then_inc(s_masks, 1)
                dve.wait_ge(s_wot, 1)
                dve.tensor_copy(wot[:, :], pt[:, :]).then_inc(s_wotc, 1)
                dve.wait_ge(s_cat, 1)
                dve.tensor_copy(wcr_t[:, :], pc[:, 0:NLOG]).then_inc(s_cat32, 1)
                dve.wait_ge(s_rows, 1)
                dve.tensor_copy(rows[:, 0:LV * H].rearrange("p (l h) -> p l h", h=H),
                                pr[:, 0:LV * H].rearrange("p (h l) -> p l h", h=H)).then_inc(s_masks, 1)
                dve.tensor_copy(rows[:, LV * H:], pr[:, LV * H:NLOG + 2 * P + E]).then_inc(s_masks, 1)
                dve.wait_ge(s_cat32, 1)
                dve.tensor_copy(wcat_hi[:, :], wcr_t[:, :]).then_inc(s_cat32, 1)
                dve.tensor_copy(fwg_hi[:, :], fwg[:, :]).then_inc(s_cat32, 1)
                dve.wait_ge(s_cat32, 3)
                dve.tensor_tensor(wcat_lo[:, :], wcr_t[:, :], wcat_hi[:, :].bitcast(F32), ALU.subtract).then_inc(s_masks, 1)
                dve.tensor_tensor(fwg_lo[:, :], fwg[:, :], fwg_hi[:, :].bitcast(F32), ALU.subtract).then_inc(s_masks, 1)
                for n, (s_in, src) in enumerate(((s_m32, m32), (s_n32, n32))):
                    dve.wait_ge(s_in, 1)
                    v = src[:, :].rearrange("c (h n) -> c h n", h=H)
                    dve.tensor_copy(mn[:, :, 2 * n, :], v).then_inc(s_hi, 1)
                    dve.wait_ge(s_hi, n + 1)
                    dve.tensor_tensor(mn[:, :, 2 * n + 1, :], v, mn[:, :, 2 * n, :].bitcast(F32),
                                      ALU.subtract).then_inc(s_lo, 1)
                dve.wait_ge(s_wet, 1)
                dve.tensor_copy(wet[:, :], pt[:, :]).then_inc(s_wet32, 1)
                dve.wait_ge(s_wet32, 1)
                dve.tensor_copy(wet_hi[:, :], wet[:, :]).then_inc(s_wet32, 1)
                dve.wait_ge(s_wet32, 2)
                dve.tensor_tensor(wet_lo[:, :], wet[:, :], wet_hi[:, :].bitcast(F32), ALU.subtract).then_inc(s_masks, 1)
                dve.wait_ge(s_table, 16)
                dve.tensor_copy(mask[:, :], masks[:, :]).then_inc(s_masks, 1)
                dve.wait_ge(s_masks, 8)


MEAN_VAR = 6


def mean_var(dve, b, stats, mv, ve, s_mv, s_ve):
    base = b * MEAN_VAR
    even, odd = stats[:, :, 1], stats[:, :, 4]
    dve.tensor_tensor(mv[:, 1, :], even, odd, ALU.add).then_inc(s_mv, 1)
    dve.tensor_tensor(mv[:, 2, :], even, odd, ALU.subtract).then_inc(s_mv, 1)
    dve.tensor_tensor(mv[:, 3, :], stats[:, :, 2], stats[:, :, 5], ALU.add).then_inc(s_mv, 1)
    dve.wait_ge(s_mv, base + 3)
    dve.tensor_scalar(mv[:, 0, :], mv[:, 1, :], 0.5, None, ALU.mult).then_inc(s_mv, 1)
    dve.scalar_tensor_tensor(mv[:, 4, :], mv[:, 2, :], 0.25, mv[:, 2, :], ALU.mult, ALU.mult).then_inc(s_mv, 1)
    dve.tensor_scalar(mv[:, 5, :], mv[:, 3, :], 1.0 / D, EPS, ALU.mult, ALU.add).then_inc(s_mv, 1)
    dve.wait_ge(s_mv, base + MEAN_VAR)
    dve.tensor_tensor(ve[:, :], mv[:, 4, :], mv[:, 5, :], ALU.add).then_inc(s_ve, 1)


def token_stage(nc, x, xt_dram, ea_dram, eb_dram, bias_dram, rows, wcat_hi, wcat_lo, c):
    with ExitStack() as ctx:
        def sb(name, shape, dt=F32):
            return ctx.enter_context(nc.sbuf_tensor(name, shape, dt))

        def sem(name):
            return ctx.enter_context(nc.semaphore(name))

        xb = sb("t_x", [P, NC, P])
        stats = sb("t_stats", [P, NC, 6])
        mv = sb("t_mv", [P, 6, NC])
        ve = sb("t_ve", [P, NC])
        mhalf = sb("t_mhalf", [P, NC])
        rstd = sb("t_rstd", [P, NC])
        xn = sb("t_xn", [P, NC, P])
        xt_hi = sb("t_xt_hi", [P, T], F32R)
        xt_lo = sb("t_xt_lo", [P, T], F32R)
        z = sb("t_z", [P, NC, NLOG])
        az = sb("t_az", [P, NC, NLOG])
        ez = sb("t_ez", [P, NC, NLOG])
        lz = sb("t_lz", [P, NC, NLOG])
        lam = sb("t_lam", [P, NC, NLOG])
        lamc = sb("t_lamc", [P, NC, NLV * H])
        g = sb("t_g", [P, NC, H])
        sums = sb("t_sums", [P, 3, NC, H])
        bias = sb("t_bias", [P, H, NT])
        lnl = sb("t_lnl", [P, NC, NLV * H])
        ell = sb("t_ell", [P, NC, NLV * H])
        onesq = sb("t_ones", [P, P])
        elt_hi = sb("t_elt_hi", [NLV * H, T], F32R)
        elt_lo = sb("t_elt_lo", [NLV * H, T], F32R)
        p_xt = ctx.enter_context(nc.psum_tensor("p_xt", [P, T], F32))
        p_z = ctx.enter_context(nc.psum_tensor("p_z", [P, 2, 512], F32))
        p_el = ctx.enter_context(nc.psum_tensor("p_el", [P, T], F32))
        p_g = ctx.enter_context(nc.psum_tensor("p_g", [P, 512], F32))

        names = ("x_in stats mv ve rstd xn xt hi lo stored logit z az ez lz lam g sums_mm sums bias lamc lnl "
                 "ell elt el_hi el_lo ones").split()
        s = {n: sem(f"t_{n}") for n in names}
        na = LOW * H

        def permuted(t, r0, r1, q):
            return t[r0:r1, :].rearrange("r (q n) -> r q n", q=q)

        def stored(dst, rows_, part, n_l, width):
            return dst[:, part * n_l * width:(part + 1) * n_l * width, :]

        with nc.Block() as block:
            @block.sync
            def _(sp):
                def load(b):
                    sp.dma_start(xb[:, :, :], x[b].rearrange("(i t) c -> t i c", i=NC)).then_inc(s["x_in"], 16)

                def store(b):
                    sp.wait_ge(s["hi"], b + 1)
                    sp.dma_start(xt_dram[b, 0], xt_hi[:, :].bitcast(F32)).then_inc(s["stored"], 16)
                    sp.wait_ge(s["lo"], b + 1)
                    sp.dma_start(xt_dram[b, 1], xt_lo[:, :].bitcast(F32)).then_inc(s["stored"], 16)
                    sp.wait_ge(s["bias"], (b + 1) * NC)
                    sp.dma_start(bias_dram[bass.ds(b * H, H)].rearrange("h s k -> s h k"),
                                 bias[:, :, :]).then_inc(s["stored"], 16)
                    sp.wait_ge(s["el_lo"], (b + 1) * 2)
                    for part, src in ((0, elt_hi), (1, elt_lo)):
                        for l in range(NLV):
                            if l < LOW:
                                dst = ea_dram[bass.ds(b * H, H), (part * LOW + l) * TA:(part * LOW + l + 1) * TA, :]
                            else:
                                k = part * HIGH + l - LOW
                                dst = eb_dram[bass.ds(b * H, H), k * TB:(k + 1) * TB, :]
                            sp.dma_start(dst.rearrange("h q n -> h (q n)"),
                                         src[l * H:(l + 1) * H, :].bitcast(F32)).then_inc(s["stored"], 16)
                    sp.wait_ge(s["stored"], (b + 1) * 16 * (3 + 2 * NLV))

                load(0)
                with sp.Fori(0, B - 1) as b:
                    store(b)
                    load(b + 1)
                store(B - 1)

            @block.gpsimd
            def _(pool):
                pool.memset(mhalf[:, :], -0.5).then_inc(s["ones"], 1)
                pool.wait_ge(s["ones"], 2)
                with pool.Fori(0, B) as b:
                    pool.wait_ge(s["ve"], b + 1)
                    pool.tensor_tensor(rstd[:, :], ve[:, :], mhalf[:, :], ALU.pow).then_inc(s["rstd"], 1)

            @block.vector
            def _(dve):
                dve.memset(onesq[:, :], 1.0).then_inc(s["ones"], 1)
                with dve.Fori(0, B) as b:
                    dve.wait_ge(s["x_in"], (b + 1) * 16)
                    for i in range(NC):
                        dve.bn_stats(stats[:, i, :], xb[:, i, :]).then_inc(s["stats"], 1)
                    dve.wait_ge(s["stats"], (b + 1) * NC)
                    mean_var(dve, b, stats, mv, ve, s["mv"], s["ve"])
                    dve.wait_ge(s["rstd"], b + 1)
                    for i in range(NC):
                        dve.tensor_scalar(xn[:, i, :], xb[:, i, :], mv[:, 0, i:i + 1], rstd[:, i:i + 1],
                                          ALU.subtract, ALU.mult).then_inc(s["xn"], 1)
                    dve.wait_ge(s["hi"], b + 1)
                    dve.tensor_tensor(xt_lo[:, :], p_xt[:, :], xt_hi[:, :].bitcast(F32), ALU.subtract).then_inc(s["lo"], 1)
                    dve.wait_ge(s["logit"], b + 1)
                    half = NC // 2
                    for k in range(2):
                        dve.tensor_tensor(z[:, k * half:(k + 1) * half, :],
                                          p_z[:, k, 0:half * NLOG].rearrange("p (i n) -> p i n", i=half),
                                          rows[:, None, 0:NLOG].broadcast_to([P, half, NLOG]), ALU.add).then_inc(s["z"], 1)
                    dve.wait_ge(s["z"], (b + 1) * 2)
                    dve.wait_ge(s["lz"], b + 1)
                    dve.scalar_tensor_tensor(lam[:, :, :], z[:, :, :], 0.0, lz[:, :, :], ALU.max, ALU.add).then_inc(s["lam"], 1)
                    dve.wait_ge(s["lam"], b + 1)
                    dve.tensor_scalar(g[:, :, :], lam[:, :, LV * H:NLOG], -1.0, None, ALU.mult).then_inc(s["g"], 1)
                    dve.tensor_scalar(lamc[:, :, :], lam[:, :, 0:NLV * H], 1e-19, None, ALU.max).then_inc(s["lamc"], 1)
                    dve.wait_ge(s["sums_mm"], b + 1)
                    dve.tensor_copy(sums[:, :, :, :].rearrange("p k i h -> p (k i h)"), p_g[:, 0:3 * NC * H]).then_inc(s["sums"], 1)
                    dve.wait_ge(s["sums"], b + 1)
                    by_head = sums[:, :, :, :].rearrange("p k i h -> p k h i")
                    dve.tensor_scalar(bias[:, :, 0:NC], by_head[:, 0], -1.0, None, ALU.mult).then_inc(s["bias"], 1)
                    dve.tensor_copy(bias[:, :, BIAS_AT[1]:BIAS_AT[1] + NC - 1], by_head[:, 1, :, 0:NC - 1]).then_inc(s["bias"], 1)
                    for d in range(2, NC):
                        n = NC - d
                        dve.wait_ge(s["bias"], b * NC + d)
                        dve.tensor_tensor(bias[:, :, BIAS_AT[d]:BIAS_AT[d] + n], bias[:, :, BIAS_AT[d - 1]:BIAS_AT[d - 1] + n],
                                          by_head[:, 2, :, d - 1:NC - 1], ALU.add).then_inc(s["bias"], 1)
                    dve.wait_ge(s["lnl"], b + 1)
                    for k in range(2):
                        i0 = k * half
                        dve.tensor_tensor(ell[:, i0:i0 + half, :].rearrange("p i (l h) -> p i l h", h=H),
                                          lnl[:, i0:i0 + half, :].rearrange("p i (l h) -> p i l h", h=H),
                                          sums[:, 0, i0:i0 + half, None, :].broadcast_to([P, half, NLV, H]),
                                          ALU.add).then_inc(s["ell"], 1)
                    for k, (r0, r1, q) in enumerate(((0, na, TA), (na, NLV * H, TB))):
                        dve.wait_ge(s["el_hi"], b * 2 + k + 1)
                        dve.tensor_tensor(permuted(elt_lo, r0, r1, q),
                                          p_el[r0:r1, :].rearrange("r (n q) -> r q n", q=q),
                                          permuted(elt_hi, r0, r1, q).bitcast(F32), ALU.subtract).then_inc(s["el_lo"], 1)

            @block.scalar
            def _(act):
                with act.Fori(0, B) as b:
                    act.wait_ge(s["xt"], b + 1)
                    act.activation(xt_hi[:, :], p_xt[:, :], ACT.Copy).then_inc(s["hi"], 1)
                    act.wait_ge(s["z"], (b + 1) * 2)
                    act.activation(az[:, :, :], z[:, :, :], ACT.Abs).then_inc(s["az"], 1)
                    act.wait_ge(s["az"], b + 1)
                    act.activation(ez[:, :, :], az[:, :, :], ACT.Exp, scale=-1.0).then_inc(s["ez"], 1)
                    act.wait_ge(s["ez"], b + 1)
                    act.activation(lz[:, :, :], ez[:, :, :], ACT.Ln, bias=1.0).then_inc(s["lz"], 1)
                    act.wait_ge(s["lamc"], b + 1)
                    act.activation(lnl[:, :, :], lamc[:, :, :], ACT.Ln).then_inc(s["lnl"], 1)
                    act.wait_ge(s["elt"], b + 1)
                    for r0, r1, q in ((0, na, TA), (na, NLV * H, TB)):
                        act.activation(permuted(elt_hi, r0, r1, q),
                                       p_el[r0:r1, :].rearrange("r (n q) -> r q n", q=q), ACT.Copy).then_inc(s["el_hi"], 1)

            @block.tensor
            def _(pe):
                pe.wait_ge(s["ones"], 2)
                with pe.Fori(0, B) as b:
                    pe.wait_ge(s["xn"], (b + 1) * NC)
                    for i in range(NC):
                        last = pe.transpose(p_xt[:, i * P:(i + 1) * P], xn[:, i, :], c("ident"))
                    last.then_inc(s["xt"], 1)
                    pe.wait_ge(s["hi"], b + 1)
                    pe.wait_ge(s["lo"], b + 1)
                    half = NC // 2
                    for i in range(NC):
                        o = p_z[:, i // half, (i % half) * NLOG:(i % half + 1) * NLOG]
                        hi, lo = xt_hi[:, i * P:(i + 1) * P], xt_lo[:, i * P:(i + 1) * P]
                        pe.matmul(o, hi, wcat_hi[:, :], start=True, stop=False)
                        pe.matmul(o, hi, wcat_lo[:, :], start=False, stop=False)
                        last = pe.matmul(o, lo, wcat_hi[:, :], start=False, stop=True)
                    last.then_inc(s["logit"], 1)
                    pe.wait_ge(s["g"], b + 1)
                    gv = g[:, :, :].rearrange("p i h -> p (i h)")
                    for k, w in enumerate((c("tri"), c("suf"), onesq[:, :])):
                        last = pe.matmul(p_g[:, k * NC * H:(k + 1) * NC * H], w, gv, start=True, stop=True)
                    last.then_inc(s["sums_mm"], 1)
                    pe.wait_ge(s["ell"], (b + 1) * 2)
                    for i in range(NC):
                        last = pe.transpose(p_el[0:NLV * H, i * P:(i + 1) * P], ell[:, i, :], c("ident"))
                    last.then_inc(s["elt"], 1)


def attention_stage(nc, mn_dram, xt_dram, ea_dram, eb_dram, bias_dram, yt_dram, m, c, negm, identr):
    with ExitStack() as ctx:
        def sb(name, shape, dt=F32):
            return ctx.enter_context(nc.sbuf_tensor(name, shape, dt))

        def pb(name, shape):
            return ctx.enter_context(nc.psum_tensor(name, shape, F32))

        def sem(name):
            return ctx.enter_context(nc.semaphore(name))

        xp = [sb(f"xp{k}", [P, T], F32R) for k in range(2)]
        xs = [sb(f"xs{k}", [P, T], F32R) for k in range(2)]
        wt = [sb(f"wt{k}", [P, 4, P], F32R) for k in range(2)]
        ea = [sb(f"ea{k}", [P, P]) for k in range(2)]
        eb = [sb(f"eb{k}", [KB, NC * NTB]) for k in range(2)]
        bias = [sb(f"bias{k}", [P, NT]) for k in range(2)]
        ra = [sb(f"ra{k}", [P, NC, NTA, TA], F32R) for k in range(2)]
        rb = [sb(f"rb{k}", [KB, NC, NTB, TB], F32R) for k in range(2)]
        q_hi = [sb(f"q_hi{k}", [P, T], F32R) for k in range(2)]
        q_lo = [sb(f"q_lo{k}", [P, T], F32R) for k in range(2)]
        v = [sb(f"v{k}", [P, NC, P]) for k in range(2)]
        w = [sb(f"w{k}", [P, NT, P]) for k in range(2)]
        NA = 3
        a = [sb(f"a{k}", [P, 512]) for k in range(NA)]
        yt = sb("yt", [P, T])
        o_ps = pb("o_ps", [P, T])
        s_ps = pb("s_ps", [P, 2, 512])
        l_ps = pb("l_ps", [P, 2, 512])
        q_ps = pb("q_ps", [P, 512])
        v_ps = pb("v_ps", [P, 512])

        xp_in = sem("xp_in")
        xs_in = [sem(f"xs_in{j}") for j in range(NC)]
        e_in = [sem(f"e_in{k}") for k in range(2)]
        w_in = [sem(f"w_in{k}") for k in range(2)]
        ra_ready, rb_ready = sem("ra_ready"), sem("rb_ready")
        l_mm, w_done = sem("l_mm"), sem("w_done")
        q_mm, q_hi_done, q_lo_done = sem("q_mm"), sem("q_hi_done"), sem("q_lo_done")
        v_mm, v_done = sem("v_mm"), sem("v_done")
        s_mm, a_done, head_done = sem("s_mm"), sem("a_done"), sem("head_done")
        y_done, y_out = sem("y_done"), sem("y_out")
        dma_a = c("dma")
        dma_b = c("dmb", KB)

        PIECE = {0: ("u", 0), 2: ("u", 1), 4: ("u", 2), 6: ("u", 3), 7: ("u", 4), 8: ("q", 0), 9: ("q", 1),
                 10: ("v", 0), 11: ("v", 1)}
        ORDER = [PIECE[g] for g in sorted(PIECE)]
        ENDS = [max(g for g in range(NG) if GROUPS[g][0] == j) + 1 for j in range(NC)]

        with nc.Block() as block:
            @block.sync
            def _(sp):
                def load_e(k, n):
                    sp.dma_start(ea[k][:, :], ea_dram[n]).then_inc(e_in[k], 16)
                    sp.dma_start(eb[k][:, :], eb_dram[n]).then_inc(e_in[k], 16)
                    sp.dma_start(bias[k][:, :], bias_dram[n]).then_inc(e_in[k], 16)

                def load_w(k, h):
                    sp.dma_start(wt[k][:, :, :].bitcast(F32), mn_dram[h]).then_inc(w_in[k], 16)

                def load_xp(b):
                    for k in range(2):
                        sp.dma_start(xp[k][:, :].bitcast(F32), xt_dram[b, k]).then_inc(xp_in, 16)

                def load_xs(b, j):
                    for k in range(2):
                        sp.dma_start(xs[k][:, j * P:(j + 1) * P].bitcast(F32),
                                     xt_dram[b, k, :, j * P:(j + 1) * P]).then_inc(xs_in[j], 16)

                def heads(b, last):
                    with sp.Fori(0, H // 2 - 1) as hp:
                        for k in range(2):
                            sp.wait_ge(v_done, 2 * (b * H + hp * 2 + k + 1))
                            load_e(k, b * H + hp * 2 + k + 2)
                            load_w(k, hp * 2 + k + 2)
                    sp.wait_ge(v_done, 2 * (b * H + H - 1))
                    if last:
                        load_e(0, 0)
                        load_w(0, 0)
                        return
                    load_e(0, b * H + H)
                    sp.wait_ge(v_done, 2 * (b * H + H))
                    load_xp(b + 1)
                    load_e(1, b * H + H + 1)
                    sp.wait_ge(xp_in, 32 * (b + 2))
                    load_w(0, 0)
                    load_w(1, 1)
                    for j in range(NC):
                        sp.wait_ge(s_mm, (b * H + H - 1) * NG + ENDS[j])
                        load_xs(b + 1, j)

                load_xp(0)
                load_e(0, 0)
                sp.wait_ge(xp_in, 32)
                load_w(0, 0)
                load_e(1, 1)
                load_w(1, 1)
                for j in range(NC):
                    load_xs(0, j)
                with sp.Fori(0, B - 1) as b:
                    heads(b, False)
                    sp.wait_ge(y_done, 2 * (b + 1))
                    sp.dma_start(yt_dram[b], yt[:, :]).then_inc(y_out, 16)
                heads(B - 1, True)
                sp.wait_ge(y_done, 2 * B)
                sp.dma_start(yt_dram[B - 1], yt[:, :]).then_inc(y_out, 16)
                sp.wait_ge(y_out, 16 * (B + 1))

            @block.gpsimd
            def _(pool):
                def expand(k, n, reused):
                    pool.wait_ge(e_in[k], 48 * (n // 2 + 1) if isinstance(n, int) else 48 * (n + 1))
                    if reused is not None:
                        pool.wait_ge(l_mm, reused)
                    pool.tensor_tensor(ra[k][:, :, :, :].rearrange("p i n q -> p (i n) q"),
                                       ea[k][:, :, None].broadcast_to([P, P, TA]),
                                       dma_a[:, None, :].broadcast_to([P, P, TA]), ALU.mult).then_inc(ra_ready, 1)
                    pool.tensor_tensor(rb[k][:, :, :, :].rearrange("p i n q -> p (i n) q"),
                                       eb[k][:, :, None].broadcast_to([KB, NC * NTB, TB]),
                                       dma_b[:, None, :].broadcast_to([KB, NC * NTB, TB]), ALU.mult).then_inc(rb_ready, 1)

                for k in range(2):
                    expand(k, k, None)
                with pool.Fori(1, NH // 2) as p:
                    for k in range(2):
                        expand(k, p, NU * (p * 2 + k - 1))
                expand(0, NH, NU * (NH - 1))

            @block.scalar
            def _(act):
                def piece(kind, u, k, n):
                    if kind == "u":
                        act.wait_ge(l_mm, n * NU + u + 1)
                        slot = 0
                        for d, i0, cnt in UNITS[u]:
                            for i in range(i0, i0 + cnt):
                                for dd in (range(d, i + 1) if d == 5 else (d,)):
                                    j = i - dd
                                    last = act.activation(
                                        w[k][:, W_AT[j] + dd, :].rearrange("p (f c) -> p f c", f=2),
                                        l_ps[:, :, slot * HF:(slot + 1) * HF], ACT.Exp,
                                        bias=bias[k][:, BIAS_AT[dd] + j:BIAS_AT[dd] + j + 1])
                                slot += 1
                        last.then_inc(w_done, 1)
                    elif kind == "q":
                        act.wait_ge(q_mm, 2 * n + u + 1)
                        act.activation(q_hi[k][:, u * 512:(u + 1) * 512], q_ps[:, :], ACT.Copy).then_inc(q_hi_done, 1)
                    else:
                        act.wait_ge(v_mm, 2 * n + u + 1)
                        act.activation(v[k][:, 4 * u:4 * u + 4, :].rearrange("p j n -> p (j n)"), v_ps[:, :],
                                       ACT.Copy).then_inc(v_done, 1)

                act.wait_ge(e_in[0], 48)
                for kind, u in ORDER:
                    piece(kind, u, 0, 0)
                with act.Fori(0, NH // 2) as p:
                    for k in range(2):
                        act.wait_ge(e_in[1 - k], 48 * (p + 1 + k))
                        act.wait_ge(a_done, NG * (p * 2 + k) + 1)
                        for kind, u in ORDER:
                            piece(kind, u, 1 - k, p * 2 + k + 1)

            @block.vector
            def _(dve):
                def low(u, k, n):
                    dve.wait_ge(q_hi_done, 2 * n + u + 1)
                    dve.tensor_tensor(q_lo[k][:, u * 512:(u + 1) * 512], q_ps[:, :],
                                      q_hi[k][:, u * 512:(u + 1) * 512].bitcast(F32), ALU.subtract).then_inc(q_lo_done, 1)

                dve.sem_inc(y_out, 16)
                for u in range(2):
                    low(u, 0, 0)
                with dve.Fori(0, B) as b:
                    with dve.Fori(0, H // 2) as hp:
                        for k in range(2):
                            n = b * H + hp * 2 + k
                            dve.wait_ge(w_done, (n + 1) * NU)
                            for g, (j, t0, t1) in enumerate(GROUPS):
                                dve.wait_ge(s_mm, n * NG + g + 1)
                                at = W_AT[j] + t0 // P - j
                                dve.tensor_tensor(a[g % NA][:, 0:t1 - t0], s_ps[:, g % 2, 0:t1 - t0],
                                                  w[k][:, at:at + (t1 - t0) // P, :].rearrange("p i n -> p (i n)"),
                                                  ALU.mult).then_inc(a_done, 1)
                                if g in (9, 10):
                                    low(g - 9, 1 - k, n + 1)
                    dve.wait_ge(head_done, H * (b + 1))
                    dve.wait_ge(y_out, 16 * (b + 1))
                    for f in range(2):
                        dve.tensor_copy(yt[:, f * 512:(f + 1) * 512], o_ps[:, f * 512:(f + 1) * 512]).then_inc(y_done, 1)

            @block.tensor
            def _(pe):
                def piece(kind, u, k, n, par_count, first):
                    if kind == "u":
                        if u == 0:
                            pe.wait_ge(ra_ready, n + 1)
                        if u == 1:
                            pe.wait_ge(rb_ready, n + 1)
                        if not (first and u == 0):
                            pe.wait_ge(w_done, n * NU + u)
                        unit(u, k).then_inc(l_mm, 1)
                    elif kind == "q":
                        if u == 0:
                            pe.wait_ge(w_in[k], 16 * par_count)
                        if not (first and u == 0):
                            pe.wait_ge(q_lo_done, 2 * n + u)
                        cols = slice(u * 512, (u + 1) * 512)
                        pe.matmul(q_ps[:, :], wt[k][:, 0, :], xp[0][:, cols], start=True, stop=False)
                        pe.matmul(q_ps[:, :], wt[k][:, 0, :], xp[1][:, cols], start=False, stop=False)
                        pe.matmul(q_ps[:, :], wt[k][:, 1, :], xp[0][:, cols], start=False, stop=True).then_inc(q_mm, 1)
                    else:
                        if not (first and u == 0):
                            pe.wait_ge(v_done, 2 * n + u)
                        for jj in range(4):
                            rows_ = slice((4 * u + jj) * P, (4 * u + jj + 1) * P)
                            o = v_ps[:, jj * P:(jj + 1) * P]
                            pe.matmul(o, xp[0][:, rows_], wt[k][:, 2, :], start=True, stop=False)
                            pe.matmul(o, xp[0][:, rows_], wt[k][:, 3, :], start=False, stop=False)
                            last = pe.matmul(o, xp[1][:, rows_], wt[k][:, 2, :], start=False, stop=True)
                        last.then_inc(v_mm, 1)

                def unit(u, k):
                    started = [False, False]
                    slot = 0
                    last = None

                    def mm(f, o, lhsT, rhs):
                        r = pe.matmul(o, lhsT, rhs, start=not started[f], stop=True, skip_group_check=True)
                        started[f] = True
                        return r

                    for d, i0, cnt in UNITS[u]:
                        bank = [l_ps[:, f, slot * HF:(slot + cnt) * HF].rearrange("p (i c) -> p i c", i=cnt)
                                for f in range(2)]
                        if d == 0:
                            for f in range(2):
                                last = mm(f, bank[f], negm[:, :],
                                          identr[:, None, f * HF:(f + 1) * HF].broadcast_to([P, cnt, HF]))
                        if d <= 1:
                            for tb in range(NTA):
                                f, at = divmod(tb * TA, HF)
                                last = mm(f, bank[f][:, :, at:at + TA], m(f"ma{d}")[:, tb * P:(tb + 1) * P],
                                          ra[k][:, i0:i0 + cnt, tb, :])
                        if d in (1, 2, 4):
                            for tb in range(NTB):
                                f, at = divmod(tb * TB, HF)
                                last = mm(f, bank[f][:, :, at:at + TB], m(f"mb{d}", KB)[:, tb * P:(tb + 1) * P],
                                          rb[k][:, i0:i0 + cnt, tb, :])
                        if d in (3, 5):
                            for f in range(2):
                                last = mm(f, bank[f], m("m9" if d == 3 else "m10", KB),
                                          rb[k][:, i0:i0 + cnt, f * NTB // 2:(f + 1) * NTB // 2, :].rearrange(
                                              "p i n q -> p i (n q)"))
                        slot += cnt
                    return last

                def scores(n, k, b, hp, g):
                    j, t0, t1 = GROUPS[g]
                    if g == 0 or GROUPS[g - 1][0] != j:
                        pe.wait_ge(xs_in[j], 32 * (b + 1))
                    if g < 2:
                        pe.wait_ge(q_lo_done, 2 * n + g + 1)
                    if g >= 2:
                        pe.wait_ge(a_done, n * NG + g - 1)
                    o = s_ps[:, g % 2, 0:t1 - t0]
                    keys = slice(j * P, (j + 1) * P)
                    pe.matmul(o, xs[0][:, keys], q_hi[k][:, t0:t1], start=True, stop=False)
                    pe.matmul(o, xs[0][:, keys], q_lo[k][:, t0:t1], start=False, stop=False)
                    pe.matmul(o, xs[1][:, keys], q_hi[k][:, t0:t1], start=False, stop=True).then_inc(s_mm, 1)

                def values(n, k, g):
                    j, t0, t1 = GROUPS[g]
                    pe.wait_ge(a_done, n * NG + g + 1)
                    if j in (0, NC // 2):
                        pe.wait_ge(v_done, 2 * n + 1 + j // 4)
                    return pe.matmul(o_ps[:, t0:t1], v[k][:, j, :], a[g % NA][:, 0:t1 - t0],
                                     start=False, stop=True, skip_group_check=True)

                def residual():
                    for f in range(2):
                        o = o_ps[:, f * 512:(f + 1) * 512]
                        for part in range(2):
                            pe.matmul(o, identr[:, :], xp[part][:, f * 512:(f + 1) * 512], start=(part == 0),
                                      stop=True, skip_group_check=True)

                for kind, u in ORDER:
                    piece(kind, u, 0, 0, 1, True)
                residual()
                with pe.Fori(0, B) as b:
                    with pe.Fori(0, H // 2) as hp:
                        for k in range(2):
                            n = b * H + hp * 2 + k
                            for g in range(NG):
                                scores(n, k, b, hp, g)
                                if g >= 2:
                                    values(n, k, g - 2)
                                if g in PIECE:
                                    kind, u = PIECE[g]
                                    piece(kind, u, 1 - k, n + 1, b * (H // 2) + hp + 1 + k, False)
                            values(n, k, NG - 2)
                            values(n, k, NG - 1).then_inc(head_done, 1)
                    pe.wait_ge(y_done, 2 * (b + 1))
                    residual()


def expert_stage(nc, x, yt_dram, out, rows, wet_hi, wet_lo, fwg_hi, fwg_lo, be_sb, c):
    with ExitStack() as ctx:
        def sb(name, shape, dt=F32):
            return ctx.enter_context(nc.sbuf_tensor(name, shape, dt))

        def sem(name):
            return ctx.enter_context(nc.semaphore(name))

        yt = sb("e_yt", [P, T])
        xb = sb("e_x", [P, NC, P])
        st = sb("e_st", [P, NC, 6])
        mv = sb("e_mv", [P, 6, NC])
        rs = sb("e_rs", [P, NC])
        r0 = sb("e_r0", [P, NC, P])
        r1 = sb("e_r1", [P, NC, P])
        r2 = sb("e_r2", [P, NC, P])
        x1 = sb("e_x1", [P, NC, P])
        st2 = sb("e_st2", [P, NC, 6])
        mv2 = sb("e_mv2", [P, 6, NC])
        rs2 = sb("e_rs2", [P, NC])
        x2 = sb("e_x2", [P, NC, P])
        x2t_hi = sb("e_x2t_hi", [P, T], F32R)
        x2t_lo = sb("e_x2t_lo", [P, T], F32R)
        gl = [sb(f"e_g{k}", [P, NC, E]) for k in range(12)]
        gm = [sb(f"e_m{k}", [P, NC]) for k in range(6)]
        ve = sb("e_ve", [P, NC])
        ve2 = sb("e_ve2", [P, NC])
        mhalf = sb("e_mhalf", [P, NC])
        gt = sb("e_gt", [E, T])
        acc = sb("e_acc", [P, NC, P])
        p_y = ctx.enter_context(nc.psum_tensor("e_py", [P, NC, P], F32))
        p_e = ctx.enter_context(nc.psum_tensor("e_pe", [P, 2, E, P], F32))
        p_g = ctx.enter_context(nc.psum_tensor("e_pg", [P, T], F32))

        names = ("mhalf ve ve2 in y_t st mv rs r0 r1 r2 x1 st2 mv2 rs2 x2 x2_t hi lo logit gate gexp g gt_mm gt be_mm init "
                 "ex_mm acc out").split()
        s = {n: sem(f"e_{n}") for n in names}
        NGATE = 17
        lng = rows[:, NLOG:NLOG + P]
        lnb = rows[:, NLOG + P:NLOG + 2 * P]
        fb = rows[:, NLOG + 2 * P:NLOG + 2 * P + E]

        def over_tiles(row, n):
            return row[:, None, :].broadcast_to([P, NC, n])

        def over_experts(col):
            return col[:, :, None].broadcast_to([P, NC, E])

        with nc.Block() as block:
            @block.sync
            def _(sp):
                def load(b):
                    sp.dma_start(yt[:, :], yt_dram[b]).then_inc(s["in"], 16)
                    sp.dma_start(xb[:, :, :], x[b].rearrange("(i t) c -> t i c", i=NC)).then_inc(s["in"], 16)

                def store(b):
                    sp.wait_ge(s["acc"], (b + 1) * NC * E)
                    sp.dma_start(out[b].rearrange("(i t) c -> t i c", i=NC), acc[:, :, :]).then_inc(s["out"], 16)
                    sp.wait_ge(s["out"], (b + 1) * 16)

                load(0)
                with sp.Fori(0, B - 1) as b:
                    store(b)
                    load(b + 1)
                store(B - 1)

            @block.gpsimd
            def _(pool):
                pool.memset(mhalf[:, :], -0.5).then_inc(s["mhalf"], 1)
                pool.wait_ge(s["mhalf"], 1)
                with pool.Fori(0, B) as b:
                    pool.wait_ge(s["ve"], b + 1)
                    pool.tensor_tensor(rs[:, :], ve[:, :], mhalf[:, :], ALU.pow).then_inc(s["rs"], 1)
                    pool.wait_ge(s["ve2"], b + 1)
                    pool.tensor_tensor(rs2[:, :], ve2[:, :], mhalf[:, :], ALU.pow).then_inc(s["rs2"], 1)

            @block.tensor
            def _(pe):
                with pe.Fori(0, B) as b:
                    pe.wait_ge(s["in"], (b + 1) * 32)
                    for i in range(NC):
                        last = pe.transpose(p_y[:, i, :], yt[:, i * P:(i + 1) * P], c("ident"))
                    last.then_inc(s["y_t"], 1)
                    pe.wait_ge(s["x2"], (b + 1) * NC)
                    for i in range(NC):
                        last = pe.transpose(p_y[:, i, :], x2[:, i, :], c("ident"))
                    last.then_inc(s["x2_t"], 1)
                    pe.wait_ge(s["hi"], b + 1)
                    pe.wait_ge(s["lo"], b + 1)

                    def three(o, i, hi, lo):
                        a_hi, a_lo = x2t_hi[:, i * P:(i + 1) * P], x2t_lo[:, i * P:(i + 1) * P]
                        pe.matmul(o, a_hi, hi, start=True, stop=False)
                        pe.matmul(o, a_hi, lo, start=False, stop=False)
                        return pe.matmul(o, a_lo, hi, start=False, stop=True)

                    for i in range(NC):
                        last = three(p_e[:, 0, 0, i * E:(i + 1) * E], i, fwg_hi[:, :], fwg_lo[:, :])
                    last.then_inc(s["logit"], 1)
                    pe.wait_ge(s["g"], b + 1)
                    for i in range(NC):
                        last = pe.transpose(p_g[0:E, i * P:(i + 1) * P], gl[11][:, i, :], c("ident"))
                    last.then_inc(s["gt_mm"], 1)
                    pe.wait_ge(s["gt"], b + 1)
                    for i in range(NC):
                        last = pe.matmul(p_y[:, i, :], gt[:, i * P:(i + 1) * P], be_sb[:, :], start=True, stop=True)
                    last.then_inc(s["be_mm"], 1)
                    for i in range(NC):
                        if i >= 2:
                            pe.wait_ge(s["acc"], b * NC * E + (i - 1) * E)
                        for f in range(2):
                            cols = slice(f * 512, (f + 1) * 512)
                            last = three(p_e[:, i % 2, 4 * f:4 * f + 4, :].rearrange("p e n -> p (e n)"), i,
                                         wet_hi[:, cols], wet_lo[:, cols])
                        last.then_inc(s["ex_mm"], 1)

            @block.scalar
            def _(act):
                with act.Fori(0, B) as b:
                    act.wait_ge(s["x2_t"], b + 1)
                    act.activation(x2t_hi[:, :], p_y[:, :, :].rearrange("p i n -> p (i n)"), ACT.Copy).then_inc(s["hi"], 1)
                    act.wait_ge(s["gate"], b * NGATE + 3)
                    act.activation(gl[2][:, :, :], gl[1][:, :, :], ACT.Exp).then_inc(s["gexp"], 1)
                    act.wait_ge(s["gt_mm"], b + 1)
                    act.activation(gt[:, :], p_g[0:E, :], ACT.Copy).then_inc(s["gt"], 1)

            @block.vector
            def _(dve):
                with dve.Fori(0, B) as b:
                    def norm(src, stats, mvv, vee, rst, dst, s_st, s_mv, s_ve, s_rs, s_out):
                        for i in range(NC):
                            dve.bn_stats(stats[:, i, :], src[:, i, :]).then_inc(s_st, 1)
                        dve.wait_ge(s_st, (b + 1) * NC)
                        mean_var(dve, b, stats, mvv, vee, s_mv, s_ve)
                        dve.wait_ge(s_rs, b + 1)
                        for i in range(NC):
                            dve.tensor_scalar(dst[:, i, :], src[:, i, :], mvv[:, 0, i:i + 1], rst[:, i:i + 1],
                                              ALU.subtract, ALU.mult).then_inc(s_out, 1)

                    dve.wait_ge(s["y_t"], b + 1)
                    norm(p_y, st, mv, ve, rs, r0, s["st"], s["mv"], s["ve"], s["rs"], s["r0"])
                    dve.wait_ge(s["r0"], (b + 1) * NC)
                    dve.tensor_tensor(r1[:, :, :], r0[:, :, :], over_tiles(lng, P), ALU.mult).then_inc(s["r1"], 1)
                    dve.wait_ge(s["r1"], b + 1)
                    dve.tensor_tensor(r2[:, :, :], r1[:, :, :], over_tiles(lnb, P), ALU.add).then_inc(s["r2"], 1)
                    dve.wait_ge(s["r2"], b + 1)
                    dve.wait_ge(s["in"], (b + 1) * 32)
                    dve.tensor_tensor(x1[:, :, :], r2[:, :, :], xb[:, :, :], ALU.add).then_inc(s["x1"], 1)
                    dve.wait_ge(s["x1"], b + 1)
                    norm(x1, st2, mv2, ve2, rs2, x2, s["st2"], s["mv2"], s["ve2"], s["rs2"], s["x2"])
                    dve.wait_ge(s["hi"], b + 1)
                    dve.tensor_tensor(x2t_lo[:, :], p_y[:, :, :].rearrange("p i n -> p (i n)"),
                                      x2t_hi[:, :].bitcast(F32), ALU.subtract).then_inc(s["lo"], 1)

                    count = [0]

                    def step(ins):
                        count[0] += 1
                        ins.then_inc(s["gate"], 1)
                        dve.wait_ge(s["gate"], b * NGATE + count[0])

                    first = over_tiles(c("first"), E)
                    dve.wait_ge(s["logit"], b + 1)
                    step(dve.tensor_tensor(gl[0][:, :, :], p_e[:, 0, 0, 0:NC * E].rearrange("p (i e) -> p i e", i=NC),
                                           over_tiles(fb, E), ALU.add))
                    step(dve.tensor_reduce(gm[0][:, :], gl[0][:, :, :], AX, ALU.max))
                    step(dve.tensor_tensor(gl[1][:, :, :], gl[0][:, :, :], over_experts(gm[0]), ALU.subtract))
                    dve.wait_ge(s["gexp"], b + 1)
                    num = gl[2]

                    def pick(vals, k, mx, eq, rank, best, one):
                        step(dve.tensor_reduce(gm[mx][:, :], vals[:, :, :], AX, ALU.max))
                        step(dve.tensor_tensor(gl[eq][:, :, :], vals[:, :, :], over_experts(gm[mx]), ALU.is_equal))
                        step(dve.tensor_tensor(gl[rank][:, :, :], gl[eq][:, :, :], first, ALU.mult))
                        step(dve.tensor_reduce(gm[best][:, :], gl[rank][:, :, :], AX, ALU.max))
                        step(dve.tensor_tensor(gl[one][:, :, :], gl[rank][:, :, :], over_experts(gm[best]), ALU.is_equal))

                    pick(num, 0, 1, 3, 4, 2, 5)
                    step(dve.scalar_tensor_tensor(gl[6][:, :, :], gl[5][:, :, :], -2.0, num[:, :, :], ALU.mult, ALU.add))
                    pick(gl[6], 1, 3, 7, 8, 4, 9)
                    step(dve.tensor_tensor(gm[5][:, :], gm[1][:, :], gm[3][:, :], ALU.add))
                    step(dve.reciprocal(gm[0][:, :], gm[5][:, :]))
                    step(dve.tensor_tensor(gl[3][:, :, :], gl[5][:, :, :], gl[9][:, :, :], ALU.add))
                    assert count[0] == NGATE, count
                    dve.tensor_tensor(gl[10][:, :, :], gl[3][:, :, :], num[:, :, :], ALU.mult).then_inc(s["init"], 1)
                    dve.wait_ge(s["init"], b * 2 + 1)
                    dve.tensor_tensor(gl[11][:, :, :], gl[10][:, :, :], over_experts(gm[0]), ALU.mult).then_inc(s["g"], 1)
                    dve.wait_ge(s["be_mm"], b + 1)
                    dve.tensor_tensor(r0[:, :, :], x1[:, :, :], p_y[:, :, :], ALU.add).then_inc(s["init"], 1)
                    dve.wait_ge(s["init"], b * 2 + 2)
                    for i in range(NC):
                        dve.wait_ge(s["ex_mm"], b * NC + i + 1)
                        for e in range(E):
                            if e:
                                dve.wait_ge(s["acc"], b * NC * E + i * E + e)
                            dve.scalar_tensor_tensor(acc[:, i, :], p_e[:, i % 2, e, :], gl[11][:, i, e:e + 1],
                                                     r0[:, i, :] if e == 0 else acc[:, i, :],
                                                     ALU.mult, ALU.add).then_inc(s["acc"], 1)


_INS = ["L0_attn_x", "L0_attn_Wq", "L0_attn_Wk", "L0_attn_Wv", "L0_attn_Wg", "L0_attn_bg", "L0_attn_Wdl",
        "L0_attn_Lparam", "L0_attn_Wo", "L0_attn_ln_g", "L0_attn_ln_b", "L0_ffn_Wg", "L0_ffn_bg", "L0_ffn_We",
        "L0_ffn_be"]


def kernel(**inputs):
    import concourse.bacc as bacc
    from concourse.bass_utils import run_bass_kernel_spmd

    nc = bacc.Bacc("TRN2", target_bir_lowering=False, num_devices=1)
    arrays, args = {}, []
    for name in _INS:
        arr = np.ascontiguousarray(inputs[name])
        arrays[f"in_{name}"] = arr
        args.append(nc.dram_tensor(f"in_{name}", arr.shape, mybir.dt.from_np(arr.dtype), kind="ExternalInput").ap())
    arrays["in_table"] = constants()
    args.append(nc.dram_tensor("in_table", [P, NCONST], F32, kind="ExternalInput").ap())
    args.append(nc.dram_tensor("out_0", [B, T, D], F32, kind="ExternalOutput").ap())
    program(nc, *args)
    r = run_bass_kernel_spmd(nc, [arrays], core_ids=[0])
    return r.results[0]["out_0"]
```

```python
from contextlib import ExitStack

import numpy as np

import concourse.bass as bass
from concourse import mybir

P = 128
B, T, D = 8, 1024, 128
H = 8
LV = 12
E = 8
NC = T // P
NH = B * H
NLV = 11
LOW = 8
HIGH = NLV - LOW
TA = P // (2 * LOW)
NTA = P // TA
TB = 16
NTB = P // TB
KB = 2 * HIGH * TB
HF = P // 2
NLOG = LV * H + H
SCALE = 1.0 / np.sqrt(np.float32(P))
EPS = 1e-5
FLOOR = -60000.0

F32 = mybir.dt.float32
F32R = mybir.dt.float32r
F16 = mybir.dt.float16
BF16 = mybir.dt.bfloat16
ALU = mybir.AluOpType
ACT = mybir.ActivationFunctionType
AX = mybir.AxisListType.X

W_AT = [sum(NC - k for k in range(j)) for j in range(NC)]
NT = sum(NC - j for j in range(NC))
BIAS_AT = [sum(NC - k for k in range(d)) for d in range(NC)]
GROUPS = []
for _j in range(NC):
    for _lo in (0, T // 2):
        _a = max(_j * P, _lo)
        if _a < _lo + T // 2:
            GROUPS.append((_j, _a, _lo + T // 2))
NG = len(GROUPS)
UNITS = [[(0, 0, 8)], [(1, 1, 7)], [(2, 2, 6)], [(3, 3, 5), (5, 5, 3)], [(4, 4, 4)]]
NU = len(UNITS)
CONST = {}
_at = 0
for _name, _n in (("ma0", NTA * P), ("ma1", NTA * P), ("mb1", NTB * P), ("mb2", NTB * P), ("mb4", NTB * P),
                  ("m9", P), ("m10", P), ("neg", P), ("ident", P), ("tri", P), ("suf", P), ("dma", TA), ("dmb", TB),
                  ("first", E)):
    CONST[_name] = (_at, _at + _n)
    _at += _n
NCONST = _at
NMASK = CONST["neg"][0]


def constants():
    def level(d):
        return np.where(d <= 0, 0, np.floor(np.log2(np.maximum(d, 1))).astype(np.int64) + 1)

    out = np.zeros((P, NCONST), np.float32)
    row = np.arange(P)
    s = np.arange(P)[None, None, :]

    def put(name, a):
        lo, hi = CONST[name]
        a = a.reshape(a.shape[0], -1)
        out[:a.shape[0], lo:hi] = a

    l_a, q_a = (row // TA % LOW)[:, None, None], (row % TA)[:, None, None]
    t_a = np.arange(NTA)[None, :, None] * TA + q_a
    put("ma0", (s <= t_a) & (level(t_a - s) == l_a))
    put("ma1", (s > t_a) & (level(P + t_a - s) == l_a))
    rb = np.arange(KB)
    l_b, q_b = (rb // TB % HIGH + LOW)[:, None, None], (rb % TB)[:, None, None]
    t_b = np.arange(NTB)[None, :, None] * TB + q_b
    for d in (1, 2, 4):
        put(f"mb{d}", level(d * P + t_b - s) == l_b)
    put("m9", np.broadcast_to(l_b[:, 0] == 9, (KB, P)))
    put("m10", np.broadcast_to(l_b[:, 0] == 10, (KB, P)))
    put("neg", row[None, :] > row[:, None])
    put("ident", row[None, :] == row[:, None])
    put("tri", row[:, None] <= row[None, :])
    put("suf", row[:, None] > row[None, :])
    put("dma", (row % TA)[:, None] == np.arange(TA)[None, :])
    put("dmb", (rb % TB)[:, None] == np.arange(TB)[None, :])
    out[:, CONST["first"][0]:CONST["first"][1]] = E - np.arange(E)
    return out


def program(nc, x, Wq, Wk, Wv, Wg, bg, Wdl, Lparam, Wo, ln_g, ln_b, fWg, fbg, fWe, fbe, table, out):
    m_dram = nc.dram_tensor("m_scratch", [H, P, 2, P], F32, kind="Internal").ap()
    n_dram = nc.dram_tensor("n_scratch", [H // 2, P, 2, 2, P], F32, kind="Internal").ap()
    xt_dram = nc.dram_tensor("xt_scratch", [B, 2, P, T], F32, kind="Internal").ap()
    ea_dram = nc.dram_tensor("ea_scratch", [NH, P, P], F16, kind="Internal").ap()
    eb_dram = nc.dram_tensor("eb_scratch", [NH, KB, NC * NTB], F16, kind="Internal").ap()
    bias_dram = nc.dram_tensor("bias_scratch", [NH, P, NT], F32, kind="Internal").ap()
    yt_dram = nc.dram_tensor("yt_scratch", [B, P, T], F32, kind="Internal").ap()

    with ExitStack() as outer:
        cst = outer.enter_context(nc.sbuf_tensor("cst", [P, NCONST - NMASK], F32))
        mask = outer.enter_context(nc.sbuf_tensor("mask", [P, NMASK], F16))
        negm = outer.enter_context(nc.sbuf_tensor("negm", [P, P], BF16))
        identb = outer.enter_context(nc.sbuf_tensor("identb", [P, P], BF16))
        identr = outer.enter_context(nc.sbuf_tensor("identr", [P, P], F32R))
        rows = outer.enter_context(nc.sbuf_tensor("rows", [P, NLOG + 2 * P + E], F32))
        wet_hi = outer.enter_context(nc.sbuf_tensor("wet_hi", [P, E * P], F32R))
        wet_lo = outer.enter_context(nc.sbuf_tensor("wet_lo", [P, E * P], F32R))
        fwg_hi = outer.enter_context(nc.sbuf_tensor("fwg_hi", [P, E], F32R))
        fwg_lo = outer.enter_context(nc.sbuf_tensor("fwg_lo", [P, E], F32R))
        be_sb = outer.enter_context(nc.sbuf_tensor("be_sb", [E, P], F32))
        wcat_hi = outer.enter_context(nc.sbuf_tensor("wcat_hi", [P, NLOG], F32R))
        wcat_lo = outer.enter_context(nc.sbuf_tensor("wcat_lo", [P, NLOG], F32R))

        def c(name, rows_=P):
            return cst[0:rows_, CONST[name][0] - NMASK:CONST[name][1] - NMASK]

        def m(name, rows_=P):
            return mask[0:rows_, CONST[name][0]:CONST[name][1]]

        weights_stage(nc, Wq, Wk, Wv, Wg, bg, Wdl, Lparam, Wo, ln_g, ln_b, fWg, fbg, fWe, fbe, table,
                      m_dram, n_dram, cst, mask, negm, identb, identr, rows, wet_hi, wet_lo, fwg_hi, fwg_lo, be_sb,
                      wcat_hi, wcat_lo, c)
        token_stage(nc, x, xt_dram, ea_dram, eb_dram, bias_dram, rows, wcat_hi, wcat_lo, c)
        attention_stage(nc, m_dram, n_dram, xt_dram, ea_dram, eb_dram, bias_dram, yt_dram, m, c, negm, identb, identr)
        expert_stage(nc, x, yt_dram, out, rows, wet_hi, wet_lo, fwg_hi, fwg_lo, be_sb, c)


def weights_stage(nc, Wq, Wk, Wv, Wg, bg, Wdl, Lparam, Wo, ln_g, ln_b, fWg, fbg, fWe, fbe, table,
                  m_dram, n_dram, cst, mask, negm, identb, identr, rows, wet_hi, wet_lo, fwg_hi, fwg_lo, be_sb,
                  wcat_hi, wcat_lo, c):
    with ExitStack() as ctx:
        def sb(name, shape, dt=F32):
            return ctx.enter_context(nc.sbuf_tensor(name, shape, dt))

        def sem(name):
            return ctx.enter_context(nc.semaphore(name))

        masks = sb("masks", [P, NMASK])
        wq = sb("wq", [P, H, P])
        wk = sb("wk", [P, H, P])
        wv = sb("wv", [P, H, P])
        wo = sb("wo", [P, H * P])
        wot = sb("wot", [P, H * P])
        we = sb("we", [P, E, P])
        wcr = sb("wcr", [NLOG, P])
        wcr_t = sb("wcr_t", [P, NLOG])
        wet = sb("wet", [P, E * P])
        fwg = sb("fwg", [P, E])
        row1 = sb("row1", [1, NLOG + 2 * P + E])
        ones = sb("ones", [1, P])
        mn = sb("mn", [P, H, 4, P], F32R)
        m32 = sb("m32", [P, H * P])
        n32 = sb("n32", [P, H * P])
        pm = ctx.enter_context(nc.psum_tensor("pm", [P, H * P], F32))
        pn = ctx.enter_context(nc.psum_tensor("pn", [P, H * P], F32))
        pt = ctx.enter_context(nc.psum_tensor("pt", [P, H * P], F32))
        pr = ctx.enter_context(nc.psum_tensor("pr", [P, 512], F32))
        pc = ctx.enter_context(nc.psum_tensor("pc", [P, 512], F32))

        s_table, s_qk, s_vo, s_small, s_we = (sem(n) for n in ("s_table", "s_qk", "s_vo", "s_small", "s_we"))
        s_cst, s_ones, s_masks = sem("s_cst"), sem("s_ones"), sem("s_masks")
        s_m, s_wot, s_wotc, s_n, s_cat, s_rows = (sem(n) for n in ("s_m", "s_wot", "s_wotc", "s_n", "s_cat", "s_rows"))
        s_wet, s_ptfree = sem("s_wet"), sem("s_ptfree")
        s_m32, s_n32, s_cat32, s_wet32 = (sem(n) for n in ("s_m32", "s_n32", "s_cat32", "s_wet32"))
        s_hi, s_lo, s_stored = sem("s_hi"), sem("s_lo"), sem("s_stored")
        n_small = 0

        with nc.Block() as block:
            @block.sync
            def _(sp):
                sp.dma_start(cst[:, :], table[:, NMASK:]).then_inc(s_cst, 16)
                sp.dma_start(wq[:, :, :], Wq.rearrange("(h e) c -> e h c", h=H)).then_inc(s_qk, 16)
                sp.dma_start(wk[:, :, :], Wk.rearrange("(h e) c -> e h c", h=H)).then_inc(s_qk, 16)
                sp.dma_start(wo[:, :], Wo).then_inc(s_vo, 16)
                sp.dma_start(wv[:, :, :], Wv.rearrange("(h e) c -> e h c", h=H)).then_inc(s_vo, 16)
                sp.dma_start(we[:, :, :], fWe.rearrange("e o c -> o e c")).then_inc(s_we, 16)
                sp.dma_start(masks[:, :], table[:, 0:NMASK]).then_inc(s_table, 16)
                sp.wait_ge(s_hi, 2)
                sp.wait_ge(s_lo, 2)
                sp.dma_start(m_dram.rearrange("h c k n -> c h (k n)"),
                             mn[:, :, 0:2, :].bitcast(F32).rearrange("c h k n -> c h (k n)")).then_inc(s_stored, 16)
                for part in range(2):
                    for e in range(2):
                        sp.dma_start(n_dram[:, :, part, e].rearrange("g c n -> c g n"),
                                     mn.bitcast(F32)[:, e::2, 2 + part, :]).then_inc(s_stored, 16)
                sp.wait_ge(s_stored, 80)

            @block.gpsimd
            def _(pool):
                pool.memset(ones[:, :], 1.0).then_inc(s_ones, 1)

            wdl_v = Wdl.rearrange("(h l) c -> l h c", h=H)
            small = [(wcr[l * H:(l + 1) * H, :], wdl_v[l]) for l in range(LV)]
            small += [(wcr[LV * H:NLOG, :], Wg),
                      (row1[0:1, 0:LV * H], Lparam.rearrange("(a h) l -> a (h l)", a=1)),
                      (row1[0:1, LV * H:NLOG], bg.rearrange("(a h) -> a h", a=1)),
                      (row1[0:1, NLOG:NLOG + P], ln_g.rearrange("(a h) -> a h", a=1)),
                      (row1[0:1, NLOG + P:NLOG + 2 * P], ln_b.rearrange("(a h) -> a h", a=1)),
                      (row1[0:1, NLOG + 2 * P:NLOG + 2 * P + E], fbg.rearrange("(a h) -> a h", a=1)),
                      (fwg[:, :], fWg), (be_sb[:, :], fbe)]
            n_small = 16 * len(small)

            @block.scalar
            def _(act):
                for dst, src in small:
                    act.dma_start(dst, src).then_inc(s_small, 16)
                act.wait_ge(s_m, 1)
                act.activation(m32[:, :], pm[:, :], ACT.Copy, scale=float(SCALE)).then_inc(s_m32, 1)
                act.wait_ge(s_n, 1)
                act.activation(n32[:, :], pn[:, :], ACT.Copy).then_inc(s_n32, 1)

            @block.tensor
            def _(pe):
                pe.wait_ge(s_qk, 32)
                for h in range(H):
                    last = pe.matmul(pm[:, h * P:(h + 1) * P], wq[:, h, :], wk[:, h, :], start=True, stop=True)
                last.then_inc(s_m, 1)
                pe.wait_ge(s_cst, 16)
                pe.wait_ge(s_vo, 32)
                for h in range(H):
                    last = pe.transpose(pt[:, h * P:(h + 1) * P], wo[:, h * P:(h + 1) * P], c("ident"))
                last.then_inc(s_wot, 1)
                pe.wait_ge(s_small, n_small)
                pe.transpose(pc[:, 0:NLOG], wcr[:, :], c("ident")[0:NLOG, 0:NLOG]).then_inc(s_cat, 1)
                pe.wait_ge(s_ones, 1)
                pe.matmul(pr[:, 0:NLOG + 2 * P + E], ones[:, :], row1[:, :], start=True, stop=True).then_inc(s_rows, 1)
                pe.wait_ge(s_wotc, 1)
                for h in range(H):
                    last = pe.matmul(pn[:, h * P:(h + 1) * P], wv[:, h, :], wot[:, h * P:(h + 1) * P],
                                     start=True, stop=True)
                last.then_inc(s_n, 1)
                pe.wait_ge(s_we, 16)
                for e in range(E):
                    last = pe.transpose(pt[:, e * P:(e + 1) * P], we[:, e, :], c("ident"))
                last.then_inc(s_wet, 1)

            @block.vector
            def _(dve):
                dve.wait_ge(s_cst, 16)
                dve.tensor_scalar(negm[:, :], c("neg"), -1e30, None, ALU.mult).then_inc(s_masks, 1)
                dve.tensor_copy(identr[:, :], c("ident")).then_inc(s_masks, 1)
                dve.tensor_copy(identb[:, :], c("ident")).then_inc(s_masks, 1)
                dve.wait_ge(s_wot, 1)
                dve.tensor_copy(wot[:, :], pt[:, :]).then_inc(s_wotc, 1)
                dve.wait_ge(s_cat, 1)
                dve.tensor_copy(wcr_t[:, :], pc[:, 0:NLOG]).then_inc(s_cat32, 1)
                dve.wait_ge(s_rows, 1)
                dve.tensor_copy(rows[:, 0:LV * H].rearrange("p (l h) -> p l h", h=H),
                                pr[:, 0:LV * H].rearrange("p (h l) -> p l h", h=H)).then_inc(s_masks, 1)
                dve.tensor_copy(rows[:, LV * H:], pr[:, LV * H:NLOG + 2 * P + E]).then_inc(s_masks, 1)
                dve.wait_ge(s_cat32, 1)
                dve.tensor_copy(wcat_hi[:, :], wcr_t[:, :]).then_inc(s_cat32, 1)
                dve.tensor_copy(fwg_hi[:, :], fwg[:, :]).then_inc(s_cat32, 1)
                dve.wait_ge(s_cat32, 3)
                dve.tensor_tensor(wcat_lo[:, :], wcr_t[:, :], wcat_hi[:, :].bitcast(F32), ALU.subtract).then_inc(s_masks, 1)
                dve.tensor_tensor(fwg_lo[:, :], fwg[:, :], fwg_hi[:, :].bitcast(F32), ALU.subtract).then_inc(s_masks, 1)
                for n, (s_in, src) in enumerate(((s_m32, m32), (s_n32, n32))):
                    dve.wait_ge(s_in, 1)
                    v = src[:, :].rearrange("c (h n) -> c h n", h=H)
                    dve.tensor_copy(mn[:, :, 2 * n, :], v).then_inc(s_hi, 1)
                    dve.wait_ge(s_hi, n + 1)
                    dve.tensor_tensor(mn[:, :, 2 * n + 1, :], v, mn[:, :, 2 * n, :].bitcast(F32),
                                      ALU.subtract).then_inc(s_lo, 1)
                dve.wait_ge(s_wet, 1)
                dve.tensor_copy(wet[:, :], pt[:, :]).then_inc(s_wet32, 1)
                dve.wait_ge(s_wet32, 1)
                dve.tensor_copy(wet_hi[:, :], wet[:, :]).then_inc(s_wet32, 1)
                dve.wait_ge(s_wet32, 2)
                dve.tensor_tensor(wet_lo[:, :], wet[:, :], wet_hi[:, :].bitcast(F32), ALU.subtract).then_inc(s_masks, 1)
                dve.wait_ge(s_table, 16)
                dve.tensor_copy(mask[:, :], masks[:, :]).then_inc(s_masks, 1)
                dve.wait_ge(s_masks, 9)


MEAN_VAR = 6


def mean_var(dve, b, stats, mv, ve, s_mv, s_ve):
    base = b * MEAN_VAR
    even, odd = stats[:, :, 1], stats[:, :, 4]
    dve.tensor_tensor(mv[:, 1, :], even, odd, ALU.add).then_inc(s_mv, 1)
    dve.tensor_tensor(mv[:, 2, :], even, odd, ALU.subtract).then_inc(s_mv, 1)
    dve.tensor_tensor(mv[:, 3, :], stats[:, :, 2], stats[:, :, 5], ALU.add).then_inc(s_mv, 1)
    dve.wait_ge(s_mv, base + 3)
    dve.tensor_scalar(mv[:, 0, :], mv[:, 1, :], 0.5, None, ALU.mult).then_inc(s_mv, 1)
    dve.scalar_tensor_tensor(mv[:, 4, :], mv[:, 2, :], 0.25, mv[:, 2, :], ALU.mult, ALU.mult).then_inc(s_mv, 1)
    dve.tensor_scalar(mv[:, 5, :], mv[:, 3, :], 1.0 / D, EPS, ALU.mult, ALU.add).then_inc(s_mv, 1)
    dve.wait_ge(s_mv, base + MEAN_VAR)
    dve.tensor_tensor(ve[:, :], mv[:, 4, :], mv[:, 5, :], ALU.add).then_inc(s_ve, 1)


def token_stage(nc, x, xt_dram, ea_dram, eb_dram, bias_dram, rows, wcat_hi, wcat_lo, c):
    with ExitStack() as ctx:
        def sb(name, shape, dt=F32):
            return ctx.enter_context(nc.sbuf_tensor(name, shape, dt))

        def sem(name):
            return ctx.enter_context(nc.semaphore(name))

        xb = sb("t_x", [P, NC, P])
        stats = sb("t_stats", [P, NC, 6])
        mv = sb("t_mv", [P, 6, NC])
        ve = sb("t_ve", [P, NC])
        mhalf = sb("t_mhalf", [P, NC])
        rstd = sb("t_rstd", [P, NC])
        xn = sb("t_xn", [P, NC, P])
        xt_hi = sb("t_xt_hi", [P, T], F32R)
        xt_lo = sb("t_xt_lo", [P, T], F32R)
        z = sb("t_z", [P, NC, NLOG])
        az = sb("t_az", [P, NC, NLOG])
        ez = sb("t_ez", [P, NC, NLOG])
        lz = sb("t_lz", [P, NC, NLOG])
        lam = sb("t_lam", [P, NC, NLOG])
        lamc = sb("t_lamc", [P, NC, NLV * H])
        g = sb("t_g", [P, NC, H])
        sums = sb("t_sums", [P, 3, NC, H])
        run = sb("t_run", [P, NC, H])
        bias = sb("t_bias", [P, H, NT])
        lnl = sb("t_lnl", [P, NC, NLV * H])
        ell = sb("t_ell", [P, NC, NLV * H])
        onesq = sb("t_ones", [P, P])
        elt_hi = sb("t_elt_hi", [NLV * H, T], F16)
        elt_lo = sb("t_elt_lo", [NLV * H, T], F16)
        p_xt = ctx.enter_context(nc.psum_tensor("p_xt", [P, T], F32))
        p_z = ctx.enter_context(nc.psum_tensor("p_z", [P, 2, 512], F32))
        p_el = ctx.enter_context(nc.psum_tensor("p_el", [P, T], F32))
        p_g = ctx.enter_context(nc.psum_tensor("p_g", [P, 512], F32))

        names = ("x_in stats mv ve rstd xn xt hi lo stored logit z az ez lz lam g sums_mm sums run bias lamc lnl "
                 "ell elt el_hi el_lo ones").split()
        s = {n: sem(f"t_{n}") for n in names}
        na = LOW * H

        def permuted(t, r0, r1, q):
            return t[r0:r1, :].rearrange("r (q n) -> r q n", q=q)

        def stored(dst, rows_, part, n_l, width):
            return dst[:, part * n_l * width:(part + 1) * n_l * width, :]

        with nc.Block() as block:
            @block.sync
            def _(sp):
                def load(b):
                    sp.dma_start(xb[:, :, :], x[b].rearrange("(i t) c -> t i c", i=NC)).then_inc(s["x_in"], 16)

                def store(b):
                    sp.wait_ge(s["hi"], b + 1)
                    sp.dma_start(xt_dram[b, 0], xt_hi[:, :].bitcast(F32)).then_inc(s["stored"], 16)
                    sp.wait_ge(s["lo"], b + 1)
                    sp.dma_start(xt_dram[b, 1], xt_lo[:, :].bitcast(F32)).then_inc(s["stored"], 16)
                    sp.wait_ge(s["bias"], (b + 1) * NC)
                    sp.dma_start(bias_dram[bass.ds(b * H, H)].rearrange("h s k -> s h k"),
                                 bias[:, :, :]).then_inc(s["stored"], 16)
                    sp.wait_ge(s["el_lo"], (b + 1) * 2)
                    for part, src in ((0, elt_hi), (1, elt_lo)):
                        for l in range(NLV):
                            if l < LOW:
                                dst = ea_dram[bass.ds(b * H, H), (part * LOW + l) * TA:(part * LOW + l + 1) * TA, :]
                            else:
                                k = part * HIGH + l - LOW
                                dst = eb_dram[bass.ds(b * H, H), k * TB:(k + 1) * TB, :]
                            sp.dma_start(dst.rearrange("h q n -> h (q n)"),
                                         src[l * H:(l + 1) * H, :]).then_inc(s["stored"], 16)
                    sp.wait_ge(s["stored"], (b + 1) * 16 * (3 + 2 * NLV))

                load(0)
                with sp.Fori(0, B - 1) as b:
                    store(b)
                    load(b + 1)
                store(B - 1)

            @block.gpsimd
            def _(pool):
                pool.memset(mhalf[:, :], -0.5).then_inc(s["ones"], 1)
                pool.wait_ge(s["ones"], 2)
                with pool.Fori(0, B) as b:
                    pool.wait_ge(s["ve"], b + 1)
                    pool.tensor_tensor(rstd[:, :], ve[:, :], mhalf[:, :], ALU.pow).then_inc(s["rstd"], 1)

            @block.vector
            def _(dve):
                dve.memset(onesq[:, :], 1.0).then_inc(s["ones"], 1)
                with dve.Fori(0, B) as b:
                    dve.wait_ge(s["x_in"], (b + 1) * 16)
                    for i in range(NC):
                        dve.bn_stats(stats[:, i, :], xb[:, i, :]).then_inc(s["stats"], 1)
                    dve.wait_ge(s["stats"], (b + 1) * NC)
                    mean_var(dve, b, stats, mv, ve, s["mv"], s["ve"])
                    dve.wait_ge(s["rstd"], b + 1)
                    for i in range(NC):
                        dve.tensor_scalar(xn[:, i, :], xb[:, i, :], mv[:, 0, i:i + 1], rstd[:, i:i + 1],
                                          ALU.subtract, ALU.mult).then_inc(s["xn"], 1)
                    dve.wait_ge(s["hi"], b + 1)
                    dve.tensor_tensor(xt_lo[:, :], p_xt[:, :], xt_hi[:, :].bitcast(F32), ALU.subtract).then_inc(s["lo"], 1)
                    dve.wait_ge(s["logit"], b + 1)
                    half = NC // 2
                    for k in range(2):
                        dve.tensor_tensor(z[:, k * half:(k + 1) * half, :],
                                          p_z[:, k, 0:half * NLOG].rearrange("p (i n) -> p i n", i=half),
                                          rows[:, None, 0:NLOG].broadcast_to([P, half, NLOG]), ALU.add).then_inc(s["z"], 1)
                    dve.wait_ge(s["z"], (b + 1) * 2)
                    dve.wait_ge(s["lz"], b + 1)
                    dve.scalar_tensor_tensor(lam[:, :, :], z[:, :, :], 0.0, lz[:, :, :], ALU.max, ALU.add).then_inc(s["lam"], 1)
                    dve.wait_ge(s["lam"], b + 1)
                    dve.tensor_scalar(g[:, :, :], lam[:, :, LV * H:NLOG], -1.0, None, ALU.mult).then_inc(s["g"], 1)
                    dve.tensor_scalar(lamc[:, :, :], lam[:, :, 0:NLV * H], 1e-19, None, ALU.max).then_inc(s["lamc"], 1)
                    dve.wait_ge(s["sums_mm"], b + 1)
                    dve.tensor_copy(sums[:, :, :, :].rearrange("p k i h -> p (k i h)"), p_g[:, 0:3 * NC * H]).then_inc(s["sums"], 1)
                    dve.wait_ge(s["sums"], b + 1)
                    by_head = sums[:, :, :, :].rearrange("p k i h -> p k h i")
                    dve.tensor_scalar(bias[:, :, 0:NC], by_head[:, 0], -1.0, -FLOOR, ALU.mult, ALU.min).then_inc(s["bias"], 1)
                    dve.tensor_scalar(run[:, :, :], sums[:, 0], FLOOR, None, ALU.max).then_inc(s["run"], 1)
                    dve.tensor_copy(bias[:, :, BIAS_AT[1]:BIAS_AT[1] + NC - 1], by_head[:, 1, :, 0:NC - 1]).then_inc(s["bias"], 1)
                    for d in range(2, NC):
                        n = NC - d
                        dve.wait_ge(s["bias"], b * NC + d)
                        dve.tensor_tensor(bias[:, :, BIAS_AT[d]:BIAS_AT[d] + n], bias[:, :, BIAS_AT[d - 1]:BIAS_AT[d - 1] + n],
                                          by_head[:, 2, :, d - 1:NC - 1], ALU.add).then_inc(s["bias"], 1)
                    dve.wait_ge(s["lnl"], b + 1)
                    dve.wait_ge(s["run"], b + 1)
                    for k in range(2):
                        i0 = k * half
                        dve.tensor_tensor(ell[:, i0:i0 + half, :].rearrange("p i (l h) -> p i l h", h=H),
                                          lnl[:, i0:i0 + half, :].rearrange("p i (l h) -> p i l h", h=H),
                                          run[:, i0:i0 + half, None, :].broadcast_to([P, half, NLV, H]),
                                          ALU.add).then_inc(s["ell"], 1)
                    for k, (r0, r1, q) in enumerate(((0, na, TA), (na, NLV * H, TB))):
                        dve.wait_ge(s["el_hi"], b * 2 + k + 1)
                        dve.tensor_tensor(permuted(elt_lo, r0, r1, q),
                                          p_el[r0:r1, :].rearrange("r (n q) -> r q n", q=q),
                                          permuted(elt_hi, r0, r1, q), ALU.subtract).then_inc(s["el_lo"], 1)

            @block.scalar
            def _(act):
                with act.Fori(0, B) as b:
                    act.wait_ge(s["xt"], b + 1)
                    act.activation(xt_hi[:, :], p_xt[:, :], ACT.Copy).then_inc(s["hi"], 1)
                    act.wait_ge(s["z"], (b + 1) * 2)
                    act.activation(az[:, :, :], z[:, :, :], ACT.Abs).then_inc(s["az"], 1)
                    act.wait_ge(s["az"], b + 1)
                    act.activation(ez[:, :, :], az[:, :, :], ACT.Exp, scale=-1.0).then_inc(s["ez"], 1)
                    act.wait_ge(s["ez"], b + 1)
                    act.activation(lz[:, :, :], ez[:, :, :], ACT.Ln, bias=1.0).then_inc(s["lz"], 1)
                    act.wait_ge(s["lamc"], b + 1)
                    act.activation(lnl[:, :, :], lamc[:, :, :], ACT.Ln).then_inc(s["lnl"], 1)
                    act.wait_ge(s["elt"], b + 1)
                    for r0, r1, q in ((0, na, TA), (na, NLV * H, TB)):
                        act.activation(permuted(elt_hi, r0, r1, q),
                                       p_el[r0:r1, :].rearrange("r (n q) -> r q n", q=q), ACT.Copy).then_inc(s["el_hi"], 1)

            @block.tensor
            def _(pe):
                pe.wait_ge(s["ones"], 2)
                with pe.Fori(0, B) as b:
                    pe.wait_ge(s["xn"], (b + 1) * NC)
                    for i in range(NC):
                        last = pe.transpose(p_xt[:, i * P:(i + 1) * P], xn[:, i, :], c("ident"))
                    last.then_inc(s["xt"], 1)
                    pe.wait_ge(s["hi"], b + 1)
                    pe.wait_ge(s["lo"], b + 1)
                    half = NC // 2
                    for i in range(NC):
                        o = p_z[:, i // half, (i % half) * NLOG:(i % half + 1) * NLOG]
                        hi, lo = xt_hi[:, i * P:(i + 1) * P], xt_lo[:, i * P:(i + 1) * P]
                        pe.matmul(o, hi, wcat_hi[:, :], start=True, stop=False)
                        pe.matmul(o, hi, wcat_lo[:, :], start=False, stop=False)
                        last = pe.matmul(o, lo, wcat_hi[:, :], start=False, stop=True)
                    last.then_inc(s["logit"], 1)
                    pe.wait_ge(s["g"], b + 1)
                    gv = g[:, :, :].rearrange("p i h -> p (i h)")
                    for k, w in enumerate((c("tri"), c("suf"), onesq[:, :])):
                        last = pe.matmul(p_g[:, k * NC * H:(k + 1) * NC * H], w, gv, start=True, stop=True)
                    last.then_inc(s["sums_mm"], 1)
                    pe.wait_ge(s["ell"], (b + 1) * 2)
                    for i in range(NC):
                        last = pe.transpose(p_el[0:NLV * H, i * P:(i + 1) * P], ell[:, i, :], c("ident"))
                    last.then_inc(s["elt"], 1)


def attention_stage(nc, m_dram, n_dram, xt_dram, ea_dram, eb_dram, bias_dram, yt_dram, m, c, negm, identb, identr):
    with ExitStack() as ctx:
        def sb(name, shape, dt=F32):
            return ctx.enter_context(nc.sbuf_tensor(name, shape, dt))

        def pb(name, shape):
            return ctx.enter_context(nc.psum_tensor(name, shape, F32))

        def sem(name):
            return ctx.enter_context(nc.semaphore(name))

        xp = [sb(f"xp{k}", [P, T], F32R) for k in range(2)]
        xs = [sb(f"xs{k}", [P, T], F32R) for k in range(2)]
        mt = [sb(f"mt{k}", [P, 2, P], F32R) for k in range(2)]
        nt = sb("nt", [P, 2, 2, P], F32R)
        ea = [sb(f"ea{k}", [P, P], F16) for k in range(2)]
        eb = [sb(f"eb{k}", [KB, NC * NTB], F16) for k in range(2)]
        bias = [sb(f"bias{k}", [P, NT]) for k in range(2)]
        ra = [sb(f"ra{k}", [P, NC, NTA, TA], F16) for k in range(2)]
        rb = [sb(f"rb{k}", [KB, NC, NTB, TB], F16) for k in range(2)]
        q_hi = [sb(f"q_hi{k}", [P, T], F32R) for k in range(2)]
        q_lo = [sb(f"q_lo{k}", [P, T], F32R) for k in range(2)]
        v = [sb(f"v{k}", [P, 2, NC, P]) for k in range(2)]
        w = [sb(f"w{k}", [P, NT, P]) for k in range(2)]
        NA = 3
        a = [sb(f"a{k}", [P, 512]) for k in range(NA)]
        yt = sb("yt", [P, T])
        o_ps = pb("o_ps", [P, T])
        s_ps = pb("s_ps", [P, 2, 512])
        l_ps = pb("l_ps", [P, 2, 512])
        q_ps = pb("q_ps", [P, 512])
        v_ps = pb("v_ps", [P, 512])

        xp_in = sem("xp_in")
        xs_in = [sem(f"xs_in{j}") for j in range(NC)]
        e_in = [sem(f"e_in{k}") for k in range(2)]
        m_in = [sem(f"m_in{k}") for k in range(2)]
        n_in = sem("n_in")
        ra_ready, rb_ready = sem("ra_ready"), sem("rb_ready")
        l_mm, w_done = sem("l_mm"), sem("w_done")
        q_mm, q_hi_done, q_done = sem("q_mm"), sem("q_hi_done"), sem("q_done")
        v_mm, v_done = sem("v_mm"), sem("v_done")
        s_mm, a_done, head_done = sem("s_mm"), sem("a_done"), sem("head_done")
        y_done, y_out = sem("y_done"), sem("y_out")
        dma_a = c("dma")
        dma_b = c("dmb", KB)

        EVEN = {0: ("u", 0), 2: ("u", 1), 4: ("u", 2), 6: ("u", 3), 8: ("q", 0), 9: ("u", 4), 10: ("q", 1)}
        ODD = EVEN | {1: ("v", 0), 3: ("v", 1), 5: ("v", 2), 7: ("v", 3)}
        PIECES = (EVEN, ODD)
        ALL = [ODD[g] for g in sorted(ODD)]
        ACT_KINDS = "uv"
        NV = 4
        Q = 4
        ENDS = [max(g for g in range(NG) if GROUPS[g][0] == j) + 1 for j in range(NC)]

        with nc.Block() as block:
            @block.sync
            def _(sp):
                def load_e(k, n):
                    sp.dma_start(ea[k][:, :], ea_dram[n]).then_inc(e_in[k], 16)
                    sp.dma_start(eb[k][:, :], eb_dram[n]).then_inc(e_in[k], 16)
                    sp.dma_start(bias[k][:, :], bias_dram[n]).then_inc(e_in[k], 16)

                def load_m(k, h):
                    sp.dma_start(mt[k][:, :, :].bitcast(F32), m_dram[h]).then_inc(m_in[k], 16)

                def load_n(g):
                    sp.dma_start(nt[:, :, :, :].bitcast(F32), n_dram[g]).then_inc(n_in, 16)

                def load_xp(b):
                    for k in range(2):
                        sp.dma_start(xp[k][:, :].bitcast(F32), xt_dram[b, k]).then_inc(xp_in, 16)

                def load_xs(b, j):
                    for k in range(2):
                        sp.dma_start(xs[k][:, j * P:(j + 1) * P].bitcast(F32),
                                     xt_dram[b, k, :, j * P:(j + 1) * P]).then_inc(xs_in[j], 16)

                def heads(b, last):
                    with sp.Fori(0, H // 2 - 1) as hp:
                        for k in range(2):
                            n = b * H + hp * 2 + k
                            sp.wait_ge(w_done, NU * (n + 1))
                            load_e(k, n + 2)
                            sp.wait_ge(q_done, 2 * (n + 1))
                            load_m(k, hp * 2 + k + 2)
                            if k == 0:
                                sp.wait_ge(v_done, NV * (b * (H // 2) + hp + 1))
                                load_n(hp + 1)
                    sp.wait_ge(w_done, NU * (b * H + H - 1))
                    if last:
                        load_e(0, 0)
                        sp.wait_ge(q_done, 2 * (b * H + H - 1))
                        load_m(0, 0)
                        sp.wait_ge(v_done, NV * (H // 2) * (b + 1))
                        load_n(0)
                        return
                    load_e(0, b * H + H)
                    sp.wait_ge(q_done, 2 * (b * H + H))
                    load_xp(b + 1)
                    sp.wait_ge(w_done, NU * (b * H + H))
                    load_e(1, b * H + H + 1)
                    sp.wait_ge(xp_in, 32 * (b + 2))
                    load_m(0, 0)
                    load_n(0)
                    load_m(1, 1)
                    for j in range(NC):
                        sp.wait_ge(s_mm, (b * H + H - 1) * NG + ENDS[j])
                        load_xs(b + 1, j)

                load_xp(0)
                load_e(0, 0)
                sp.wait_ge(xp_in, 32)
                load_m(0, 0)
                load_n(0)
                load_e(1, 1)
                load_m(1, 1)
                for j in range(NC):
                    load_xs(0, j)
                with sp.Fori(0, B - 1) as b:
                    heads(b, False)
                    sp.wait_ge(y_done, 2 * (b + 1))
                    sp.dma_start(yt_dram[b], yt[:, :]).then_inc(y_out, 16)
                heads(B - 1, True)
                sp.wait_ge(y_done, 2 * B)
                sp.dma_start(yt_dram[B - 1], yt[:, :]).then_inc(y_out, 16)
                sp.wait_ge(y_out, 16 * (B + 1))

            @block.gpsimd
            def _(pool):
                def expand(k, n, reused):
                    pool.wait_ge(e_in[k], 48 * (n // 2 + 1) if isinstance(n, int) else 48 * (n + 1))
                    if reused is not None:
                        pool.wait_ge(l_mm, reused)
                    pool.tensor_tensor(ra[k][:, :, :, :].rearrange("p i n q -> p (i n) q"),
                                       ea[k][:, :, None].broadcast_to([P, P, TA]),
                                       dma_a[:, None, :].broadcast_to([P, P, TA]), ALU.mult).then_inc(ra_ready, 1)
                    pool.tensor_tensor(rb[k][:, :, :, :].rearrange("p i n q -> p (i n) q"),
                                       eb[k][:, :, None].broadcast_to([KB, NC * NTB, TB]),
                                       dma_b[:, None, :].broadcast_to([KB, NC * NTB, TB]), ALU.mult).then_inc(rb_ready, 1)

                for k in range(2):
                    expand(k, k, None)
                with pool.Fori(1, NH // 2) as p:
                    for k in range(2):
                        expand(k, p, NU * (p * 2 + k - 1))
                expand(0, NH, NU * (NH - 1))

            @block.scalar
            def _(act):
                def piece(kind, u, k, n):
                    if kind == "u":
                        act.wait_ge(l_mm, n * NU + u + 1)
                        slot = 0
                        for d, i0, cnt in UNITS[u]:
                            for i in range(i0, i0 + cnt):
                                for dd in (range(d, i + 1) if d == 5 else (d,)):
                                    j = i - dd
                                    last = act.activation(
                                        w[k][:, W_AT[j] + dd, :].rearrange("p (f c) -> p f c", f=2),
                                        l_ps[:, :, slot * HF:(slot + 1) * HF], ACT.Exp,
                                        bias=bias[k][:, BIAS_AT[dd] + j:BIAS_AT[dd] + j + 1])
                                slot += 1
                        last.then_inc(w_done, 1)
                    else:
                        act.wait_ge(v_mm, NV * n + u + 1)
                        act.activation(v[k][:, :, 2 * u:2 * u + 2, :].rearrange("p e j n -> p j e n"),
                                       v_ps[:, :].rearrange("p (j e n) -> p j e n", j=2, e=2),
                                       ACT.Copy).then_inc(v_done, 1)

                act.wait_ge(e_in[0], 48)
                for kind, u in ALL:
                    if kind in ACT_KINDS:
                        piece(kind, u, 0, 0)
                with act.Fori(0, NH // Q) as p:
                    for k in range(Q):
                        act.wait_ge(e_in[(k + 1) % 2], 48 * (p * (Q // 2) + (k + 1) // 2 + 1))
                        act.wait_ge(a_done, NG * (p * Q + k) + 1)
                        for g in range(NG):
                            if g in PIECES[k % 2] and PIECES[k % 2][g][0] in ACT_KINDS:
                                kind, u = PIECES[k % 2][g]
                                if kind == "u":
                                    piece(kind, u, (k + 1) % 2, p * Q + k + 1)
                                else:
                                    piece(kind, u, (k // 2 + 1) % 2, p * (Q // 2) + k // 2 + 1)

            @block.vector
            def _(dve):
                def high(u, k, n):
                    dve.wait_ge(q_mm, 2 * n + u + 1)
                    dve.tensor_copy(q_hi[k][:, u * 512:(u + 1) * 512], q_ps[:, :]).then_inc(q_hi_done, 1)

                def low(u, k, n):
                    dve.wait_ge(q_hi_done, 2 * n + u + 1)
                    dve.tensor_tensor(q_lo[k][:, u * 512:(u + 1) * 512], q_ps[:, :],
                                      q_hi[k][:, u * 512:(u + 1) * 512].bitcast(F32), ALU.subtract).then_inc(q_done, 1)

                dve.sem_inc(y_out, 16)
                for u in range(2):
                    high(u, 0, 0)
                    low(u, 0, 0)
                with dve.Fori(0, B) as b:
                    with dve.Fori(0, H // Q) as hp:
                        for k in range(Q):
                            n = b * H + hp * Q + k
                            dve.wait_ge(w_done, (n + 1) * NU)
                            for g, (j, t0, t1) in enumerate(GROUPS):
                                dve.wait_ge(s_mm, n * NG + g + 1)
                                at = W_AT[j] + t0 // P - j
                                dve.tensor_tensor(a[g % NA][:, 0:t1 - t0], s_ps[:, g % 2, 0:t1 - t0],
                                                  w[k % 2][:, at:at + (t1 - t0) // P, :].rearrange("p i n -> p (i n)"),
                                                  ALU.mult).then_inc(a_done, 1)
                                if g in (9, 11):
                                    high((g - 9) // 2, (k + 1) % 2, n + 1)
                                    low((g - 9) // 2, (k + 1) % 2, n + 1)
                    dve.wait_ge(head_done, H * (b + 1))
                    dve.wait_ge(y_out, 16 * (b + 1))
                    for f in range(2):
                        dve.tensor_copy(yt[:, f * 512:(f + 1) * 512], o_ps[:, f * 512:(f + 1) * 512]).then_inc(y_done, 1)

            @block.tensor
            def _(pe):
                def piece(kind, u, k, n, loads, first):
                    if kind == "u":
                        if u == 0:
                            pe.wait_ge(ra_ready, n + 1)
                        if u == 1:
                            pe.wait_ge(rb_ready, n + 1)
                        if not (first and u == 0):
                            pe.wait_ge(w_done, n * NU + u)
                        unit(u, k).then_inc(l_mm, 1)
                    elif kind == "q":
                        if u == 0:
                            pe.wait_ge(m_in[k], 16 * loads)
                        if not (first and u == 0):
                            pe.wait_ge(q_done, 2 * n + u)
                        cols = slice(u * 512, (u + 1) * 512)
                        pe.matmul(q_ps[:, :], mt[k][:, 0, :], xp[0][:, cols], start=True, stop=False)
                        pe.matmul(q_ps[:, :], mt[k][:, 0, :], xp[1][:, cols], start=False, stop=False)
                        pe.matmul(q_ps[:, :], mt[k][:, 1, :], xp[0][:, cols], start=False, stop=True).then_inc(q_mm, 1)
                    else:
                        if u == 0:
                            pe.wait_ge(n_in, 16 * loads)
                        if not (first and u == 0):
                            pe.wait_ge(v_done, NV * n + u)
                        n_hi, n_lo = (nt[:, part, :, :].rearrange("p e n -> p (e n)") for part in range(2))
                        for jj in range(2):
                            keys = slice((2 * u + jj) * P, (2 * u + jj + 1) * P)
                            o = v_ps[:, jj * 2 * P:(jj + 1) * 2 * P]
                            pe.matmul(o, xp[0][:, keys], n_hi, start=True, stop=False)
                            pe.matmul(o, xp[0][:, keys], n_lo, start=False, stop=False)
                            last = pe.matmul(o, xp[1][:, keys], n_hi, start=False, stop=True)
                        last.then_inc(v_mm, 1)

                def unit(u, k):
                    started = [False, False]
                    slot = 0
                    last = None

                    def mm(f, o, lhsT, rhs):
                        r = pe.matmul(o, lhsT, rhs, start=not started[f], stop=True, skip_group_check=True)
                        started[f] = True
                        return r

                    for d, i0, cnt in UNITS[u]:
                        bank = [l_ps[:, f, slot * HF:(slot + cnt) * HF].rearrange("p (i c) -> p i c", i=cnt)
                                for f in range(2)]
                        if d == 0:
                            for f in range(2):
                                last = mm(f, bank[f], negm[:, :],
                                          identb[:, None, f * HF:(f + 1) * HF].broadcast_to([P, cnt, HF]))
                        if d <= 1:
                            for tb in range(NTA):
                                f, at = divmod(tb * TA, HF)
                                last = mm(f, bank[f][:, :, at:at + TA], m(f"ma{d}")[:, tb * P:(tb + 1) * P],
                                          ra[k][:, i0:i0 + cnt, tb, :])
                        if d in (1, 2, 4):
                            for tb in range(NTB):
                                f, at = divmod(tb * TB, HF)
                                last = mm(f, bank[f][:, :, at:at + TB], m(f"mb{d}", KB)[:, tb * P:(tb + 1) * P],
                                          rb[k][:, i0:i0 + cnt, tb, :])
                        if d in (3, 5):
                            for f in range(2):
                                last = mm(f, bank[f], m("m9" if d == 3 else "m10", KB),
                                          rb[k][:, i0:i0 + cnt, f * NTB // 2:(f + 1) * NTB // 2, :].rearrange(
                                              "p i n q -> p i (n q)"))
                        slot += cnt
                    return last

                def scores(n, k, b, g):
                    j, t0, t1 = GROUPS[g]
                    if g == 0 or GROUPS[g - 1][0] != j:
                        pe.wait_ge(xs_in[j], 32 * (b + 1))
                    if g < 2:
                        pe.wait_ge(q_done, 2 * n + g + 1)
                    if g >= 2:
                        pe.wait_ge(a_done, n * NG + g - 1)
                    o = s_ps[:, g % 2, 0:t1 - t0]
                    keys = slice(j * P, (j + 1) * P)
                    pe.matmul(o, xs[0][:, keys], q_hi[k][:, t0:t1], start=True, stop=False)
                    pe.matmul(o, xs[0][:, keys], q_lo[k][:, t0:t1], start=False, stop=False)
                    pe.matmul(o, xs[1][:, keys], q_hi[k][:, t0:t1], start=False, stop=True).then_inc(s_mm, 1)

                def values(n, k, pair, g):
                    j, t0, t1 = GROUPS[g]
                    pe.wait_ge(a_done, n * NG + g + 1)
                    if k % 2 == 0 and g == 0:
                        pe.wait_ge(v_done, NV * (pair + 1))
                    return pe.matmul(o_ps[:, t0:t1], v[k // 2 % 2][:, k % 2, j, :], a[g % NA][:, 0:t1 - t0],
                                     start=False, stop=True, skip_group_check=True)

                def residual():
                    for f in range(2):
                        o = o_ps[:, f * 512:(f + 1) * 512]
                        for part in range(2):
                            pe.matmul(o, identr[:, :], xp[part][:, f * 512:(f + 1) * 512], start=(part == 0),
                                      stop=True, skip_group_check=True)

                for kind, u in ALL:
                    piece(kind, u, 0, 0, 1, True)
                residual()
                with pe.Fori(0, B) as b:
                    with pe.Fori(0, H // Q) as hp:
                        for k in range(Q):
                            n = b * H + hp * Q + k
                            pair = b * (H // 2) + hp * (Q // 2) + k // 2
                            for g in range(NG):
                                scores(n, k % 2, b, g)
                                if g >= 2:
                                    values(n, k, pair, g - 2)
                                if g in PIECES[k % 2]:
                                    kind, u = PIECES[k % 2][g]
                                    if kind == "v":
                                        piece(kind, u, (k // 2 + 1) % 2, pair + 1, pair + 2, False)
                                    else:
                                        piece(kind, u, (k + 1) % 2, n + 1, pair + 1 + k % 2, False)
                            values(n, k, pair, NG - 2)
                            values(n, k, pair, NG - 1).then_inc(head_done, 1)
                    pe.wait_ge(y_done, 2 * (b + 1))
                    residual()


def expert_stage(nc, x, yt_dram, out, rows, wet_hi, wet_lo, fwg_hi, fwg_lo, be_sb, c):
    with ExitStack() as ctx:
        def sb(name, shape, dt=F32):
            return ctx.enter_context(nc.sbuf_tensor(name, shape, dt))

        def sem(name):
            return ctx.enter_context(nc.semaphore(name))

        yt = sb("e_yt", [P, T])
        xb = sb("e_x", [P, NC, P])
        st = sb("e_st", [P, NC, 6])
        mv = sb("e_mv", [P, 6, NC])
        rs = sb("e_rs", [P, NC])
        r0 = sb("e_r0", [P, NC, P])
        r1 = sb("e_r1", [P, NC, P])
        r2 = sb("e_r2", [P, NC, P])
        x1 = sb("e_x1", [P, NC, P])
        st2 = sb("e_st2", [P, NC, 6])
        mv2 = sb("e_mv2", [P, 6, NC])
        rs2 = sb("e_rs2", [P, NC])
        x2 = sb("e_x2", [P, NC, P])
        x2t_hi = sb("e_x2t_hi", [P, T], F32R)
        x2t_lo = sb("e_x2t_lo", [P, T], F32R)
        gl = [sb(f"e_g{k}", [P, NC, E]) for k in range(12)]
        gm = [sb(f"e_m{k}", [P, NC]) for k in range(6)]
        ve = sb("e_ve", [P, NC])
        ve2 = sb("e_ve2", [P, NC])
        mhalf = sb("e_mhalf", [P, NC])
        gt = sb("e_gt", [E, T])
        acc = sb("e_acc", [P, NC, P])
        p_y = ctx.enter_context(nc.psum_tensor("e_py", [P, NC, P], F32))
        p_e = ctx.enter_context(nc.psum_tensor("e_pe", [P, 2, E, P], F32))
        p_g = ctx.enter_context(nc.psum_tensor("e_pg", [P, T], F32))

        names = ("mhalf ve ve2 in y_t st mv rs r0 r1 r2 x1 st2 mv2 rs2 x2 x2_t hi lo logit gate gexp g gt_mm gt be_mm init "
                 "ex_mm acc out").split()
        s = {n: sem(f"e_{n}") for n in names}
        NGATE = 17
        lng = rows[:, NLOG:NLOG + P]
        lnb = rows[:, NLOG + P:NLOG + 2 * P]
        fb = rows[:, NLOG + 2 * P:NLOG + 2 * P + E]

        def over_tiles(row, n):
            return row[:, None, :].broadcast_to([P, NC, n])

        def over_experts(col):
            return col[:, :, None].broadcast_to([P, NC, E])

        with nc.Block() as block:
            @block.sync
            def _(sp):
                def load(b):
                    sp.dma_start(yt[:, :], yt_dram[b]).then_inc(s["in"], 16)
                    sp.dma_start(xb[:, :, :], x[b].rearrange("(i t) c -> t i c", i=NC)).then_inc(s["in"], 16)

                def store(b):
                    sp.wait_ge(s["acc"], (b + 1) * NC * E)
                    sp.dma_start(out[b].rearrange("(i t) c -> t i c", i=NC), acc[:, :, :]).then_inc(s["out"], 16)
                    sp.wait_ge(s["out"], (b + 1) * 16)

                load(0)
                with sp.Fori(0, B - 1) as b:
                    store(b)
                    load(b + 1)
                store(B - 1)

            @block.gpsimd
            def _(pool):
                pool.memset(mhalf[:, :], -0.5).then_inc(s["mhalf"], 1)
                pool.wait_ge(s["mhalf"], 1)
                with pool.Fori(0, B) as b:
                    pool.wait_ge(s["ve"], b + 1)
                    pool.tensor_tensor(rs[:, :], ve[:, :], mhalf[:, :], ALU.pow).then_inc(s["rs"], 1)
                    pool.wait_ge(s["ve2"], b + 1)
                    pool.tensor_tensor(rs2[:, :], ve2[:, :], mhalf[:, :], ALU.pow).then_inc(s["rs2"], 1)

            @block.tensor
            def _(pe):
                with pe.Fori(0, B) as b:
                    pe.wait_ge(s["in"], (b + 1) * 32)
                    for i in range(NC):
                        last = pe.transpose(p_y[:, i, :], yt[:, i * P:(i + 1) * P], c("ident"))
                    last.then_inc(s["y_t"], 1)
                    pe.wait_ge(s["x2"], (b + 1) * NC)
                    for i in range(NC):
                        last = pe.transpose(p_y[:, i, :], x2[:, i, :], c("ident"))
                    last.then_inc(s["x2_t"], 1)
                    pe.wait_ge(s["hi"], b + 1)
                    pe.wait_ge(s["lo"], b + 1)

                    def three(o, i, hi, lo):
                        a_hi, a_lo = x2t_hi[:, i * P:(i + 1) * P], x2t_lo[:, i * P:(i + 1) * P]
                        pe.matmul(o, a_hi, hi, start=True, stop=False)
                        pe.matmul(o, a_hi, lo, start=False, stop=False)
                        return pe.matmul(o, a_lo, hi, start=False, stop=True)

                    for i in range(NC):
                        last = three(p_e[:, 0, 0, i * E:(i + 1) * E], i, fwg_hi[:, :], fwg_lo[:, :])
                    last.then_inc(s["logit"], 1)
                    pe.wait_ge(s["g"], b + 1)
                    for i in range(NC):
                        last = pe.transpose(p_g[0:E, i * P:(i + 1) * P], gl[11][:, i, :], c("ident"))
                    last.then_inc(s["gt_mm"], 1)
                    pe.wait_ge(s["gt"], b + 1)
                    for i in range(NC):
                        last = pe.matmul(p_y[:, i, :], gt[:, i * P:(i + 1) * P], be_sb[:, :], start=True, stop=True)
                    last.then_inc(s["be_mm"], 1)
                    for i in range(NC):
                        if i >= 2:
                            pe.wait_ge(s["acc"], b * NC * E + (i - 1) * E)
                        for f in range(2):
                            cols = slice(f * 512, (f + 1) * 512)
                            last = three(p_e[:, i % 2, 4 * f:4 * f + 4, :].rearrange("p e n -> p (e n)"), i,
                                         wet_hi[:, cols], wet_lo[:, cols])
                        last.then_inc(s["ex_mm"], 1)

            @block.scalar
            def _(act):
                with act.Fori(0, B) as b:
                    act.wait_ge(s["x2_t"], b + 1)
                    act.activation(x2t_hi[:, :], p_y[:, :, :].rearrange("p i n -> p (i n)"), ACT.Copy).then_inc(s["hi"], 1)
                    act.wait_ge(s["gate"], b * NGATE + 3)
                    act.activation(gl[2][:, :, :], gl[1][:, :, :], ACT.Exp).then_inc(s["gexp"], 1)
                    act.wait_ge(s["gt_mm"], b + 1)
                    act.activation(gt[:, :], p_g[0:E, :], ACT.Copy).then_inc(s["gt"], 1)

            @block.vector
            def _(dve):
                with dve.Fori(0, B) as b:
                    def norm(src, stats, mvv, vee, rst, dst, s_st, s_mv, s_ve, s_rs, s_out):
                        for i in range(NC):
                            dve.bn_stats(stats[:, i, :], src[:, i, :]).then_inc(s_st, 1)
                        dve.wait_ge(s_st, (b + 1) * NC)
                        mean_var(dve, b, stats, mvv, vee, s_mv, s_ve)
                        dve.wait_ge(s_rs, b + 1)
                        for i in range(NC):
                            dve.tensor_scalar(dst[:, i, :], src[:, i, :], mvv[:, 0, i:i + 1], rst[:, i:i + 1],
                                              ALU.subtract, ALU.mult).then_inc(s_out, 1)

                    dve.wait_ge(s["y_t"], b + 1)
                    norm(p_y, st, mv, ve, rs, r0, s["st"], s["mv"], s["ve"], s["rs"], s["r0"])
                    dve.wait_ge(s["r0"], (b + 1) * NC)
                    dve.tensor_tensor(r1[:, :, :], r0[:, :, :], over_tiles(lng, P), ALU.mult).then_inc(s["r1"], 1)
                    dve.wait_ge(s["r1"], b + 1)
                    dve.tensor_tensor(r2[:, :, :], r1[:, :, :], over_tiles(lnb, P), ALU.add).then_inc(s["r2"], 1)
                    dve.wait_ge(s["r2"], b + 1)
                    dve.wait_ge(s["in"], (b + 1) * 32)
                    dve.tensor_tensor(x1[:, :, :], r2[:, :, :], xb[:, :, :], ALU.add).then_inc(s["x1"], 1)
                    dve.wait_ge(s["x1"], b + 1)
                    norm(x1, st2, mv2, ve2, rs2, x2, s["st2"], s["mv2"], s["ve2"], s["rs2"], s["x2"])
                    dve.wait_ge(s["hi"], b + 1)
                    dve.tensor_tensor(x2t_lo[:, :], p_y[:, :, :].rearrange("p i n -> p (i n)"),
                                      x2t_hi[:, :].bitcast(F32), ALU.subtract).then_inc(s["lo"], 1)

                    count = [0]

                    def step(ins):
                        count[0] += 1
                        ins.then_inc(s["gate"], 1)
                        dve.wait_ge(s["gate"], b * NGATE + count[0])

                    first = over_tiles(c("first"), E)
                    dve.wait_ge(s["logit"], b + 1)
                    step(dve.tensor_tensor(gl[0][:, :, :], p_e[:, 0, 0, 0:NC * E].rearrange("p (i e) -> p i e", i=NC),
                                           over_tiles(fb, E), ALU.add))
                    step(dve.tensor_reduce(gm[0][:, :], gl[0][:, :, :], AX, ALU.max))
                    step(dve.tensor_tensor(gl[1][:, :, :], gl[0][:, :, :], over_experts(gm[0]), ALU.subtract))
                    dve.wait_ge(s["gexp"], b + 1)
                    num = gl[2]

                    def pick(vals, k, mx, eq, rank, best, one):
                        step(dve.tensor_reduce(gm[mx][:, :], vals[:, :, :], AX, ALU.max))
                        step(dve.tensor_tensor(gl[eq][:, :, :], vals[:, :, :], over_experts(gm[mx]), ALU.is_equal))
                        step(dve.tensor_tensor(gl[rank][:, :, :], gl[eq][:, :, :], first, ALU.mult))
                        step(dve.tensor_reduce(gm[best][:, :], gl[rank][:, :, :], AX, ALU.max))
                        step(dve.tensor_tensor(gl[one][:, :, :], gl[rank][:, :, :], over_experts(gm[best]), ALU.is_equal))

                    pick(num, 0, 1, 3, 4, 2, 5)
                    step(dve.scalar_tensor_tensor(gl[6][:, :, :], gl[5][:, :, :], -2.0, num[:, :, :], ALU.mult, ALU.add))
                    pick(gl[6], 1, 3, 7, 8, 4, 9)
                    step(dve.tensor_tensor(gm[5][:, :], gm[1][:, :], gm[3][:, :], ALU.add))
                    step(dve.reciprocal(gm[0][:, :], gm[5][:, :]))
                    step(dve.tensor_tensor(gl[3][:, :, :], gl[5][:, :, :], gl[9][:, :, :], ALU.add))
                    assert count[0] == NGATE, count
                    dve.tensor_tensor(gl[10][:, :, :], gl[3][:, :, :], num[:, :, :], ALU.mult).then_inc(s["init"], 1)
                    dve.wait_ge(s["init"], b * 2 + 1)
                    dve.tensor_tensor(gl[11][:, :, :], gl[10][:, :, :], over_experts(gm[0]), ALU.mult).then_inc(s["g"], 1)
                    dve.wait_ge(s["be_mm"], b + 1)
                    dve.tensor_tensor(r0[:, :, :], x1[:, :, :], p_y[:, :, :], ALU.add).then_inc(s["init"], 1)
                    dve.wait_ge(s["init"], b * 2 + 2)
                    for i in range(NC):
                        dve.wait_ge(s["ex_mm"], b * NC + i + 1)
                        for e in range(E):
                            if e:
                                dve.wait_ge(s["acc"], b * NC * E + i * E + e)
                            dve.scalar_tensor_tensor(acc[:, i, :], p_e[:, i % 2, e, :], gl[11][:, i, e:e + 1],
                                                     r0[:, i, :] if e == 0 else acc[:, i, :],
                                                     ALU.mult, ALU.add).then_inc(s["acc"], 1)


_INS = ["L0_attn_x", "L0_attn_Wq", "L0_attn_Wk", "L0_attn_Wv", "L0_attn_Wg", "L0_attn_bg", "L0_attn_Wdl",
        "L0_attn_Lparam", "L0_attn_Wo", "L0_attn_ln_g", "L0_attn_ln_b", "L0_ffn_Wg", "L0_ffn_bg", "L0_ffn_We",
        "L0_ffn_be"]


def kernel(**inputs):
    import concourse.bacc as bacc
    from concourse.bass_utils import run_bass_kernel_spmd

    nc = bacc.Bacc("TRN2", target_bir_lowering=False, num_devices=1)
    arrays, args = {}, []
    for name in _INS:
        arr = np.ascontiguousarray(inputs[name])
        arrays[f"in_{name}"] = arr
        args.append(nc.dram_tensor(f"in_{name}", arr.shape, mybir.dt.from_np(arr.dtype), kind="ExternalInput").ap())
    arrays["in_table"] = constants()
    args.append(nc.dram_tensor("in_table", [P, NCONST], F32, kind="ExternalInput").ap())
    args.append(nc.dram_tensor("out_0", [B, T, D], F32, kind="ExternalOutput").ap())
    program(nc, *args)
    r = run_bass_kernel_spmd(nc, [arrays], core_ids=[0])
    return r.results[0]["out_0"]
```

```python
from contextlib import ExitStack

import numpy as np

import concourse.bass as bass
from concourse import mybir

P = 128
B, T, D = 8, 1024, 128
H = 8
LV = 12
E = 8
NC = T // P
NH = B * H
NLV = 11
LOW = 8
HIGH = NLV - LOW
TA = P // (2 * LOW)
NTA = P // TA
TB = 16
NTB = P // TB
KB = 2 * HIGH * TB
HF = P // 2
NLOG = LV * H + H
BE = 33
SCALE = 1.0 / np.sqrt(np.float32(P))
EPS = 1e-5
FLOOR = -60000.0

F32 = mybir.dt.float32
F32R = mybir.dt.float32r
F16 = mybir.dt.float16
BF16 = mybir.dt.bfloat16
ALU = mybir.AluOpType
ACT = mybir.ActivationFunctionType
AX = mybir.AxisListType.X

W_AT = [sum(NC - k for k in range(j)) for j in range(NC)]
NT = sum(NC - j for j in range(NC))
BIAS_AT = [sum(NC - k for k in range(d)) for d in range(NC)]
GROUPS = []
for _j in range(NC):
    for _lo in (0, T // 2):
        _a = max(_j * P, _lo)
        if _a < _lo + T // 2:
            GROUPS.append((_j, _a, _lo + T // 2))
NG = len(GROUPS)
UNITS = [[(0, 0, 8)], [(1, 1, 7)], [(2, 2, 6)], [(3, 3, 5), (5, 5, 3)], [(4, 4, 4)]]
NU = len(UNITS)
CONST = {}
_at = 0
for _name, _n in (("ma0", NTA * P), ("ma1", NTA * P), ("mb1", NTB * P), ("mb2", NTB * P), ("mb4", NTB * P),
                  ("m9", P), ("m10", P), ("neg", P), ("ident", P), ("tri", P), ("suf", P), ("dma", TA), ("dmb", TB),
                  ("first", E)):
    CONST[_name] = (_at, _at + _n)
    _at += _n
NCONST = _at
NMASK = CONST["neg"][0]


def constants():
    def level(d):
        return np.where(d <= 0, 0, np.floor(np.log2(np.maximum(d, 1))).astype(np.int64) + 1)

    out = np.zeros((P, NCONST), np.float32)
    row = np.arange(P)
    s = np.arange(P)[None, None, :]

    def put(name, a):
        lo, hi = CONST[name]
        a = a.reshape(a.shape[0], -1)
        out[:a.shape[0], lo:hi] = a

    l_a, q_a = (row // TA % LOW)[:, None, None], (row % TA)[:, None, None]
    t_a = np.arange(NTA)[None, :, None] * TA + q_a
    put("ma0", (s <= t_a) & (level(t_a - s) == l_a))
    put("ma1", (s > t_a) & (level(P + t_a - s) == l_a))
    rb = np.arange(KB)
    l_b, q_b = (rb // TB % HIGH + LOW)[:, None, None], (rb % TB)[:, None, None]
    t_b = np.arange(NTB)[None, :, None] * TB + q_b
    for d in (1, 2, 4):
        put(f"mb{d}", level(d * P + t_b - s) == l_b)
    put("m9", np.broadcast_to(l_b[:, 0] == 9, (KB, P)))
    put("m10", np.broadcast_to(l_b[:, 0] == 10, (KB, P)))
    put("neg", row[None, :] > row[:, None])
    put("ident", row[None, :] == row[:, None])
    put("tri", row[:, None] <= row[None, :])
    put("suf", row[:, None] > row[None, :])
    put("dma", (row % TA)[:, None] == np.arange(TA)[None, :])
    put("dmb", (rb % TB)[:, None] == np.arange(TB)[None, :])
    out[:, CONST["first"][0]:CONST["first"][1]] = E - np.arange(E)
    return out


def program(nc, x, Wq, Wk, Wv, Wg, bg, Wdl, Lparam, Wo, ln_g, ln_b, fWg, fbg, fWe, fbe, table, out):
    m_dram = nc.dram_tensor("m_scratch", [H, P, 2, P], F32, kind="Internal").ap()
    n_dram = nc.dram_tensor("n_scratch", [H // 2, P, 2, 2, P], F32, kind="Internal").ap()
    xt_dram = nc.dram_tensor("xt_scratch", [B, 2, P, T], F32, kind="Internal").ap()
    ea_dram = nc.dram_tensor("ea_scratch", [B, 2, H * LOW, T], F16, kind="Internal").ap()
    eb_dram = nc.dram_tensor("eb_scratch", [B, 2, H * HIGH, T], F16, kind="Internal").ap()
    bias_dram = nc.dram_tensor("bias_scratch", [NH, P, NT], F32, kind="Internal").ap()
    yt_dram = nc.dram_tensor("yt_scratch", [B, P, T], F32, kind="Internal").ap()

    with ExitStack() as outer:
        cst = outer.enter_context(nc.sbuf_tensor("cst", [P, NCONST - NMASK], F32))
        mask = outer.enter_context(nc.sbuf_tensor("mask", [P, NMASK], F16))
        negm = outer.enter_context(nc.sbuf_tensor("negm", [P, P], BF16))
        identb = outer.enter_context(nc.sbuf_tensor("identb", [P, P], BF16))
        identr = outer.enter_context(nc.sbuf_tensor("identr", [P, P], F32R))
        rows = outer.enter_context(nc.sbuf_tensor("rows", [P, NLOG + 2 * P + E], F32))
        wet_hi = outer.enter_context(nc.sbuf_tensor("wet_hi", [P, E * P], F32R))
        wet_lo = outer.enter_context(nc.sbuf_tensor("wet_lo", [P, E * P], F32R))
        fwg_hi = outer.enter_context(nc.sbuf_tensor("fwg_hi", [P, E], F32R))
        fwg_lo = outer.enter_context(nc.sbuf_tensor("fwg_lo", [P, E], F32R))
        be2 = outer.enter_context(nc.sbuf_tensor("be2", [BE, E * P], F32R))
        onesr = outer.enter_context(nc.sbuf_tensor("onesr", [BE, P], F32R))
        wcat_hi = outer.enter_context(nc.sbuf_tensor("wcat_hi", [P, NLOG], F32R))
        wcat_lo = outer.enter_context(nc.sbuf_tensor("wcat_lo", [P, NLOG], F32R))

        def c(name, rows_=P):
            return cst[0:rows_, CONST[name][0] - NMASK:CONST[name][1] - NMASK]

        def m(name, rows_=P):
            return mask[0:rows_, CONST[name][0]:CONST[name][1]]

        weights_stage(nc, Wq, Wk, Wv, Wg, bg, Wdl, Lparam, Wo, ln_g, ln_b, fWg, fbg, fWe, fbe, table,
                      m_dram, n_dram, cst, mask, negm, identb, identr, rows, wet_hi, wet_lo, fwg_hi, fwg_lo, be2, onesr,
                      wcat_hi, wcat_lo, c)
        token_stage(nc, x, table, mask, xt_dram, ea_dram, eb_dram, bias_dram, rows, wcat_hi, wcat_lo, c)
        attention_stage(nc, m_dram, n_dram, xt_dram, ea_dram, eb_dram, bias_dram, yt_dram, m, c, negm, identb, identr)
        expert_stage(nc, x, yt_dram, out, rows, wet_hi, wet_lo, fwg_hi, fwg_lo, be2, onesr, c)


def weights_stage(nc, Wq, Wk, Wv, Wg, bg, Wdl, Lparam, Wo, ln_g, ln_b, fWg, fbg, fWe, fbe, table,
                  m_dram, n_dram, cst, mask, negm, identb, identr, rows, wet_hi, wet_lo, fwg_hi, fwg_lo, be2, onesr,
                  wcat_hi, wcat_lo, c):
    with ExitStack() as ctx:
        def sb(name, shape, dt=F32):
            return ctx.enter_context(nc.sbuf_tensor(name, shape, dt))

        def sem(name):
            return ctx.enter_context(nc.semaphore(name))

        wq = sb("wq", [P, H, P])
        wk = sb("wk", [P, H, P])
        wv = sb("wv", [P, H, P])
        wo = sb("wo", [P, H * P])
        wot = sb("wot", [P, H * P])
        we = sb("we", [P, E, P])
        wcr = sb("wcr", [NLOG, P])
        wcr_t = sb("wcr_t", [P, NLOG])
        wet = sb("wet", [P, E * P])
        fwg = sb("fwg", [P, E])
        row1 = sb("row1", [1, NLOG + 2 * P + E])
        ones = sb("ones", [BE, P])
        be_rows = sb("be_rows", [BE, E * P])
        mn = sb("mn", [P, H, 4, P], F32R)
        m32 = sb("m32", [P, H * P])
        n32 = sb("n32", [P, H * P])
        pm = ctx.enter_context(nc.psum_tensor("pm", [P, H * P], F32))
        pn = ctx.enter_context(nc.psum_tensor("pn", [P, H * P], F32))
        pt = ctx.enter_context(nc.psum_tensor("pt", [P, H * P], F32))
        pr = ctx.enter_context(nc.psum_tensor("pr", [P, 512], F32))
        pc = ctx.enter_context(nc.psum_tensor("pc", [P, 512], F32))

        s_qk, s_vo, s_small, s_we = (sem(n) for n in ("s_qk", "s_vo", "s_small", "s_we"))
        s_cst, s_ones, s_masks = sem("s_cst"), sem("s_ones"), sem("s_masks")
        s_m, s_wot, s_wotc, s_n, s_cat, s_rows = (sem(n) for n in ("s_m", "s_wot", "s_wotc", "s_n", "s_cat", "s_rows"))
        s_wet, s_be = sem("s_wet"), sem("s_be")
        s_m32, s_n32, s_cat32, s_wet32 = (sem(n) for n in ("s_m32", "s_n32", "s_cat32", "s_wet32"))
        s_hi, s_lo, s_stored = sem("s_hi"), sem("s_lo"), sem("s_stored")
        n_small = 0

        with nc.Block() as block:
            @block.sync
            def _(sp):
                sp.dma_start(cst[:, :], table[:, NMASK:]).then_inc(s_cst, 16)
                sp.dma_start(wq[:, :, :], Wq.rearrange("(h e) c -> e h c", h=H)).then_inc(s_qk, 16)
                sp.dma_start(wk[:, :, :], Wk.rearrange("(h e) c -> e h c", h=H)).then_inc(s_qk, 16)
                sp.dma_start(wo[:, :], Wo).then_inc(s_vo, 16)
                sp.dma_start(wv[:, :, :], Wv.rearrange("(h e) c -> e h c", h=H)).then_inc(s_vo, 16)
                sp.dma_start(we[:, :, :], fWe.rearrange("e o c -> o e c")).then_inc(s_we, 16)
                sp.wait_ge(s_hi, 2)
                sp.wait_ge(s_lo, 2)
                sp.dma_start(m_dram.rearrange("h c k n -> c h (k n)"),
                             mn[:, :, 0:2, :].bitcast(F32).rearrange("c h k n -> c h (k n)")).then_inc(s_stored, 16)
                for part in range(2):
                    for e in range(2):
                        sp.dma_start(n_dram[:, :, part, e].rearrange("g c n -> c g n"),
                                     mn.bitcast(F32)[:, e::2, 2 + part, :]).then_inc(s_stored, 16)
                sp.wait_ge(s_stored, 80)

            @block.gpsimd
            def _(pool):
                pool.memset(ones[:, :], 1.0).then_inc(s_ones, 1)
                pool.memset(be_rows[:, :], 0.0).then_inc(s_ones, 1)

            wdl_v = Wdl.rearrange("(h l) c -> l h c", h=H)
            small = [(wcr[l * H:(l + 1) * H, :], wdl_v[l]) for l in range(LV)]
            small += [(wcr[LV * H:NLOG, :], Wg),
                      (row1[0:1, 0:LV * H], Lparam.rearrange("(a h) l -> a (h l)", a=1)),
                      (row1[0:1, LV * H:NLOG], bg.rearrange("(a h) -> a h", a=1)),
                      (row1[0:1, NLOG:NLOG + P], ln_g.rearrange("(a h) -> a h", a=1)),
                      (row1[0:1, NLOG + P:NLOG + 2 * P], ln_b.rearrange("(a h) -> a h", a=1)),
                      (row1[0:1, NLOG + 2 * P:NLOG + 2 * P + E], fbg.rearrange("(a h) -> a h", a=1)),
                      (fwg[:, :], fWg)]
            small += [(be_rows[r:r + 1, :], fbe.rearrange("(a e) o -> a (e o)", a=1)) for r in (0, BE - 1)]
            n_small = 16 * len(small)

            @block.scalar
            def _(act):
                act.wait_ge(s_ones, 2)
                for dst, src in small:
                    act.dma_start(dst, src).then_inc(s_small, 16)
                act.wait_ge(s_m, 1)
                act.activation(m32[:, :], pm[:, :], ACT.Copy, scale=float(SCALE)).then_inc(s_m32, 1)
                act.wait_ge(s_n, 1)
                act.activation(n32[:, :], pn[:, :], ACT.Copy).then_inc(s_n32, 1)

            @block.tensor
            def _(pe):
                pe.wait_ge(s_qk, 32)
                for h in range(H):
                    last = pe.matmul(pm[:, h * P:(h + 1) * P], wq[:, h, :], wk[:, h, :], start=True, stop=True)
                last.then_inc(s_m, 1)
                pe.wait_ge(s_cst, 16)
                pe.wait_ge(s_vo, 32)
                for h in range(H):
                    last = pe.transpose(pt[:, h * P:(h + 1) * P], wo[:, h * P:(h + 1) * P], c("ident"))
                last.then_inc(s_wot, 1)
                pe.wait_ge(s_small, n_small)
                pe.transpose(pc[:, 0:NLOG], wcr[:, :], c("ident")[0:NLOG, 0:NLOG]).then_inc(s_cat, 1)
                pe.wait_ge(s_ones, 1)
                pe.matmul(pr[:, 0:NLOG + 2 * P + E], ones[0:1, :], row1[:, :], start=True, stop=True).then_inc(s_rows, 1)
                pe.wait_ge(s_wotc, 1)
                for h in range(H):
                    last = pe.matmul(pn[:, h * P:(h + 1) * P], wv[:, h, :], wot[:, h * P:(h + 1) * P],
                                     start=True, stop=True)
                last.then_inc(s_n, 1)
                pe.wait_ge(s_we, 16)
                for e in range(E):
                    last = pe.transpose(pt[:, e * P:(e + 1) * P], we[:, e, :], c("ident"))
                last.then_inc(s_wet, 1)

            @block.vector
            def _(dve):
                dve.wait_ge(s_cst, 16)
                dve.tensor_scalar(negm[:, :], c("neg"), -1e30, None, ALU.mult).then_inc(s_masks, 1)
                dve.tensor_copy(identr[:, :], c("ident")).then_inc(s_masks, 1)
                dve.tensor_copy(identb[:, :], c("ident")).then_inc(s_masks, 1)
                dve.wait_ge(s_wot, 1)
                dve.tensor_copy(wot[:, :], pt[:, :]).then_inc(s_wotc, 1)
                dve.wait_ge(s_cat, 1)
                dve.tensor_copy(wcr_t[:, :], pc[:, 0:NLOG]).then_inc(s_cat32, 1)
                dve.wait_ge(s_rows, 1)
                dve.tensor_copy(rows[:, 0:LV * H].rearrange("p (l h) -> p l h", h=H),
                                pr[:, 0:LV * H].rearrange("p (h l) -> p l h", h=H)).then_inc(s_masks, 1)
                dve.tensor_copy(rows[:, LV * H:], pr[:, LV * H:NLOG + 2 * P + E]).then_inc(s_masks, 1)
                dve.wait_ge(s_cat32, 1)
                dve.tensor_copy(wcat_hi[:, :], wcr_t[:, :]).then_inc(s_cat32, 1)
                dve.tensor_copy(fwg_hi[:, :], fwg[:, :]).then_inc(s_cat32, 1)
                dve.wait_ge(s_cat32, 3)
                dve.tensor_tensor(wcat_lo[:, :], wcr_t[:, :], wcat_hi[:, :].bitcast(F32), ALU.subtract).then_inc(s_masks, 1)
                dve.tensor_tensor(fwg_lo[:, :], fwg[:, :], fwg_hi[:, :].bitcast(F32), ALU.subtract).then_inc(s_masks, 1)
                for n, (s_in, src) in enumerate(((s_m32, m32), (s_n32, n32))):
                    dve.wait_ge(s_in, 1)
                    v = src[:, :].rearrange("c (h n) -> c h n", h=H)
                    dve.tensor_copy(mn[:, :, 2 * n, :], v).then_inc(s_hi, 1)
                    dve.wait_ge(s_hi, n + 1)
                    dve.tensor_tensor(mn[:, :, 2 * n + 1, :], v, mn[:, :, 2 * n, :].bitcast(F32),
                                      ALU.subtract).then_inc(s_lo, 1)
                dve.wait_ge(s_small, n_small)
                dve.wait_ge(s_ones, 2)
                dve.tensor_copy(onesr[:, :], ones[:, :]).then_inc(s_masks, 1)
                dve.tensor_copy(be2[:, :], be_rows[:, :]).then_inc(s_be, 1)
                dve.wait_ge(s_be, 1)
                last_row = slice(BE - 1, BE)
                dve.tensor_tensor(be2[last_row, :], be_rows[last_row, :], be2[last_row, :].bitcast(F32),
                                  ALU.subtract).then_inc(s_masks, 1)
                dve.wait_ge(s_wet, 1)
                dve.tensor_copy(wet[:, :], pt[:, :]).then_inc(s_wet32, 1)
                dve.wait_ge(s_wet32, 1)
                dve.tensor_copy(wet_hi[:, :], wet[:, :]).then_inc(s_wet32, 1)
                dve.wait_ge(s_wet32, 2)
                dve.tensor_tensor(wet_lo[:, :], wet[:, :], wet_hi[:, :].bitcast(F32), ALU.subtract).then_inc(s_masks, 1)
                dve.wait_ge(s_masks, 10)


MEAN_VAR = 6


def mean_var(dve, b, stats, mv, ve, s_mv, s_ve, sign=1.0):
    base = b * MEAN_VAR
    even, odd = stats[:, :, 1], stats[:, :, 4]
    dve.tensor_tensor(mv[:, 1, :], even, odd, ALU.add).then_inc(s_mv, 1)
    dve.tensor_tensor(mv[:, 2, :], even, odd, ALU.subtract).then_inc(s_mv, 1)
    dve.tensor_tensor(mv[:, 3, :], stats[:, :, 2], stats[:, :, 5], ALU.add).then_inc(s_mv, 1)
    dve.wait_ge(s_mv, base + 3)
    dve.tensor_scalar(mv[:, 0, :], mv[:, 1, :], 0.5 * sign, None, ALU.mult).then_inc(s_mv, 1)
    dve.scalar_tensor_tensor(mv[:, 4, :], mv[:, 2, :], 0.25, mv[:, 2, :], ALU.mult, ALU.mult).then_inc(s_mv, 1)
    dve.tensor_scalar(mv[:, 5, :], mv[:, 3, :], 1.0 / D, EPS, ALU.mult, ALU.add).then_inc(s_mv, 1)
    dve.wait_ge(s_mv, base + MEAN_VAR)
    dve.tensor_tensor(ve[:, :], mv[:, 4, :], mv[:, 5, :], ALU.add).then_inc(s_ve, 1)


def token_stage(nc, x, table, mask, xt_dram, ea_dram, eb_dram, bias_dram, rows, wcat_hi, wcat_lo, c):
    with ExitStack() as ctx:
        def sb(name, shape, dt=F32):
            return ctx.enter_context(nc.sbuf_tensor(name, shape, dt))

        def sem(name):
            return ctx.enter_context(nc.semaphore(name))

        masks = sb("t_masks", [P, NMASK])
        xb = sb("t_x", [P, NC, P])
        stats = sb("t_stats", [P, NC, 6])
        mv = sb("t_mv", [P, 6, NC])
        ve = sb("t_ve", [P, NC])
        mhalf = sb("t_mhalf", [P, NC])
        rstd = sb("t_rstd", [P, NC])
        xn = sb("t_xn", [P, NC, P])
        xt_hi = [sb(f"t_xt_hi{k}", [P, T], F32R) for k in range(2)]
        xt_lo = [sb(f"t_xt_lo{k}", [P, T], F32R) for k in range(2)]
        z = sb("t_z", [P, NC, NLOG])
        az = sb("t_az", [P, NC, NLOG])
        ez = sb("t_ez", [P, NC, NLOG])
        lz = sb("t_lz", [P, NC, NLOG])
        lam = sb("t_lam", [P, NC, NLOG])
        lamc = sb("t_lamc", [P, NC, NLV * H])
        g = sb("t_g", [P, NC, H])
        sums = sb("t_sums", [P, 3, NC, H])
        run = sb("t_run", [P, NC, H])
        bias = [sb(f"t_bias{k}", [P, H, NT]) for k in range(2)]
        lnl = sb("t_lnl", [P, NC, NLV * H])
        ell = sb("t_ell", [P, NC, NLV * H])
        onesq = sb("t_ones", [P, P])
        elt_hi = [sb(f"t_elt_hi{k}", [NLV * H, T], F16) for k in range(2)]
        elt_lo = [sb(f"t_elt_lo{k}", [NLV * H, T], F16) for k in range(2)]
        p_xt = ctx.enter_context(nc.psum_tensor("p_xt", [P, T], F32))
        p_z = ctx.enter_context(nc.psum_tensor("p_z", [P, 2, 512], F32))
        p_el = ctx.enter_context(nc.psum_tensor("p_el", [P, T], F32))
        p_g = ctx.enter_context(nc.psum_tensor("p_g", [P, 512], F32))

        names = ("x_in stats mv ve rstd xn xt hi lo logit z az ez lz lam g sums_mm sums run bias lamc lnl "
                 "ell elt el_hi el_lo ones").split()
        s = {n: sem(f"t_{n}") for n in names}
        xt_stored, bias_stored, el_stored = ([sem(f"t_{n}{k}") for k in range(2)]
                                             for n in ("xt_stored", "bias_stored", "el_stored"))
        XT, BI, EL = 2 * 16, 16, 4 * 16
        masks_in, masks_done = sem("t_masks_in"), sem("t_masks_done")
        na = LOW * H
        half = NC // 2

        def permuted(t, r0, r1, q):
            return t[r0:r1, :].rearrange("r (q n) -> r q n", q=q)

        def sequences(eng, step):
            with eng.Fori(0, B // 2 - 1) as p:
                for k in range(2):
                    step(p * 2 + k, k, p, True, True)
            step(B - 2, 0, B // 2 - 1, True, False)
            step(B - 1, 1, B // 2 - 1, False, False)

        with nc.Block() as block:
            @block.sync
            def _(sp):
                def load(b):
                    sp.dma_start(xb[:, :, :], x[b].rearrange("(i t) c -> t i c", i=NC)).then_inc(s["x_in"], 16)

                def store_xt(n, k):
                    sp.wait_ge(s["lo"], n + 1)
                    sp.dma_start(xt_dram[n, 0], xt_hi[k][:, :].bitcast(F32)).then_inc(xt_stored[k], 16)
                    sp.dma_start(xt_dram[n, 1], xt_lo[k][:, :].bitcast(F32)).then_inc(xt_stored[k], 16)

                def step(b, k, p, next_, after):
                    if after:
                        sp.wait_ge(s["xn"], (b + 2) * NC)
                        load(b + 2)
                    sp.wait_ge(s["bias"], (b + 1) * NC)
                    sp.dma_start(bias_dram[bass.ds(b * H, H)].rearrange("h s k -> s h k"),
                                 bias[k][:, :, :]).then_inc(bias_stored[k], 16)
                    if next_:
                        store_xt(b + 1, 1 - k)
                    sp.wait_ge(s["el_lo"], (b + 1) * 2)
                    for part, src in ((0, elt_hi[k]), (1, elt_lo[k])):
                        sp.dma_start(ea_dram[b, part], src[0:na, :]).then_inc(el_stored[k], 16)
                        sp.dma_start(eb_dram[b, part], src[na:NLV * H, :]).then_inc(el_stored[k], 16)

                load(0)
                sp.wait_ge(s["xn"], NC)
                load(1)
                store_xt(0, 0)
                sp.dma_start(masks[:, :], table[:, 0:NMASK]).then_inc(masks_in, 16)
                sequences(sp, step)
                for k in range(2):
                    sp.wait_ge(xt_stored[k], XT * (B // 2 + 1))
                    sp.wait_ge(bias_stored[k], BI * (B // 2 + 1))
                    sp.wait_ge(el_stored[k], EL * (B // 2 + 1))

            @block.gpsimd
            def _(pool):
                pool.memset(mhalf[:, :], -0.5).then_inc(s["ones"], 1)
                for k in range(2):
                    pool.sem_inc(xt_stored[k], XT)
                    pool.sem_inc(bias_stored[k], BI)
                    pool.sem_inc(el_stored[k], EL)
                pool.wait_ge(s["ones"], 2)
                with pool.Fori(0, B) as b:
                    pool.wait_ge(s["ve"], b + 1)
                    pool.tensor_tensor(rstd[:, :], ve[:, :], mhalf[:, :], ALU.pow).then_inc(s["rstd"], 1)
                pool.wait_ge(masks_in, 16)
                pool.tensor_copy(mask[:, :], masks[:, :]).then_inc(masks_done, 1)
                pool.wait_ge(masks_done, 1)

            @block.vector
            def _(dve):
                def statistics(n):
                    dve.wait_ge(s["x_in"], (n + 1) * 16)
                    for i in range(NC):
                        dve.bn_stats(stats[:, i, :], xb[:, i, :]).then_inc(s["stats"], 1)
                    dve.wait_ge(s["stats"], (n + 1) * NC)
                    mean_var(dve, n, stats, mv, ve, s["mv"], s["ve"])

                def normalise(n):
                    dve.wait_ge(s["rstd"], n + 1)
                    for i in range(NC):
                        dve.tensor_scalar(xn[:, i, :], xb[:, i, :], mv[:, 0, i:i + 1], rstd[:, i:i + 1],
                                          ALU.subtract, ALU.mult).then_inc(s["xn"], 1)

                def low(n, k):
                    dve.wait_ge(s["hi"], n + 1)
                    dve.tensor_tensor(xt_lo[k][:, :], p_xt[:, :], xt_hi[k][:, :].bitcast(F32), ALU.subtract).then_inc(s["lo"], 1)

                def add_biases(n):
                    dve.wait_ge(s["logit"], n + 1)
                    for f in range(2):
                        dve.tensor_tensor(z[:, f * half:(f + 1) * half, :],
                                          p_z[:, f, 0:half * NLOG].rearrange("p (i n) -> p i n", i=half),
                                          rows[:, None, 0:NLOG].broadcast_to([P, half, NLOG]), ALU.add).then_inc(s["z"], 1)

                def softplus(b):
                    dve.wait_ge(s["lz"], b + 1)
                    dve.scalar_tensor_tensor(lam[:, :, :], z[:, :, :], 0.0, lz[:, :, :], ALU.max, ALU.add).then_inc(s["lam"], 1)
                    dve.wait_ge(s["lam"], b + 1)
                    dve.tensor_scalar(g[:, :, :], lam[:, :, LV * H:NLOG], -1.0, None, ALU.mult).then_inc(s["g"], 1)
                    dve.tensor_scalar(lamc[:, :, :], lam[:, :, 0:NLV * H], 1e-19, None, ALU.max).then_inc(s["lamc"], 1)

                def decays(b, k, p):
                    dve.wait_ge(s["sums_mm"], b + 1)
                    dve.tensor_copy(sums[:, :, :, :].rearrange("p k i h -> p (k i h)"), p_g[:, 0:3 * NC * H]).then_inc(s["sums"], 1)
                    dve.wait_ge(s["sums"], b + 1)
                    dve.wait_ge(bias_stored[k], BI * (p + 1))
                    by_head = sums[:, :, :, :].rearrange("p k i h -> p k h i")
                    dve.tensor_scalar(bias[k][:, :, 0:NC], by_head[:, 0], -1.0, -FLOOR, ALU.mult, ALU.min).then_inc(s["bias"], 1)
                    dve.tensor_scalar(run[:, :, :], sums[:, 0], FLOOR, None, ALU.max).then_inc(s["run"], 1)
                    dve.tensor_copy(bias[k][:, :, BIAS_AT[1]:BIAS_AT[1] + NC - 1], by_head[:, 1, :, 0:NC - 1]).then_inc(s["bias"], 1)
                    for d in range(2, NC):
                        n = NC - d
                        dve.wait_ge(s["bias"], b * NC + d)
                        dve.tensor_tensor(bias[k][:, :, BIAS_AT[d]:BIAS_AT[d] + n],
                                          bias[k][:, :, BIAS_AT[d - 1]:BIAS_AT[d - 1] + n],
                                          by_head[:, 2, :, d - 1:NC - 1], ALU.add).then_inc(s["bias"], 1)

                def level_logs(b):
                    dve.wait_ge(s["lnl"], b + 1)
                    dve.wait_ge(s["run"], b + 1)
                    for f in range(2):
                        i0 = f * half
                        for l0, l1, at in ((0, LOW, 0), (LOW, NLV, na)):
                            n_l = l1 - l0
                            dve.tensor_tensor(ell[:, i0:i0 + half, at:at + n_l * H].rearrange("p i (h l) -> p i l h", h=H),
                                              lnl[:, i0:i0 + half, l0 * H:l1 * H].rearrange("p i (l h) -> p i l h", h=H),
                                              run[:, i0:i0 + half, None, :].broadcast_to([P, half, n_l, H]),
                                              ALU.add).then_inc(s["ell"], 1)

                def low_logs(b, k):
                    for f, (r0, r1, q) in enumerate(((0, na, TA), (na, NLV * H, TB))):
                        dve.wait_ge(s["el_hi"], b * 2 + f + 1)
                        dve.tensor_tensor(permuted(elt_lo[k], r0, r1, q),
                                          p_el[r0:r1, :].rearrange("r (n q) -> r q n", q=q),
                                          permuted(elt_hi[k], r0, r1, q), ALU.subtract).then_inc(s["el_lo"], 1)

                def step(b, k, p, next_, after):
                    if next_:
                        statistics(b + 1)
                    softplus(b)
                    if next_:
                        normalise(b + 1)
                    decays(b, k, p)
                    level_logs(b)
                    if next_:
                        low(b + 1, 1 - k)
                    low_logs(b, k)
                    if next_:
                        add_biases(b + 1)

                dve.memset(onesq[:, :], 1.0).then_inc(s["ones"], 1)
                statistics(0)
                normalise(0)
                low(0, 0)
                add_biases(0)
                sequences(dve, step)

            @block.scalar
            def _(act):
                def high(n, k, fills):
                    act.wait_ge(s["xt"], n + 1)
                    act.wait_ge(xt_stored[k], XT * (fills + 1))
                    act.activation(xt_hi[k][:, :], p_xt[:, :], ACT.Copy).then_inc(s["hi"], 1)

                def step(b, k, p, next_, after):
                    act.wait_ge(s["z"], (b + 1) * 2)
                    act.activation(az[:, :, :], z[:, :, :], ACT.Abs).then_inc(s["az"], 1)
                    act.wait_ge(s["az"], b + 1)
                    act.activation(ez[:, :, :], az[:, :, :], ACT.Exp, scale=-1.0).then_inc(s["ez"], 1)
                    act.wait_ge(s["ez"], b + 1)
                    act.activation(lz[:, :, :], ez[:, :, :], ACT.Ln, bias=1.0).then_inc(s["lz"], 1)
                    act.wait_ge(s["lamc"], b + 1)
                    act.activation(lnl[:, :, :], lamc[:, :, :], ACT.Ln).then_inc(s["lnl"], 1)
                    if next_:
                        high(b + 1, 1 - k, p + k)
                    act.wait_ge(s["elt"], b + 1)
                    act.wait_ge(el_stored[k], EL * (p + 1))
                    for r0, r1, q in ((0, na, TA), (na, NLV * H, TB)):
                        act.activation(permuted(elt_hi[k], r0, r1, q),
                                       p_el[r0:r1, :].rearrange("r (n q) -> r q n", q=q), ACT.Copy).then_inc(s["el_hi"], 1)

                high(0, 0, 0)
                sequences(act, step)

            @block.tensor
            def _(pe):
                def transpose_x(n):
                    pe.wait_ge(s["xn"], (n + 1) * NC)
                    for i in range(NC):
                        last = pe.transpose(p_xt[:, i * P:(i + 1) * P], xn[:, i, :], c("ident"))
                    last.then_inc(s["xt"], 1)

                def logits(n, k):
                    pe.wait_ge(s["hi"], n + 1)
                    pe.wait_ge(s["lo"], n + 1)
                    for i in range(NC):
                        o = p_z[:, i // half, (i % half) * NLOG:(i % half + 1) * NLOG]
                        hi, lo = xt_hi[k][:, i * P:(i + 1) * P], xt_lo[k][:, i * P:(i + 1) * P]
                        pe.matmul(o, hi, wcat_hi[:, :], start=True, stop=False)
                        pe.matmul(o, hi, wcat_lo[:, :], start=False, stop=False)
                        last = pe.matmul(o, lo, wcat_hi[:, :], start=False, stop=True)
                    last.then_inc(s["logit"], 1)

                def step(b, k, p, next_, after):
                    pe.wait_ge(s["g"], b + 1)
                    gv = g[:, :, :].rearrange("p i h -> p (i h)")
                    for f, w in enumerate((c("tri"), c("suf"), onesq[:, :])):
                        last = pe.matmul(p_g[:, f * NC * H:(f + 1) * NC * H], w, gv, start=True, stop=True)
                    last.then_inc(s["sums_mm"], 1)
                    if next_:
                        transpose_x(b + 1)
                    pe.wait_ge(s["ell"], (b + 1) * 4)
                    for i in range(NC):
                        last = pe.transpose(p_el[0:NLV * H, i * P:(i + 1) * P], ell[:, i, :], c("ident"))
                    last.then_inc(s["elt"], 1)
                    if next_:
                        logits(b + 1, 1 - k)

                pe.wait_ge(s["ones"], 2)
                transpose_x(0)
                logits(0, 0)
                sequences(pe, step)


def attention_stage(nc, m_dram, n_dram, xt_dram, ea_dram, eb_dram, bias_dram, yt_dram, m, c, negm, identb, identr):
    with ExitStack() as ctx:
        def sb(name, shape, dt=F32):
            return ctx.enter_context(nc.sbuf_tensor(name, shape, dt))

        def pb(name, shape):
            return ctx.enter_context(nc.psum_tensor(name, shape, F32))

        def sem(name):
            return ctx.enter_context(nc.semaphore(name))

        xp = [sb(f"xp{k}", [P, T], F32R) for k in range(2)]
        xs = [sb(f"xs{k}", [P, T], F32R) for k in range(2)]
        mt = [sb(f"mt{k}", [P, 2, P], F32R) for k in range(2)]
        nt = sb("nt", [P, 2, 2, P], F32R)
        ea = [sb(f"ea{k}", [P, P], F16) for k in range(2)]
        eb = [sb(f"eb{k}", [KB, NC * NTB], F16) for k in range(2)]
        bias = [sb(f"bias{k}", [P, NT]) for k in range(2)]
        ra = [sb(f"ra{k}", [P, NC, NTA, TA], F16) for k in range(2)]
        rb = [sb(f"rb{k}", [KB, NC, NTB, TB], F16) for k in range(2)]
        q_hi = [sb(f"q_hi{k}", [P, T], F32R) for k in range(2)]
        q_lo = [sb(f"q_lo{k}", [P, T], F32R) for k in range(2)]
        v_hi = [sb(f"v_hi{k}", [P, 2, NC, P], F32R) for k in range(2)]
        v_lo = [sb(f"v_lo{k}", [P, 2, NC, P], F32R) for k in range(2)]
        w = [sb(f"w{k}", [P, NT, P]) for k in range(2)]
        LAG = 4
        NA = LAG + 1
        TAIL = NG - 3
        a = [sb(f"a{k}", [P, 512]) for k in range(NA)]
        a_hi = [sb(f"a_hi{k}", [P, 512], F32R) for k in range(NA)]
        a_lo = [sb(f"a_lo{k}", [P, 512], F32R) for k in range(NA)]
        yt = sb("yt", [P, T])
        o_ps = pb("o_ps", [P, T])
        s_ps = pb("s_ps", [P, 2, 512])
        l_ps = pb("l_ps", [P, 2, 512])
        q_ps = pb("q_ps", [P, 512])
        v_ps = pb("v_ps", [P, 512])

        xp_in = sem("xp_in")
        xs_in = [sem(f"xs_in{j}") for j in range(NC)]
        e_in = [sem(f"e_in{k}") for k in range(2)]
        m_in = [sem(f"m_in{k}") for k in range(2)]
        n_in = sem("n_in")
        ra_ready, rb_ready = sem("ra_ready"), sem("rb_ready")
        l_mm, w_done = sem("l_mm"), sem("w_done")
        q_mm, q_hi_done, q_done = sem("q_mm"), sem("q_hi_done"), sem("q_done")
        v_mm, v_hi_done, v_done = sem("v_mm"), sem("v_hi_done"), sem("v_done")
        s_mm, a_done, a_hi_done, a_lo_done, a_tail_done, head_done = (
            sem(n) for n in ("s_mm", "a_done", "a_hi_done", "a_lo_done", "a_tail_done", "head_done"))
        y_done, y_out = sem("y_done"), sem("y_out")
        E_IN = 5 * 16
        dma_a = c("dma")
        dma_b = c("dmb", KB)

        EVEN = {0: [("u", 0)], 1: [("q", 0)], 3: [("u", 1)], 4: [("q", 1)], 5: [("u", 2)], 7: [("u", 3)], 10: [("u", 4)]}
        ODD = EVEN | {2: [("v", 0)], 6: [("v", 1)], 8: [("v", 2)], 11: [("v", 3)]}
        PIECES = (EVEN, ODD)
        ALL = [piece for g in sorted(ODD) for piece in ODD[g]]
        EXPAND_A, EXPAND_B = 0, 4
        V_LOW = {4: 0, 7: 1, 9: 2, 11: 3}
        Q_PARTS = {2: 0, 5: 1}
        ACT_KINDS = "uv"
        NV = 4
        Q = 4
        assert H // Q == 2
        ENDS = [max(g for g in range(NG) if GROUPS[g][0] == j) + 1 for j in range(NC)]

        with nc.Block() as block:
            @block.sync
            def _(sp):
                def load_e(k, b, h):
                    for part in range(2):
                        sp.dma_start(ea[k][part * LOW * TA:(part + 1) * LOW * TA, :],
                                     ea_dram[b, part, bass.ds(h * LOW, LOW), :]
                                     .rearrange("l (q n) -> (l q) n", q=TA)).then_inc(e_in[k], 16)
                        sp.dma_start(eb[k][part * HIGH * TB:(part + 1) * HIGH * TB, :],
                                     eb_dram[b, part, bass.ds(h * HIGH, HIGH), :]
                                     .rearrange("l (q n) -> (l q) n", q=TB)).then_inc(e_in[k], 16)
                    sp.dma_start(bias[k][:, :], bias_dram[b * H + h]).then_inc(e_in[k], 16)

                def load_m(k, h):
                    sp.dma_start(mt[k][:, :, :].bitcast(F32), m_dram[h]).then_inc(m_in[k], 16)

                def load_n(g):
                    sp.dma_start(nt[:, :, :, :].bitcast(F32), n_dram[g]).then_inc(n_in, 16)

                def load_xp(b):
                    for k in range(2):
                        sp.dma_start(xp[k][:, :].bitcast(F32), xt_dram[b, k]).then_inc(xp_in, 16)

                def load_xs(b, j):
                    for k in range(2):
                        sp.dma_start(xs[k][:, j * P:(j + 1) * P].bitcast(F32),
                                     xt_dram[b, k, :, j * P:(j + 1) * P]).then_inc(xs_in[j], 16)

                def heads(b, last):
                    with sp.Fori(0, H // 2 - 1) as hp:
                        for k in range(2):
                            n = b * H + hp * 2 + k
                            sp.wait_ge(w_done, NU * (n + 1))
                            load_e(k, b, hp * 2 + k + 2)
                            sp.wait_ge(q_done, 2 * (n + 1))
                            load_m(k, hp * 2 + k + 2)
                            if k == 0:
                                sp.wait_ge(v_done, NV * (b * (H // 2) + hp + 1))
                                load_n(hp + 1)
                    sp.wait_ge(w_done, NU * (b * H + H - 1))
                    if last:
                        load_e(0, 0, 0)
                        sp.wait_ge(q_done, 2 * (b * H + H - 1))
                        load_m(0, 0)
                        sp.wait_ge(v_done, NV * (H // 2) * (b + 1))
                        load_n(0)
                        sp.sem_inc(xp_in, 32)
                        return
                    load_e(0, b + 1, 0)
                    sp.wait_ge(q_done, 2 * (b * H + H - 1))
                    load_m(0, 0)
                    sp.wait_ge(v_done, NV * (H // 2) * (b + 1))
                    load_n(0)
                    sp.wait_ge(q_mm, 2 * (b * H + H))
                    load_xp(b + 1)
                    sp.wait_ge(w_done, NU * (b * H + H))
                    load_e(1, b + 1, 1)
                    load_m(1, 1)
                    for j in range(NC):
                        sp.wait_ge(s_mm, (b * H + H - 1) * NG + ENDS[j])
                        load_xs(b + 1, j)

                load_xp(0)
                load_e(0, 0, 0)
                load_m(0, 0)
                load_n(0)
                load_e(1, 0, 1)
                load_m(1, 1)
                for j in range(NC):
                    load_xs(0, j)
                with sp.Fori(0, B - 1) as b:
                    heads(b, False)
                    sp.wait_ge(y_done, 2 * (b + 1))
                    sp.dma_start(yt_dram[b], yt[:, :]).then_inc(y_out, 16)
                heads(B - 1, True)
                sp.wait_ge(y_done, 2 * B)
                sp.dma_start(yt_dram[B - 1], yt[:, :]).then_inc(y_out, 16)
                sp.wait_ge(y_out, 16 * (B + 1))

            @block.gpsimd
            def _(pool):
                def expand_a(k, fills):
                    pool.wait_ge(e_in[k], E_IN * fills)
                    pool.tensor_tensor(ra[k][:, :, :, :].rearrange("p i n q -> p (i n) q"),
                                       ea[k][:, :, None].broadcast_to([P, P, TA]),
                                       dma_a[:, None, :].broadcast_to([P, P, TA]), ALU.mult).then_inc(ra_ready, 1)

                def expand_b(k):
                    pool.tensor_tensor(rb[k][:, :, :, :].rearrange("p i n q -> p (i n) q"),
                                       eb[k][:, :, None].broadcast_to([KB, NC * NTB, TB]),
                                       dma_b[:, None, :].broadcast_to([KB, NC * NTB, TB]), ALU.mult).then_inc(rb_ready, 1)

                def head(n, k, fills):
                    for g, (j, t0, t1) in enumerate(GROUPS[:TAIL]):
                        pool.wait_ge(a_hi_done, n * NG + g + 1)
                        pool.tensor_tensor(a_lo[g % NA][:, 0:t1 - t0], a[g % NA][:, 0:t1 - t0],
                                           a_hi[g % NA][:, 0:t1 - t0].bitcast(F32), ALU.subtract).then_inc(a_lo_done, 1)
                        if g == EXPAND_A and fills is not None:
                            pool.wait_ge(l_mm, NU * (n + 1))
                            expand_a(k, fills)
                        if g == EXPAND_B and fills is not None:
                            expand_b(k)

                for k in range(2):
                    expand_a(k, 1)
                    expand_b(k)
                with pool.Fori(0, NH // 2 - 1) as p:
                    for k in range(2):
                        head(p * 2 + k, k, p + 2)
                head(NH - 2, 0, NH // 2 + 1)
                head(NH - 1, 1, None)

            @block.scalar
            def _(act):
                def piece(kind, u, k, n):
                    if kind == "u":
                        act.wait_ge(l_mm, n * NU + u + 1)
                        slot = 0
                        for d, i0, cnt in UNITS[u]:
                            for i in range(i0, i0 + cnt):
                                for dd in (range(d, i + 1) if d == 5 else (d,)):
                                    j = i - dd
                                    last = act.activation(
                                        w[k][:, W_AT[j] + dd, :].rearrange("p (f c) -> p f c", f=2),
                                        l_ps[:, :, slot * HF:(slot + 1) * HF], ACT.Exp,
                                        bias=bias[k][:, BIAS_AT[dd] + j:BIAS_AT[dd] + j + 1])
                                slot += 1
                        last.then_inc(w_done, 1)
                    else:
                        act.wait_ge(v_mm, NV * n + u + 1)
                        act.activation(v_hi[k][:, :, 2 * u:2 * u + 2, :].rearrange("p e j n -> p j e n"),
                                       v_ps[:, :].rearrange("p (j e n) -> p j e n", j=2, e=2),
                                       ACT.Copy).then_inc(v_hi_done, 1)

                act.wait_ge(e_in[0], E_IN)
                for kind, u in ALL:
                    if kind in ACT_KINDS:
                        piece(kind, u, 0, 0)
                with act.Fori(0, NH // Q) as p:
                    for k in range(Q):
                        act.wait_ge(e_in[(k + 1) % 2], E_IN * (p * (Q // 2) + (k + 1) // 2 + 1))
                        act.wait_ge(a_done, NG * (p * Q + k) + 1)
                        for g in range(NG):
                            for kind, u in PIECES[k % 2].get(g, ()):
                                if kind not in ACT_KINDS:
                                    continue
                                if kind == "u":
                                    piece(kind, u, (k + 1) % 2, p * Q + k + 1)
                                else:
                                    piece(kind, u, (k // 2 + 1) % 2, p * (Q // 2) + k // 2 + 1)

            @block.vector
            def _(dve):
                def high(u, k, n):
                    dve.wait_ge(q_mm, 2 * n + u + 1)
                    dve.tensor_copy(q_hi[k][:, u * 512:(u + 1) * 512], q_ps[:, :]).then_inc(q_hi_done, 1)

                def low(u, k, n):
                    dve.wait_ge(q_hi_done, 2 * n + u + 1)
                    dve.tensor_tensor(q_lo[k][:, u * 512:(u + 1) * 512], q_ps[:, :],
                                      q_hi[k][:, u * 512:(u + 1) * 512].bitcast(F32), ALU.subtract).then_inc(q_done, 1)

                def low_v(u, k, n):
                    dve.wait_ge(v_hi_done, NV * n + u + 1)
                    dve.tensor_tensor(v_lo[k][:, :, 2 * u:2 * u + 2, :].rearrange("p e j n -> p j e n"),
                                      v_ps[:, :].rearrange("p (j e n) -> p j e n", j=2, e=2),
                                      v_hi[k][:, :, 2 * u:2 * u + 2, :].bitcast(F32).rearrange("p e j n -> p j e n"),
                                      ALU.subtract).then_inc(v_done, 1)

                dve.sem_inc(y_out, 16)
                for kind, u in ALL:
                    if kind == "q":
                        high(u, 0, 0)
                        low(u, 0, 0)
                    elif kind == "v":
                        low_v(u, 0, 0)
                with dve.Fori(0, B) as b:
                    with dve.Fori(0, H // Q) as hp:
                        for k in range(Q):
                            n = b * H + hp * Q + k
                            dve.wait_ge(w_done, (n + 1) * NU)
                            for g, (j, t0, t1) in enumerate(GROUPS):
                                dve.wait_ge(s_mm, n * NG + g + 1)
                                at = W_AT[j] + t0 // P - j
                                dve.tensor_tensor(a[g % NA][:, 0:t1 - t0], s_ps[:, g % 2, 0:t1 - t0],
                                                  w[k % 2][:, at:at + (t1 - t0) // P, :].rearrange("p i n -> p (i n)"),
                                                  ALU.mult).then_inc(a_done, 1)
                                dve.wait_ge(a_done, n * NG + g + 1)
                                dve.tensor_copy(a_hi[g % NA][:, 0:t1 - t0], a[g % NA][:, 0:t1 - t0]).then_inc(a_hi_done, 1)
                                if g >= TAIL:
                                    dve.wait_ge(a_hi_done, n * NG + g + 1)
                                    dve.tensor_tensor(a_lo[g % NA][:, 0:t1 - t0], a[g % NA][:, 0:t1 - t0],
                                                      a_hi[g % NA][:, 0:t1 - t0].bitcast(F32),
                                                      ALU.subtract).then_inc(a_tail_done, 1)
                                if g in Q_PARTS:
                                    high(Q_PARTS[g], (k + 1) % 2, n + 1)
                                    low(Q_PARTS[g], (k + 1) % 2, n + 1)
                                if k % 2 and g in V_LOW:
                                    pair = b * (H // 2) + hp * (Q // 2) + k // 2
                                    low_v(V_LOW[g], (k // 2 + 1) % 2, pair + 1)
                    dve.wait_ge(head_done, H * (b + 1))
                    dve.wait_ge(y_out, 16 * (b + 1))
                    for f in range(2):
                        dve.tensor_copy(yt[:, f * 512:(f + 1) * 512], o_ps[:, f * 512:(f + 1) * 512]).then_inc(y_done, 1)

            @block.tensor
            def _(pe):
                def piece(kind, u, k, n, loads, first):
                    if kind == "u":
                        if u == 0:
                            pe.wait_ge(ra_ready, n + 1)
                        if u == 1:
                            pe.wait_ge(rb_ready, n + 1)
                        if not (first and u == 0):
                            pe.wait_ge(w_done, n * NU + u)
                        unit(u, k).then_inc(l_mm, 1)
                    elif kind == "q":
                        if u == 0:
                            pe.wait_ge(m_in[k], 16 * loads)
                        if not (first and u == 0):
                            pe.wait_ge(q_done, 2 * n + u)
                        cols = slice(u * 512, (u + 1) * 512)
                        pe.matmul(q_ps[:, :], mt[k][:, 0, :], xp[0][:, cols], start=True, stop=False)
                        pe.matmul(q_ps[:, :], mt[k][:, 0, :], xp[1][:, cols], start=False, stop=False)
                        pe.matmul(q_ps[:, :], mt[k][:, 1, :], xp[0][:, cols], start=False, stop=True).then_inc(q_mm, 1)
                    else:
                        if u == 0:
                            pe.wait_ge(n_in, 16 * loads)
                        if not (first and u == 0):
                            pe.wait_ge(v_done, NV * n + u)
                        n_hi, n_lo = (nt[:, part, :, :].rearrange("p e n -> p (e n)") for part in range(2))
                        for jj in range(2):
                            keys = slice((2 * u + jj) * P, (2 * u + jj + 1) * P)
                            o = v_ps[:, jj * 2 * P:(jj + 1) * 2 * P]
                            pe.matmul(o, xp[0][:, keys], n_hi, start=True, stop=False)
                            pe.matmul(o, xp[0][:, keys], n_lo, start=False, stop=False)
                            last = pe.matmul(o, xp[1][:, keys], n_hi, start=False, stop=True)
                        last.then_inc(v_mm, 1)

                def unit(u, k):
                    started = [False, False]
                    slot = 0
                    last = None

                    def mm(f, o, lhsT, rhs):
                        r = pe.matmul(o, lhsT, rhs, start=not started[f], stop=True, skip_group_check=True)
                        started[f] = True
                        return r

                    for d, i0, cnt in UNITS[u]:
                        bank = [l_ps[:, f, slot * HF:(slot + cnt) * HF].rearrange("p (i c) -> p i c", i=cnt)
                                for f in range(2)]
                        if d == 0:
                            for f in range(2):
                                last = mm(f, bank[f], negm[:, :],
                                          identb[:, None, f * HF:(f + 1) * HF].broadcast_to([P, cnt, HF]))
                        if d <= 1:
                            for tb in range(NTA):
                                f, at = divmod(tb * TA, HF)
                                last = mm(f, bank[f][:, :, at:at + TA], m(f"ma{d}")[:, tb * P:(tb + 1) * P],
                                          ra[k][:, i0:i0 + cnt, tb, :])
                        if d in (1, 2, 4):
                            for tb in range(NTB):
                                f, at = divmod(tb * TB, HF)
                                last = mm(f, bank[f][:, :, at:at + TB], m(f"mb{d}", KB)[:, tb * P:(tb + 1) * P],
                                          rb[k][:, i0:i0 + cnt, tb, :])
                        if d in (3, 5):
                            for f in range(2):
                                last = mm(f, bank[f], m("m9" if d == 3 else "m10", KB),
                                          rb[k][:, i0:i0 + cnt, f * NTB // 2:(f + 1) * NTB // 2, :].rearrange(
                                              "p i n q -> p i (n q)"))
                        slot += cnt
                    return last

                def scores(n, k, b, g):
                    j, t0, t1 = GROUPS[g]
                    if g == 0 or GROUPS[g - 1][0] != j:
                        pe.wait_ge(xs_in[j], 32 * (b + 1))
                    if g < 2:
                        pe.wait_ge(q_done, 2 * n + g + 1)
                    if g >= 2:
                        pe.wait_ge(a_done, n * NG + g - 1)
                    o = s_ps[:, g % 2, 0:t1 - t0]
                    keys = slice(j * P, (j + 1) * P)
                    pe.matmul(o, xs[0][:, keys], q_hi[k][:, t0:t1], start=True, stop=False)
                    pe.matmul(o, xs[0][:, keys], q_lo[k][:, t0:t1], start=False, stop=False)
                    pe.matmul(o, xs[1][:, keys], q_hi[k][:, t0:t1], start=False, stop=True).then_inc(s_mm, 1)

                def values(n, k, pair, g):
                    j, t0, t1 = GROUPS[g]
                    if g < TAIL:
                        pe.wait_ge(a_lo_done, n * TAIL + g + 1)
                    else:
                        pe.wait_ge(a_tail_done, n * (NG - TAIL) + g - TAIL + 1)
                    if k % 2 == 0 and g == 0:
                        pe.wait_ge(v_done, NV * (pair + 1))
                    v_h, v_l = (t[k // 2 % 2][:, k % 2, j, :] for t in (v_hi, v_lo))
                    for lhs, rhs in ((v_h, a_hi), (v_h, a_lo), (v_l, a_hi)):
                        last = pe.matmul(o_ps[:, t0:t1], lhs, rhs[g % NA][:, 0:t1 - t0],
                                         start=False, stop=True, skip_group_check=True)
                    return last

                def residual(b):
                    for f in range(2):
                        if b is not None:
                            pe.wait_ge(y_done, 2 * b + f + 1)
                        o = o_ps[:, f * 512:(f + 1) * 512]
                        for part in range(2):
                            pe.matmul(o, identr[:, :], xp[part][:, f * 512:(f + 1) * 512], start=(part == 0),
                                      stop=True, skip_group_check=True)

                pe.wait_ge(xp_in, 32)
                for kind, u in ALL:
                    piece(kind, u, 0, 0, 1, True)
                residual(None)
                with pe.Fori(0, B) as b:
                    with pe.Fori(0, H // Q) as hp:
                        for k in range(Q):
                            n = b * H + hp * Q + k
                            pair = b * (H // 2) + hp * (Q // 2) + k // 2
                            for g in range(NG):
                                scores(n, k % 2, b, g)
                                if g >= LAG:
                                    values(n, k, pair, g - LAG)
                                for kind, u in PIECES[k % 2].get(g, ()):
                                    if kind == "q" and u == 0 and k == Q - 1:
                                        pe.wait_ge(xp_in, 32 * (b + hp + 1))
                                    if kind == "v":
                                        piece(kind, u, (k // 2 + 1) % 2, pair + 1, pair + 2, False)
                                    else:
                                        piece(kind, u, (k + 1) % 2, n + 1, pair + 1 + k % 2, False)
                            for g in range(NG - LAG, NG):
                                last = values(n, k, pair, g)
                            last.then_inc(head_done, 1)
                    residual(b)


def expert_stage(nc, x, yt_dram, out, rows, wet_hi, wet_lo, fwg_hi, fwg_lo, be2, onesr, c):
    with ExitStack() as ctx:
        def sb(name, shape, dt=F32):
            return ctx.enter_context(nc.sbuf_tensor(name, shape, dt))

        def sem(name):
            return ctx.enter_context(nc.semaphore(name))

        yt = sb("e_yt", [P, T])
        xb = sb("e_x", [P, NC, P])
        st1, st2 = (sb(f"e_st{k}", [P, NC, 6]) for k in range(2))
        mv1, mv2 = (sb(f"e_mv{k}", [P, 6, NC]) for k in range(2))
        ve1, ve2 = (sb(f"e_ve{k}", [P, NC]) for k in range(2))
        rs1, rs2 = (sb(f"e_rs{k}", [P, NC]) for k in range(2))
        sh1, sh2 = (sb(f"e_sh{k}", [P, NC]) for k in range(2))
        r0 = sb("e_r0", [P, NC, P])
        r1 = sb("e_r1", [P, NC, P])
        r2 = sb("e_r2", [P, NC, P])
        x1 = [sb(f"e_x1{k}", [P, NC, P]) for k in range(2)]
        x2 = sb("e_x2", [P, NC, P])
        x2t_hi = [sb(f"e_x2t_hi{k}", [P, T], F32R) for k in range(2)]
        x2t_lo = [sb(f"e_x2t_lo{k}", [P, T], F32R) for k in range(2)]
        gl = [sb(f"e_g{k}", [P, NC, E]) for k in range(12)]
        gm = [sb(f"e_m{k}", [P, NC]) for k in range(6)]
        mhalf = sb("e_mhalf", [P, NC])
        part = sb("e_part", [P, NC, P])
        acc_a = [sb(f"e_acc_a{k}", [P, NC, P]) for k in range(2)]
        acc_b = [sb(f"e_acc_b{k}", [P, NC, P]) for k in range(2)]
        total = sb("e_total", [P, NC, P])
        p_y = ctx.enter_context(nc.psum_tensor("e_py", [P, NC, P], F32))
        p_t = ctx.enter_context(nc.psum_tensor("e_pt", [P, T], F32))
        p_e = ctx.enter_context(nc.psum_tensor("e_pe", [P, 2, E, P], F32))

        names = ("mhalf y_in x_in y_t st1 mv1 ve1 rs1 sh1 r0 r1 r2 x1 st2 mv2 ve2 rs2 sh2 x2 x2_t hi lo logit gate gexp "
                 "gates ex_mm part chain tile_done total").split()
        s = {n: sem(f"e_{n}") for n in names}
        s_out = [sem(f"e_out{f}") for f in range(2)]
        NGATE = 18
        lng = rows[:, NLOG:NLOG + P]
        lnb = rows[:, NLOG + P:NLOG + 2 * P]
        fb = rows[:, NLOG + 2 * P:NLOG + 2 * P + E]
        HC = NC // 2
        FREE = 2
        CHAIN_A = (0, 1, 2, 3)
        CHAIN_B = (4, 5, 6)

        def over(row, n, tiles=NC):
            return row[:, None, :].broadcast_to([P, tiles, n])

        def over_experts(col):
            return col[:, :, None].broadcast_to([P, NC, E])

        BN2_AT = 0
        BN1_AT = 3
        LOW_AT = 6
        Y_AT = 3
        X2_AT = 6
        NORM2_AT = (3, 4)
        HIGH_AT = 5
        NORM1_AT = (6, 7)

        def sequences(eng, step):
            with eng.Fori(0, B // 2 - 1) as p:
                for k in range(2):
                    step(p * 2 + k, k, True, True)
            step(B - 2, 0, True, False)
            step(B - 1, 1, False, False)

        with nc.Block() as block:
            @block.sync
            def _(sp):
                def load_y(b):
                    sp.dma_start(yt[:, :], yt_dram[b]).then_inc(s["y_in"], 16)

                def load_x(b):
                    sp.dma_start(xb[:, :, :], x[b].rearrange("(i t) c -> t i c", i=NC)).then_inc(s["x_in"], 16)

                def store(b, f):
                    tiles = slice(f * HC, (f + 1) * HC)
                    sp.wait_ge(s["total"], b * 2 + f + 1)
                    sp.dma_start(out[b].rearrange("(i t) c -> t i c", i=NC)[:, tiles],
                                 total[:, tiles, :]).then_inc(s_out[f], 16)

                load_y(0)
                load_x(0)
                for n in range(1, 3):
                    sp.wait_ge(s["y_t"], n)
                    load_y(n)
                    sp.wait_ge(s["x1"], 2 * n)
                    load_x(n)
                with sp.Fori(0, B - 3) as b:
                    sp.wait_ge(s["y_t"], b + 3)
                    load_y(b + 3)
                    store(b, 0)
                    sp.wait_ge(s["x1"], (b + 3) * 2)
                    load_x(b + 3)
                    store(b, 1)
                for b in range(B - 3, B):
                    for f in range(2):
                        store(b, f)
                for f in range(2):
                    sp.wait_ge(s_out[f], 16 * (B + 1))

            @block.gpsimd
            def _(pool):
                def deviation(n, ve, mv, rs, sh, s_ve, s_rs, s_sh):
                    pool.wait_ge(s_ve, n + 1)
                    pool.tensor_tensor(rs[:, :], ve[:, :], mhalf[:, :], ALU.pow).then_inc(s_rs, 1)
                    pool.wait_ge(s_rs, n + 1)
                    pool.tensor_tensor(sh[:, :], mv[:, 0, :], rs[:, :], ALU.mult).then_inc(s_sh, 1)

                halves = [slice(f * HC, (f + 1) * HC) for f in range(2)]

                def affine(n):
                    for f, t in enumerate(halves):
                        pool.wait_ge(s["r0"], n * NC + (f + 1) * HC)
                        pool.tensor_tensor(r1[:, t, :], r0[:, t, :], over(lng, P, HC), ALU.mult).then_inc(s["r1"], 1)
                    for f, t in enumerate(halves):
                        pool.wait_ge(s["r1"], n * 2 + f + 1)
                        pool.tensor_tensor(r2[:, t, :], r1[:, t, :], over(lnb, P, HC), ALU.add).then_inc(s["r2"], 1)

                def residual(n, k):
                    pool.wait_ge(s["x_in"], (n + 1) * 16)
                    for f, t in enumerate(halves):
                        pool.wait_ge(s["r2"], n * 2 + f + 1)
                        pool.tensor_tensor(x1[k][:, t, :], r2[:, t, :], xb[:, t, :], ALU.add).then_inc(s["x1"], 1)

                def first(n):
                    deviation(n, ve1, mv1, rs1, sh1, s["ve1"], s["rs1"], s["sh1"])
                    affine(n)

                def second(n):
                    deviation(n, ve2, mv2, rs2, sh2, s["ve2"], s["rs2"], s["sh2"])

                def finish(b, k, f):
                    t = slice(f * HC, (f + 1) * HC)
                    pool.wait_ge(s["tile_done"], FREE + b * NC + (f + 1) * HC)
                    pool.wait_ge(s_out[f], 16 * (b + 1))
                    pool.tensor_tensor(total[:, t, :], acc_a[k][:, t, :], acc_b[k][:, t, :], ALU.add).then_inc(s["total"], 1)

                def step(b, k, next_, after):
                    if next_:
                        second(b + 1)
                    finish(b, k, 0)
                    if after:
                        first(b + 2)
                    finish(b, k, 1)
                    if after:
                        residual(b + 2, k)

                pool.memset(mhalf[:, :], -0.5).then_inc(s["mhalf"], 1)
                for f in range(2):
                    pool.sem_inc(s_out[f], 16)
                pool.wait_ge(s["mhalf"], 1)
                first(0)
                residual(0, 0)
                second(0)
                first(1)
                residual(1, 1)
                sequences(pool, step)

            @block.tensor
            def _(pe):
                def three(o, a_hi, a_lo, hi, lo, start=True):
                    pe.matmul(o, a_hi, hi, start=start, stop=False)
                    pe.matmul(o, a_hi, lo, start=False, stop=False)
                    return pe.matmul(o, a_lo, hi, start=False, stop=True)

                def transpose_y(n):
                    pe.wait_ge(s["y_in"], (n + 1) * 16)
                    for i in range(NC):
                        last = pe.transpose(p_y[:, i, :], yt[:, i * P:(i + 1) * P], c("ident"))
                    last.then_inc(s["y_t"], 1)

                def transpose_x2(n):
                    pe.wait_ge(s["x2"], (n + 1) * NC)
                    for i in range(NC):
                        last = pe.transpose(p_t[:, i * P:(i + 1) * P], x2[:, i, :], c("ident"))
                    last.then_inc(s["x2_t"], 1)

                def logits(n, k):
                    pe.wait_ge(s["hi"], n + 1)
                    pe.wait_ge(s["lo"], n + 1)
                    for i in range(NC):
                        t = slice(i * P, (i + 1) * P)
                        last = three(p_t[:, i * E:(i + 1) * E], x2t_hi[k][:, t], x2t_lo[k][:, t],
                                     fwg_hi[:, :], fwg_lo[:, :])
                    last.then_inc(s["logit"], 1)

                def experts(b, k, i):
                    pe.wait_ge(s["tile_done"], b * NC + i + 1)
                    t = slice(i * P, (i + 1) * P)
                    for f in range(2):
                        cols = slice(f * 512, (f + 1) * 512)
                        o = p_e[:, i % 2, 4 * f:4 * f + 4, :].rearrange("p e n -> p (e n)")
                        pe.matmul(o, onesr[:, :], be2[:, cols], start=True, stop=False)
                        last = three(o, x2t_hi[k][:, t], x2t_lo[k][:, t], wet_hi[:, cols], wet_lo[:, cols], start=False)
                    last.then_inc(s["ex_mm"], 1)

                def step(b, k, next_, after):
                    for i in range(NC):
                        experts(b, k, i)
                        if after and i == Y_AT:
                            transpose_y(b + 2)
                        if next_ and i == X2_AT:
                            transpose_x2(b + 1)
                    if next_:
                        logits(b + 1, 1 - k)

                transpose_y(0)
                transpose_x2(0)
                transpose_y(1)
                logits(0, 0)
                sequences(pe, step)

            @block.scalar
            def _(act):
                def apply(n, f, src, rs, sh, dst, s_sh, s_dst):
                    act.wait_ge(s_sh, n + 1)
                    for i in range(f * HC, (f + 1) * HC):
                        act.activation(dst[:, i, :], src[:, i, :], ACT.Identity, bias=sh[:, i:i + 1],
                                       scale=rs[:, i:i + 1]).then_inc(s_dst, 1)

                def first(n, f):
                    apply(n, f, p_y, rs1, sh1, r0, s["sh1"], s["r0"])

                def second(n, k, f):
                    act.wait_ge(s["x1"], (n + 1) * 2)
                    apply(n, f, x1[k], rs2, sh2, x2, s["sh2"], s["x2"])

                def high(n, k):
                    act.wait_ge(s["x2_t"], n + 1)
                    act.activation(x2t_hi[k][:, :], p_t[:, :], ACT.Copy).then_inc(s["hi"], 1)

                def share(b, i):
                    act.wait_ge(s["ex_mm"], b * NC + i + 1)
                    act.activation(part[:, i, :], p_e[:, i % 2, E - 1, :], ACT.Copy,
                                   scale=gl[11][:, i, E - 1:E]).then_inc(s["part"], 1)

                def numerators(n):
                    act.wait_ge(s["gate"], n * NGATE + 3)
                    act.activation(gl[2][:, :, :], gl[1][:, :, :], ACT.Exp).then_inc(s["gexp"], 1)

                def step(b, k, next_, after):
                    act.wait_ge(s["gates"], b + 1)
                    for i in range(NC):
                        share(b, i)
                        if next_ and i in NORM2_AT:
                            second(b + 1, 1 - k, NORM2_AT.index(i))
                        if next_ and i == HIGH_AT:
                            high(b + 1, 1 - k)
                        if after and i in NORM1_AT:
                            first(b + 2, NORM1_AT.index(i))
                    if next_:
                        numerators(b + 1)

                for f in range(2):
                    first(0, f)
                for f in range(2):
                    second(0, 0, f)
                high(0, 0)
                for f in range(2):
                    first(1, f)
                numerators(0)
                sequences(act, step)

            @block.vector
            def _(dve):
                def statistics(n, src, stats, mv, ve, s_st, s_mv, s_ve):
                    for i in range(NC):
                        dve.bn_stats(stats[:, i, :], src[:, i, :]).then_inc(s_st, 1)
                    dve.wait_ge(s_st, (n + 1) * NC)
                    mean_var(dve, n, stats, mv, ve, s_mv, s_ve, -1.0)

                def first(n):
                    dve.wait_ge(s["y_t"], n + 1)
                    statistics(n, p_y, st1, mv1, ve1, s["st1"], s["mv1"], s["ve1"])

                def second(n, k):
                    dve.wait_ge(s["x1"], (n + 1) * 2)
                    statistics(n, x1[k], st2, mv2, ve2, s["st2"], s["mv2"], s["ve2"])

                def low(n, k):
                    dve.wait_ge(s["hi"], n + 1)
                    dve.tensor_tensor(x2t_lo[k][:, :], p_t[:, :], x2t_hi[k][:, :].bitcast(F32),
                                      ALU.subtract).then_inc(s["lo"], 1)

                def gates(b):
                    count = [0]

                    def link(ins):
                        count[0] += 1
                        ins.then_inc(s["gate"], 1)
                        dve.wait_ge(s["gate"], b * NGATE + count[0])

                    place = over(c("first"), E)
                    dve.wait_ge(s["logit"], b + 1)
                    link(dve.tensor_tensor(gl[0][:, :, :], p_t[:, 0:NC * E].rearrange("p (i e) -> p i e", i=NC),
                                           over(fb, E), ALU.add))
                    link(dve.tensor_reduce(gm[0][:, :], gl[0][:, :, :], AX, ALU.max))
                    link(dve.tensor_tensor(gl[1][:, :, :], gl[0][:, :, :], over_experts(gm[0]), ALU.subtract))
                    dve.wait_ge(s["gexp"], b + 1)
                    num = gl[2]

                    def pick(vals, mx, eq, rank, best, one):
                        link(dve.tensor_reduce(gm[mx][:, :], vals[:, :, :], AX, ALU.max))
                        link(dve.tensor_tensor(gl[eq][:, :, :], vals[:, :, :], over_experts(gm[mx]), ALU.is_equal))
                        link(dve.tensor_tensor(gl[rank][:, :, :], gl[eq][:, :, :], place, ALU.mult))
                        link(dve.tensor_reduce(gm[best][:, :], gl[rank][:, :, :], AX, ALU.max))
                        link(dve.tensor_tensor(gl[one][:, :, :], gl[rank][:, :, :], over_experts(gm[best]), ALU.is_equal))

                    pick(num, 1, 3, 4, 2, 5)
                    link(dve.scalar_tensor_tensor(gl[6][:, :, :], gl[5][:, :, :], -2.0, num[:, :, :], ALU.mult, ALU.add))
                    pick(gl[6], 3, 7, 8, 4, 9)
                    link(dve.tensor_tensor(gm[5][:, :], gm[1][:, :], gm[3][:, :], ALU.add))
                    link(dve.reciprocal(gm[0][:, :], gm[5][:, :]))
                    link(dve.tensor_tensor(gl[3][:, :, :], gl[5][:, :, :], gl[9][:, :, :], ALU.add))
                    link(dve.tensor_tensor(gl[10][:, :, :], gl[3][:, :, :], num[:, :, :], ALU.mult))
                    assert count[0] == NGATE, count
                    dve.tensor_tensor(gl[11][:, :, :], gl[10][:, :, :], over_experts(gm[0]), ALU.mult).then_inc(s["gates"], 1)
                    dve.wait_ge(s["gates"], b + 1)

                def add_up(b, k, i):
                    dve.wait_ge(s["ex_mm"], b * NC + i + 1)
                    links = (b * NC + i) * (E - 2)
                    order = [(q, r) for r in range(len(CHAIN_A)) for q, ch in enumerate((CHAIN_A, CHAIN_B)) if r < len(ch)]
                    for at, (q, r) in enumerate(order):
                        e = (CHAIN_A, CHAIN_B)[q][r]
                        acc = (acc_a, acc_b)[q][k]
                        if r:
                            dve.wait_ge(s["chain"], links + at - 1)
                        elif q:
                            dve.wait_ge(s["part"], b * NC + i + 1)
                        before = acc if r else (x1[k], part)[q]
                        ins = dve.scalar_tensor_tensor(acc[:, i, :], p_e[:, i % 2, e, :], gl[11][:, i, e:e + 1],
                                                       before[:, i, :], ALU.mult, ALU.add)
                        if at == len(order) - 1:
                            ins.then_inc(s["tile_done"], 1)
                        else:
                            ins.then_inc(s["chain"], 1)

                def step(b, k, next_, after):
                    for i in range(NC):
                        add_up(b, k, i)
                        if next_ and i == BN2_AT:
                            second(b + 1, 1 - k)
                        if after and i == BN1_AT:
                            first(b + 2)
                        if next_ and i == LOW_AT:
                            low(b + 1, 1 - k)
                    if next_:
                        gates(b + 1)

                dve.sem_inc(s["tile_done"], FREE)
                first(0)
                second(0, 0)
                first(1)
                low(0, 0)
                gates(0)
                sequences(dve, step)


_INS = ["L0_attn_x", "L0_attn_Wq", "L0_attn_Wk", "L0_attn_Wv", "L0_attn_Wg", "L0_attn_bg", "L0_attn_Wdl",
        "L0_attn_Lparam", "L0_attn_Wo", "L0_attn_ln_g", "L0_attn_ln_b", "L0_ffn_Wg", "L0_ffn_bg", "L0_ffn_We",
        "L0_ffn_be"]


def kernel(**inputs):
    import concourse.bacc as bacc
    from concourse.bass_utils import run_bass_kernel_spmd

    nc = bacc.Bacc("TRN2", target_bir_lowering=False, num_devices=1)
    arrays, args = {}, []
    for name in _INS:
        arr = np.ascontiguousarray(inputs[name])
        arrays[f"in_{name}"] = arr
        args.append(nc.dram_tensor(f"in_{name}", arr.shape, mybir.dt.from_np(arr.dtype), kind="ExternalInput").ap())
    arrays["in_table"] = constants()
    args.append(nc.dram_tensor("in_table", [P, NCONST], F32, kind="ExternalInput").ap())
    args.append(nc.dram_tensor("out_0", [B, T, D], F32, kind="ExternalOutput").ap())
    program(nc, *args)
    r = run_bass_kernel_spmd(nc, [arrays], core_ids=[0])
    return r.results[0]["out_0"]
```
